# Optimizing a Trainium2 kernel written in Bass

```python
import numpy as np
import jax
import jax.numpy as jnp

def _softmax(x, axis=-1):
    return jax.nn.softmax(x, axis=axis)

def _gelu(x):
    return jax.nn.gelu(x, approximate=True)

def _silu(x):
    return jax.nn.silu(x)

def _sigmoid(x):
    return jax.nn.sigmoid(x)

def _layernorm(x, axis=-1, eps=1e-05):
    m = jnp.mean(x, axis=axis, keepdims=True)
    v = jnp.var(x, axis=axis, keepdims=True)
    return (x - m) / jnp.sqrt(v + eps)

def _scatter_add(tgt, idx, src, axis=0):
    return tgt.at[idx].add(src)

def _segment_sum(src, seg, n):
    return jax.ops.segment_sum(src, seg, n)
kernel_name = 'mk_gps_d2_gnn_r8_344d21'

def setup_inputs(seed: int=0):
    np.random.seed(seed)
    _w = jnp.asarray

    def _rec_inputs():
        import jax
        import jax.numpy as jnp
        _gk = jax.random.key(seed)
        x = -0.0003019 + 1 * jax.random.normal(jax.random.fold_in(_gk, 1), (1250, 1024), jnp.float32)
        _s = jax.random.randint(jax.random.fold_in(_gk, 2), (10000,), 0, 1250, jnp.int32)
        _d = jax.random.randint(jax.random.fold_in(_gk, 3), (10000,), 0, 1250, jnp.int32)
        _loop = jnp.arange(1250, dtype=jnp.int32)
        src = jnp.concatenate([_s, _d, _loop])
        dst = jnp.concatenate([_d, _s, _loop])
        _o = jnp.argsort(dst, stable=True)
        src = src[_o]
        dst = dst[_o]
        return (x, src, dst)
    x, src, dst = _rec_inputs()

    def _L0_gnn_setup():
        import jax, jax.numpy as jnp
        import numpy as np
        N = 2500
        E = 40000
        IN = 1024
        HID = 256
        H = 4
        D = HID // H
        OUT = 1024
        EPS = 1e-06
        NEG_SLOPE = 0.2
        key = jax.random.key(seed)
        ks = jax.random.split(key, 8)
        x = jax.random.normal(ks[0], (N, IN), dtype=jnp.float32)
        edge_index = jax.random.randint(ks[1], (2, E), 0, N, dtype=jnp.int64)
        s = 0.02
        return {'x': x, 'edge_index': edge_index, 'rms_w': jnp.ones((IN,), dtype=jnp.float32), 'W_down': jax.random.normal(ks[2], (IN, HID), dtype=jnp.float32) * s, 'Wl': jax.random.normal(ks[3], (HID, HID), dtype=jnp.float32) * s, 'Wr': jax.random.normal(ks[4], (HID, HID), dtype=jnp.float32) * s, 'att': jax.random.normal(ks[5], (H, D), dtype=jnp.float32) * s, 'W_up': jax.random.normal(ks[6], (HID, OUT), dtype=jnp.float32) * s}
    _L0_gnn_all = _L0_gnn_setup()
    _L0_gnn_in = {k: v for k, v in _L0_gnn_all.items() if k in ('rms_w', 'W_down', 'Wl', 'Wr', 'att', 'W_up')}
    del _L0_gnn_all

    def _L0_mix_setup():
        import jax, jax.numpy as jnp
        import numpy as np
        B, T, D = (4, 512, 1024)
        H = 16
        DK = D // H
        EPS = 1e-06

        def _phi(x):
            return jax.nn.elu(x) + 1.0
        key = jax.random.key(seed)
        ks = jax.random.split(key, 9)
        s = 1.0 / np.sqrt(D)
        return {'x': jax.random.normal(ks[0], (B, T, D), dtype=jnp.float32), 'Wq': jax.random.uniform(ks[1], (D, D), jnp.float32, -s, s), 'bq': jax.random.uniform(ks[2], (D,), jnp.float32, -s, s), 'Wk': jax.random.uniform(ks[3], (D, D), jnp.float32, -s, s), 'bk': jax.random.uniform(ks[4], (D,), jnp.float32, -s, s), 'Wv': jax.random.uniform(ks[5], (D, D), jnp.float32, -s, s), 'bv': jax.random.uniform(ks[6], (D,), jnp.float32, -s, s), 'Wo': jax.random.uniform(ks[7], (D, D), jnp.float32, -s, s), 'bo': jax.random.uniform(ks[8], (D,), jnp.float32, -s, s)}
    _L0_mix_all = _L0_mix_setup()
    _L0_mix_in = {k: v for k, v in _L0_mix_all.items() if k in ('Wq', 'bq', 'Wk', 'bk', 'Wv', 'bv', 'Wo', 'bo')}
    del _L0_mix_all

    def _L0_ffn_setup():
        import jax, jax.numpy as jnp
        import numpy as np
        NUM_EXPERTS = 8
        EXPERT_CAPACITY = 2.0
        key = jax.random.key(seed)
        k1, k2, k3, k4 = jax.random.split(key, 4)
        B, T, C, H, E = (4, 512, 1024, 512, NUM_EXPERTS)
        x = jax.random.normal(k1, (B, T, C), jnp.float32)
        gate_w = jax.random.normal(k2, (C, E), jnp.float32) * 0.02
        w1 = jax.random.normal(k3, (E, C, H), jnp.float32) * 0.02
        w2 = jax.random.normal(k4, (E, H, C), jnp.float32) * 0.02
        return {'x': x, 'gate_w': gate_w, 'w1': w1, 'w2': w2}
    _L0_ffn_all = _L0_ffn_setup()
    _L0_ffn_in = {k: v for k, v in _L0_ffn_all.items() if k in ('gate_w', 'w1', 'w2')}
    del _L0_ffn_all

    def _L1_gnn_setup():
        import jax, jax.numpy as jnp
        import numpy as np
        N_NODES = 3125
        N_EDGES = 50000
        D = 1024

        def _sage_layer(h, edge_src, edge_dst, deg_inv, W_self, W_neigh, b):
            msg = h[edge_src]
            agg = jax.ops.segment_sum(msg, edge_dst, num_segments=h.shape[0])
            mean = agg * deg_inv[:, None]
            return h @ W_self + mean @ W_neigh + b
        key = jax.random.key(seed)
        ks = jax.random.split(key, 8)
        s = 1.0 / np.sqrt(D)
        return {'x': jax.random.normal(ks[0], (N_NODES, D), dtype=jnp.float32), 'edge_src': jax.random.randint(ks[1], (N_EDGES,), 0, N_NODES, dtype=jnp.int32), 'edge_dst': jax.random.randint(ks[2], (N_EDGES,), 0, N_NODES, dtype=jnp.int32), 'W_self0': jax.random.normal(ks[3], (D, D), dtype=jnp.float32) * s, 'W_neigh0': jax.random.normal(ks[4], (D, D), dtype=jnp.float32) * s, 'b0': jnp.zeros((D,), dtype=jnp.float32), 'W_self1': jax.random.normal(ks[5], (D, D), dtype=jnp.float32) * s, 'W_neigh1': jax.random.normal(ks[6], (D, D), dtype=jnp.float32) * s, 'b1': jnp.zeros((D,), dtype=jnp.float32)}
    _L1_gnn_all = _L1_gnn_setup()
    _L1_gnn_in = {k: v for k, v in _L1_gnn_all.items() if k in ('W_self0', 'W_neigh0', 'b0', 'W_self1', 'W_neigh1', 'b1')}
    del _L1_gnn_all

    def _L1_mix_setup():
        import jax, jax.numpy as jnp
        import numpy as np
        B, S, D_MODEL, N_HEADS = (4, 1024, 1024, 16)
        D_K = D_MODEL // N_HEADS
        key = jax.random.key(seed)
        k1, k2, k3 = jax.random.split(key, 3)
        x = jax.random.normal(k1, (B, S, D_MODEL), dtype=jnp.float32)
        w_qkv = jax.random.normal(k2, (D_MODEL, 3 * D_MODEL), dtype=jnp.float32) * (1.0 / np.sqrt(D_MODEL))
        w_o = jax.random.normal(k3, (D_MODEL, D_MODEL), dtype=jnp.float32) * (1.0 / np.sqrt(D_MODEL))
        return {'x': x, 'w_qkv': w_qkv, 'w_o': w_o}
    _L1_mix_all = _L1_mix_setup()
    _L1_mix_in = {k: v for k, v in _L1_mix_all.items() if k in ('w_qkv', 'w_o')}
    del _L1_mix_all

    def _L1_ffn_setup():
        import jax, jax.numpy as jnp
        import numpy as np
        key = jax.random.key(seed)
        k0, k1, k2, k3 = jax.random.split(key, 4)
        B, S, D, F, E = (8, 256, 1024, 256, 8)
        x = jax.random.normal(k0, (B, S, D), dtype=jnp.float32)
        Wg = jax.random.normal(k1, (D, E), dtype=jnp.float32) * 0.02
        W1 = jax.random.normal(k2, (E, D, F), dtype=jnp.float32) * 0.02
        W2 = jax.random.normal(k3, (E, F, D), dtype=jnp.float32) * 0.02
        return {'x': x, 'Wg': Wg, 'W1': W1, 'W2': W2}
    _L1_ffn_all = _L1_ffn_setup()
    _L1_ffn_in = {k: v for k, v in _L1_ffn_all.items() if k in ('Wg', 'W1', 'W2')}
    del _L1_ffn_all
    return {'x': x, 'src': src, 'dst': dst, 'L0_gnn_rms_w': _L0_gnn_in['rms_w'], 'L0_gnn_W_down': _L0_gnn_in['W_down'], 'L0_gnn_Wl': _L0_gnn_in['Wl'], 'L0_gnn_Wr': _L0_gnn_in['Wr'], 'L0_gnn_att': _L0_gnn_in['att'], 'L0_gnn_W_up': _L0_gnn_in['W_up'], 'L0_mix_Wq': _L0_mix_in['Wq'], 'L0_mix_bq': _L0_mix_in['bq'], 'L0_mix_Wk': _L0_mix_in['Wk'], 'L0_mix_bk': _L0_mix_in['bk'], 'L0_mix_Wv': _L0_mix_in['Wv'], 'L0_mix_bv': _L0_mix_in['bv'], 'L0_mix_Wo': _L0_mix_in['Wo'], 'L0_mix_bo': _L0_mix_in['bo'], 'L0_ffn_gate_w': _L0_ffn_in['gate_w'], 'L0_ffn_w1': _L0_ffn_in['w1'], 'L0_ffn_w2': _L0_ffn_in['w2'], 'L1_gnn_W_self0': _L1_gnn_in['W_self0'], 'L1_gnn_W_neigh0': _L1_gnn_in['W_neigh0'], 'L1_gnn_b0': _L1_gnn_in['b0'], 'L1_gnn_W_self1': _L1_gnn_in['W_self1'], 'L1_gnn_W_neigh1': _L1_gnn_in['W_neigh1'], 'L1_gnn_b1': _L1_gnn_in['b1'], 'L1_mix_w_qkv': _L1_mix_in['w_qkv'], 'L1_mix_w_o': _L1_mix_in['w_o'], 'L1_ffn_Wg': _L1_ffn_in['Wg'], 'L1_ffn_W1': _L1_ffn_in['W1'], 'L1_ffn_W2': _L1_ffn_in['W2']}

def reference(x, src, dst, L0_gnn_rms_w, L0_gnn_W_down, L0_gnn_Wl, L0_gnn_Wr, L0_gnn_att, L0_gnn_W_up, L0_mix_Wq, L0_mix_bq, L0_mix_Wk, L0_mix_bk, L0_mix_Wv, L0_mix_bv, L0_mix_Wo, L0_mix_bo, L0_ffn_gate_w, L0_ffn_w1, L0_ffn_w2, L1_gnn_W_self0, L1_gnn_W_neigh0, L1_gnn_b0, L1_gnn_W_self1, L1_gnn_W_neigh1, L1_gnn_b1, L1_mix_w_qkv, L1_mix_w_o, L1_ffn_Wg, L1_ffn_W1, L1_ffn_W2):
    import jax
    import jax.numpy as jnp

    def _L0_gnn_ref(x, edge_index, rms_w, W_down, Wl, Wr, att, W_up):
        import jax, jax.numpy as jnp
        import numpy as np
        N = 2500
        E = 40000
        IN = 1024
        HID = 256
        H = 4
        D = HID // H
        OUT = 1024
        EPS = 1e-06
        NEG_SLOPE = 0.2
        n = x.shape[0]
        ms = jnp.mean(jnp.square(x), axis=-1, keepdims=True)
        x = x * jax.lax.rsqrt(ms + EPS) * rms_w
        x = x @ W_down
        loop = jnp.arange(n, dtype=edge_index.dtype)
        src = jnp.concatenate([edge_index[0], loop])
        dst = jnp.concatenate([edge_index[1], loop])
        xl = (x @ Wl).reshape(n, H, D)
        xr = (x @ Wr).reshape(n, H, D)
        msg = xl[src] + xr[dst]
        act = jnp.where(msg > 0, msg, NEG_SLOPE * msg)
        e = jnp.einsum('ehd,hd->eh', act, att)
        m = jax.ops.segment_max(e, dst, num_segments=n)
        p = jnp.exp(e - m[dst])
        denom = jax.ops.segment_sum(p, dst, num_segments=n)
        alpha = p / (denom[dst] + 1e-16)
        out = jax.ops.segment_sum(alpha[..., None] * xl[src], dst, num_segments=n)
        out = out.reshape(n, HID)
        return out @ W_up

    def _L0_mix_ref(x, Wq, bq, Wk, bk, Wv, bv, Wo, bo):
        import jax, jax.numpy as jnp
        import numpy as np
        B, T, D = (4, 512, 1024)
        H = 16
        DK = D // H
        EPS = 1e-06

        def _phi(x):
            return jax.nn.elu(x) + 1.0
        Bq, Tq, _ = x.shape

        def heads(y):
            return y.reshape(Bq, Tq, H, DK).transpose(0, 2, 1, 3)
        q = _phi(heads(x @ Wq.T + bq))
        k = _phi(heads(x @ Wk.T + bk))
        v = heads(x @ Wv.T + bv)
        kv = jnp.einsum('bhtd,bhtm->bhdm', k, v)
        z = 1.0 / (jnp.einsum('bhtd,bhd->bht', q, k.sum(axis=2) + EPS) + EPS)
        out = jnp.einsum('bhtd,bhdm,bht->bhtm', q, kv, z)
        out = out.transpose(0, 2, 1, 3).reshape(Bq, Tq, -1)
        return out @ Wo.T + bo

    def _L0_ffn_ref(x, gate_w, w1, w2):
        import jax, jax.numpy as jnp
        import numpy as np
        NUM_EXPERTS = 8
        EXPERT_CAPACITY = 2.0
        B, T, C = x.shape
        E = gate_w.shape[1]
        cap = int(EXPERT_CAPACITY * T / E)
        scores = jnp.einsum('BTC,CE->BTE', x, gate_w)
        probs = jax.nn.softmax(scores, axis=-1)
        probs_et = jnp.transpose(probs, (0, 2, 1))
        top_p, top_idx = jax.lax.top_k(probs_et, cap)
        xin = jnp.take_along_axis(x[:, None, :, :], top_idx[..., None], axis=2)
        h = jax.nn.gelu(jnp.einsum('BElC,ECH->BElH', xin, w1), approximate=False)
        y = jnp.einsum('BElH,EHC->BElC', h, w2)
        y = y * top_p[..., None]
        b_idx = jnp.arange(B)[:, None, None]
        out = jnp.zeros((B, T, C), x.dtype).at[b_idx, top_idx].add(y)
        return out

    def _L1_gnn_ref(x, edge_src, edge_dst, W_self0, W_neigh0, b0, W_self1, W_neigh1, b1):
        import jax, jax.numpy as jnp
        import numpy as np
        N_NODES = 3125
        N_EDGES = 50000
        D = 1024

        def _sage_layer(h, edge_src, edge_dst, deg_inv, W_self, W_neigh, b):
            msg = h[edge_src]
            agg = jax.ops.segment_sum(msg, edge_dst, num_segments=h.shape[0])
            mean = agg * deg_inv[:, None]
            return h @ W_self + mean @ W_neigh + b
        N = x.shape[0]
        deg = jax.ops.segment_sum(jnp.ones_like(edge_dst, dtype=x.dtype), edge_dst, num_segments=N)
        deg_inv = 1.0 / jnp.maximum(deg, 1.0)
        h = jax.nn.relu(_sage_layer(x, edge_src, edge_dst, deg_inv, W_self0, W_neigh0, b0))
        out = _sage_layer(h, edge_src, edge_dst, deg_inv, W_self1, W_neigh1, b1)
        return out

    def _L1_mix_ref(x, w_qkv, w_o):
        import jax, jax.numpy as jnp
        import numpy as np
        B, S, D_MODEL, N_HEADS = (4, 1024, 1024, 16)
        D_K = D_MODEL // N_HEADS
        b, s, dm = x.shape
        h, d = (N_HEADS, D_K)
        qkv = (x @ w_qkv).reshape(b, s, 3, h, d)
        q, k, v = (qkv[:, :, 0], qkv[:, :, 1], qkv[:, :, 2])
        q = jax.nn.elu(q) + 1.0
        k = jax.nn.elu(k) + 1.0
        kv = jnp.einsum('bnhd,bnhf->bhdf', k, v)
        k_sum = k.sum(axis=1)
        numerator = jnp.einsum('bnhd,bhdf->bnhf', q, kv)
        denominator = jnp.einsum('bnhd,bhd->bnh', q, k_sum)[..., None] + 1e-06
        attn = (numerator / denominator).reshape(b, s, dm)
        return attn @ w_o

    def _L1_ffn_ref(x, Wg, W1, W2):
        import jax, jax.numpy as jnp
        import numpy as np
        B, S, D = x.shape
        E = Wg.shape[1]
        T = B * S
        cap = max(1, T // E)
        xt = x.reshape(T, D)
        logits = xt @ Wg
        probs = jax.nn.softmax(logits, axis=-1)
        pT = probs.T
        _, top_idx = jax.lax.top_k(pT, cap)
        sel = jnp.zeros((E, T), dtype=bool).at[jnp.arange(E)[:, None], top_idx].set(True)
        masked = jnp.where(sel, pT, -jnp.inf)
        assigned = sel.any(axis=0)
        tok2exp = jnp.where(assigned, jnp.argmax(masked, axis=0), jnp.argmax(pT, axis=0))
        weights = jnp.take_along_axis(probs, tok2exp[:, None], axis=1)[:, 0]
        out = jnp.zeros_like(xt)
        for e in range(E):
            gate = jnp.where(tok2exp == e, weights, 0.0)
            h = jax.nn.gelu(xt @ W1[e], approximate=False) @ W2[e]
            out = out + gate[:, None] * h
        return out.reshape(B, S, D)
    edge_index = jnp.stack([src, dst])
    xn = _layernorm(x, axis=-1)
    x = x + _L0_gnn_ref(xn, edge_index, L0_gnn_rms_w, L0_gnn_W_down, L0_gnn_Wl, L0_gnn_Wr, L0_gnn_att, L0_gnn_W_up) + _L0_mix_ref(xn[None], L0_mix_Wq, L0_mix_bq, L0_mix_Wk, L0_mix_bk, L0_mix_Wv, L0_mix_bv, L0_mix_Wo, L0_mix_bo)[0]
    x = x + _L0_ffn_ref(_layernorm(x, axis=-1)[None], L0_ffn_gate_w, L0_ffn_w1, L0_ffn_w2)[0]
    xn = _layernorm(x, axis=-1)
    x = x + _L1_gnn_ref(xn, src, dst, L1_gnn_W_self0, L1_gnn_W_neigh0, L1_gnn_b0, L1_gnn_W_self1, L1_gnn_W_neigh1, L1_gnn_b1) + _L1_mix_ref(xn[None], L1_mix_w_qkv, L1_mix_w_o)[0]
    x = x + _L1_ffn_ref(_layernorm(x, axis=-1)[None], L1_ffn_Wg, L1_ffn_W1, L1_ffn_W2)[0]
    return x

_drawn_inputs = setup_inputs


def setup_inputs(seed=0):
    import zlib

    import numpy as np

    out = dict(_drawn_inputs(seed))
    spreads = {'L0_gnn_rms_w': (1.0, 0.6), 'L1_gnn_b0': (0.0, 0.1), 'L1_gnn_b1': (0.0, 0.1)}
    factors = {'L0_gnn_W_down': 3.22,
     'L0_gnn_Wl': 3.205,
     'L0_gnn_Wr': 8.0,
     'L0_gnn_att': 8.0,
     'L0_gnn_W_up': 3.212,
     'L0_mix_Wq': 30.791,
     'L0_mix_bq': 200.0,
     'L0_mix_Wk': 22.154,
     'L0_mix_bk': 200.0,
     'L0_mix_Wv': 4.398,
     'L0_mix_bv': 3.676,
     'L0_mix_Wo': 3.003,
     'L0_mix_bo': 7.248,
     'L0_ffn_gate_w': 2.798,
     'L1_ffn_Wg': 4.859,
     'L1_ffn_W1': 4.871,
     'L1_ffn_W2': 4.576}
    for name, (base, spread) in spreads.items():
        noise = np.random.default_rng([zlib.crc32(name.encode()), seed]).standard_normal(out[name].shape)
        drawn = base * np.exp(spread * noise) if base else spread * noise
        out[name] = jnp.asarray(drawn.astype(out[name].dtype))
    for name, factor in factors.items():
        out[name] = (out[name] * factor).astype(out[name].dtype)
    return out
```

```python
import math
import concourse.bass as bass
from concourse import mybir
from contextlib import ExitStack

F32 = mybir.dt.float32
F32R = mybir.dt.float32r
BF16 = mybir.dt.bfloat16
I32 = mybir.dt.int32
U32 = mybir.dt.uint32
ALU = mybir.AluOpType
ACT = mybir.ActivationFunctionType
AX = mybir.AxisListType

N = 1250
D = 1024
P = 128
R = 125
T = N // R
KD = D // P
CHUNKS = [(0, 418), (418, 416), (834, 416)]
SLAB = 256
NSLAB = D // SLAB
BANK = 512
NEG = -1.0e30


class Link:

    def __init__(self, eng, sem, base=0):
        self.eng, self.sem, self.base, self.count = eng, sem, base, 0

    def __call__(self, ins):
        self.count += 1
        ins.then_inc(self.sem, 1)
        self.eng.wait_ge(self.sem, self.base + self.count)


class Phase:

    def __init__(self, nc, name):
        self.nc, self.name, self.ctx, self.held = nc, name, ExitStack(), []

    def __enter__(self):
        return self

    def __exit__(self, *exc):
        if self.held:
            self.nc.clear_and_free_semaphores(self.held)
            self.nc.all_engine_barrier()
        return self.ctx.__exit__(*exc)

    def sb(self, name, shape, dt):
        return self.ctx.enter_context(self.nc.sbuf_tensor(f"{self.name}_{name}", shape, dt))

    def ps(self, name, shape, dt=F32):
        return self.ctx.enter_context(self.nc.psum_tensor(f"{self.name}_{name}", shape, dt))

    def sem(self, name):
        self.held.append(self.nc.alloc_semaphore(f"{self.name}_{name}"))
        return self.held[-1]

    def sems(self, name, n):
        return [self.sem(f"{name}{i}") for i in range(n)]


def constants_phase(nc, ident, hole, scores):
    with Phase(nc, "const") as ph:
        s_zero, s_id, s_hole = ph.sem("zero"), ph.sem("id"), ph.sem("hole")
        s_fill = nc.alloc_semaphore("scores_filled")
        rows = scores.rearrange("(t p s) h -> t p (s h)", p=R, s=N)
        with nc.Block() as block:
            @block.gpsimd
            def _(pool):
                pool.memset(ident[:, :], 0.0).then_inc(s_zero, 1)
                pool.memset(hole[:, :], NEG).then_inc(s_hole, 1)
                pool.wait_ge(s_zero, 1)
                pool.affine_select(out=ident[:, :], in_=ident[:, :], compare_op=ALU.not_equal, fill=1.0,
                                   base=0, pattern=[[-1, P]], channel_multiplier=1).then_inc(s_id, 1)

            @block.sync
            def _(sp):
                sp.wait_ge(s_hole, 1)
                for t in range(T):
                    for h in range(4):
                        sp.dma_start(rows[t][:, h * N:(h + 1) * N], hole[:, :]).then_inc(s_fill, 16)
        return s_fill, 16 * 4 * T


def norm_phase(nc, name, src, act_hi, act_lo, ident, dst=None, rms=None, normalize=True):
    with Phase(nc, name) as ph:
        x = ph.sb("x", [R, 2, D], F32)
        y = ph.sb("y", [R, 2, D], F32)
        stats = ph.sb("stats", [R, 2, 2, 6], F32)
        mv = ph.sb("mv", [R, 2, 2], F32)
        dev = ph.sb("dev", [R, 2, 2], F32)
        rstd = ph.sb("rstd", [R, 2, 1], F32)
        square = ph.sb("square", [R, D], F32)
        sumsq = ph.sb("sumsq", [R, T], F32)
        pt = [ph.ps(f"pt{h}", [P, 2, BANK]) for h in range(2)]
        s_x = ph.sems("x_in", 2)
        s_var, s_dev, s_y = ph.sem("var"), ph.sem("dev"), ph.sem("y")
        s_tr, s_hi, s_lo = ph.sem("tr"), ph.sem("hi"), ph.sem("lo")
        s_out = ph.sems("out", 2)
        s_link, s_sq, s_rms, s_rdev = ph.sem("link"), ph.sem("sq"), ph.sem("rms"), ph.sem("rdev")
        rows = src.rearrange("(t p) c -> t p c", p=R)
        out_rows = dst.rearrange("(t p) c -> t p c", p=R) if dst is not None else None
        feed = y if normalize else x

        with nc.Block() as block:
            @block.sync
            def _(sp):
                def load(t):
                    if t >= 2:
                        sp.wait_ge(s_y if normalize else s_tr, t - 1)
                    sp.dma_start(x[:, t % 2, :], rows[t]).then_inc(s_x[t % 2], 16)

                load(0)
                for t in range(T):
                    if t + 1 < T:
                        load(t + 1)
                    if dst is not None:
                        sp.wait_ge(s_y, t + 1)
                        sp.dma_start(out_rows[t], y[:, t % 2, :]).then_inc(s_out[t % 2], 16)
                if dst is not None:
                    for h in range(2):
                        sp.wait_ge(s_out[h], 16 * (T // 2))

            @block.vector
            def _(dve):
                with dve.Fori(0, T // 2) as i:
                    link = Link(dve, s_link, 2 * 6 * i)
                    if normalize:
                        for h in range(2):
                            dve.wait_ge(s_x[h], 16 * i + 16)
                            for half in range(2):
                                ins = dve.bn_stats(stats[:, h, half, :], x[:, h, half * BANK:(half + 1) * BANK])
                            link(ins)
                            dve.memset(dev[:, h, 0:1], 0.0)
                            link(dve.bn_aggr(mv[:, h, :], stats[:, h, :, :].rearrange("p a b -> p (a b)")))
                            dve.tensor_scalar(dev[:, h, 0:1], mv[:, h, 1:2], 1e-5, None, ALU.add).then_inc(s_var, 1)
                            dve.wait_ge(s_dev, 2 * i + h + 1)
                            link(dve.reciprocal(rstd[:, h, :], dev[:, h, 1:2]))
                            link(dve.tensor_scalar(dev[:, h, 1:2], rstd[:, h, :], rstd[:, h, :], dev[:, h, 0:1],
                                                   ALU.mult, ALU.mult))
                            link(dve.tensor_scalar(dev[:, h, 1:2], dev[:, h, 1:2], -0.5, 1.5, ALU.mult, ALU.add))
                            link(dve.tensor_tensor(rstd[:, h, :], rstd[:, h, :], dev[:, h, 1:2], ALU.mult))
                            dve.wait_ge(s_tr, 2 * i)
                            if dst is not None:
                                dve.wait_ge(s_out[h], 16 * i)
                            if rms is not None:
                                dve.wait_ge(s_sq, 2 * i)
                            dve.tensor_scalar(y[:, h, :], x[:, h, :], mv[:, h, 0:1], rstd[:, h, :],
                                              ALU.subtract, ALU.mult).then_inc(s_y, 1)
                    for h in range(2):
                        dve.wait_ge(s_hi, 2 * i + h + 1)
                        for b in range(2):
                            cols = slice(4 * b, 4 * b + 4)
                            at = bass.ds(2 * R * i + R * h, R)
                            ins = dve.tensor_tensor(
                                act_lo[:, cols, at], pt[h][:, b, 0:4 * R].rearrange("p (k r) -> p k r", k=4),
                                act_hi[:, cols, at].bitcast(F32), ALU.subtract)
                        ins.then_inc(s_lo, 1)
                if rms is not None:
                    dve.wait_ge(s_sq, T)
                    dve.tensor_scalar(rms[:, :], sumsq[:, :], 1.0 / D, 1e-6, ALU.mult, ALU.add).then_inc(s_rms, 1)
                    dve.wait_ge(s_rdev, 1)
                    dve.reciprocal(rms[:, :], sumsq[:, :]).then_inc(s_rms, 1)
                    dve.wait_ge(s_rms, 2)

            @block.scalar
            def _(act):
                with act.Fori(0, T // 2) as i:
                    if normalize:
                        for h in range(2):
                            act.wait_ge(s_var, 2 * i + h + 1)
                            act.activation(dev[:, h, 1:2], dev[:, h, 0:1], ACT.Sqrt).then_inc(s_dev, 1)
                    for h in range(2):
                        if rms is not None:
                            act.wait_ge(s_y, 2 * i + h + 1)
                            act.wait_ge(s_sq, 2 * i + h)
                            act.activation(square[:, :], y[:, h, :], ACT.Square,
                                           accum_out=sumsq[:, bass.ds(2 * i + h, 1)]).then_inc(s_sq, 1)
                        act.wait_ge(s_tr, 2 * i + h + 1)
                        for b in range(2):
                            ins = act.activation(act_hi[:, 4 * b:4 * b + 4, bass.ds(2 * R * i + R * h, R)],
                                                 pt[h][:, b, 0:4 * R].rearrange("p (k r) -> p k r", k=4), ACT.Copy)
                        ins.then_inc(s_hi, 1)
                if rms is not None:
                    act.wait_ge(s_rms, 1)
                    act.activation(sumsq[:, :], rms[:, :], ACT.Sqrt).then_inc(s_rdev, 1)

            @block.tensor
            def _(pe):
                with pe.Fori(0, T // 2) as i:
                    for h in range(2):
                        if normalize:
                            pe.wait_ge(s_y, 2 * i + h + 1)
                        else:
                            pe.wait_ge(s_x[h], 16 * i + 16)
                        pe.wait_ge(s_lo, 2 * i)
                        for k in range(KD):
                            ins = pe.transpose(pt[h][:, k // 4, (k % 4) * R:(k % 4 + 1) * R],
                                               feed[:, h, k * P:(k + 1) * P], ident[0:R, 0:R])
                        ins.then_inc(s_tr, 1)
HID = 256
HEADS = 4
HD = HID // HEADS
EDGES = 21250
ET = EDGES // R
EB = 5
PAIRS = ET // 2
KH = HID // P
XW = HD + 2


def weights_phase(nc, weights, wt, ident):
    with Phase(nc, "wt") as ph:
        raw = ph.sb("raw", [P, 2, D], F32)
        out = ph.sb("out", [P, 2, KD, P], F32)
        pt = [ph.ps(f"pt{h}", [P, 2, BANK]) for h in range(2)]
        s_raw, s_out = ph.sems("raw", 2), ph.sems("out", 2)
        s_tr, s_a, s_v = ph.sem("tr"), ph.sem("a"), ph.sem("v")
        n = len(weights) * KD
        with nc.Block() as block:
            @block.sync
            def _(sp):
                def load(j):
                    if j >= 2:
                        sp.wait_ge(s_tr, j - 1)
                    sp.dma_start(raw[:, j % 2, :], weights[j // KD][(j % KD) * P:(j % KD + 1) * P, :]) \
                        .then_inc(s_raw[j % 2], 16)

                load(0)
                for j in range(n):
                    if j + 1 < n:
                        load(j + 1)
                    sp.wait_ge(s_a, j + 1)
                    sp.wait_ge(s_v, j + 1)
                    cols = slice((j % KD) * P, (j % KD + 1) * P)
                    sp.dma_start(wt[j // KD].rearrange("(k p) o -> p k o", p=P)[:, :, cols],
                                 out[:, j % 2, :, :]).then_inc(s_out[j % 2], 16)
                for h in range(2):
                    sp.wait_ge(s_out[h], 16 * n // 2)

            @block.tensor
            def _(pe):
                with pe.Fori(0, n // 2) as i:
                    for h in range(2):
                        pe.wait_ge(s_raw[h], 16 * i + 16)
                        pe.wait_ge(s_a, 2 * i)
                        pe.wait_ge(s_v, 2 * i)
                        for k in range(KD):
                            ins = pe.transpose(pt[h][:, k // 4, (k % 4) * P:(k % 4 + 1) * P],
                                               raw[:, h, k * P:(k + 1) * P], ident[:, :])
                        ins.then_inc(s_tr, 1)

            @block.scalar
            def _(act):
                with act.Fori(0, n // 2) as i:
                    for h in range(2):
                        act.wait_ge(s_tr, 2 * i + h + 1)
                        act.wait_ge(s_out[h], 16 * i)
                        act.activation(out[:, h, 0:4, :].rearrange("p k o -> p (k o)"), pt[h][:, 0, :],
                                       ACT.Copy).then_inc(s_a, 1)

            @block.vector
            def _(dve):
                with dve.Fori(0, n // 2) as i:
                    for h in range(2):
                        dve.wait_ge(s_tr, 2 * i + h + 1)
                        dve.wait_ge(s_out[h], 16 * i)
                        dve.tensor_copy(out[:, h, 4:8, :].rearrange("p k o -> p (k o)"), pt[h][:, 1, :]) \
                            .then_inc(s_v, 1)


def mm3(pe, out, lhs, rhs, first, last):
    pe.matmul(out, lhs[0], rhs[0], start=first, stop=False)
    pe.matmul(out, lhs[0], rhs[1], start=False, stop=False)
    return pe.matmul(out, lhs[1], rhs[0], start=False, stop=last)


def gat_project_phase(nc, act_hi, act_lo, rms, rms_w, w_down, wl, wr, xl, xr):
    with Phase(nc, "proj") as ph:
        wd = ph.sb("wd", [P, KD, HID], F32)
        wd_hi, wd_lo = (ph.sb(f"wd_{s}", [P, KD, HID], F32R) for s in ("hi", "lo"))
        gain = ph.sb("gain", [P, KD], F32)
        wlr = ph.sb("wlr", [P, KH, 2 * HID], F32)
        wlr_hi, wlr_lo = (ph.sb(f"wlr_{s}", [P, KH, 2 * HID], F32R) for s in ("hi", "lo"))
        d_hi, d_lo = (ph.sb(f"down_{s}", [P, KH, N], F32R) for s in ("hi", "lo"))
        out = ph.sb("out", [R, 2, 2 * HID], F32)
        bank = [ph.ps(f"bank{b}", [P, BANK]) for b in range(4)]
        s_w, s_wlr, s_gain = ph.sem("w"), ph.sem("wlr"), ph.sem("scaled")
        s_whi, s_wlo = ph.sem("whi"), ph.sem("wlo")
        s_mm, s_hi, s_lo = ph.sem("mm"), ph.sem("hi"), ph.sem("lo")
        s_xm, s_xo, s_st = ph.sem("xm"), ph.sem("xo"), ph.sems("st", 2)
        units = [(m, c) for m in range(KH) for c in range(len(CHUNKS))]
        with nc.Block() as block:
            @block.sync
            def _(sp):
                sp.dma_start(wd[:, :, :], w_down.rearrange("(k p) n -> p k n", p=P)).then_inc(s_w, 16)
                sp.dma_start(gain[:, :], rms_w.rearrange("(k p) -> p k", p=P),
                             allow_slow_non_contiguous=True).then_inc(s_w, 16)
                for j, w in enumerate((wl, wr)):
                    sp.dma_start(wlr[:, :, j * HID:(j + 1) * HID], w.rearrange("(k p) n -> p k n", p=P)) \
                        .then_inc(s_wlr, 16)
                for t in range(T):
                    sp.wait_ge(s_xo, t + 1)
                    for j, x in enumerate((xl, xr)):
                        sp.dma_start(x[t * R:(t + 1) * R, :], out[:, t % 2, j * HID:(j + 1) * HID]) \
                            .then_inc(s_st[t % 2], 16)
                for h in range(2):
                    sp.wait_ge(s_st[h], 32 * T // 2)

            @block.vector
            def _(dve):
                dve.wait_ge(s_w, 32)
                for k in range(KD):
                    dve.tensor_scalar(wd[:, k, :], wd[:, k, :], gain[:, k:k + 1], None, ALU.mult).then_inc(s_gain, 1)
                dve.wait_ge(s_whi, 1)
                dve.tensor_tensor(wd_lo[:, :, :], wd[:, :, :], wd_hi[:, :, :].bitcast(F32), ALU.subtract) \
                   .then_inc(s_wlo, 1)
                dve.wait_ge(s_whi, 2)
                dve.tensor_tensor(wlr_lo[:, :, :], wlr[:, :, :], wlr_hi[:, :, :].bitcast(F32), ALU.subtract) \
                   .then_inc(s_wlo, 1)
                for u, (m, c) in enumerate(units):
                    o, n = CHUNKS[c]
                    dve.wait_ge(s_hi, u + 1)
                    dve.tensor_tensor(d_lo[:, m, o:o + n], bank[u % 4][:, 0:n], d_hi[:, m, o:o + n].bitcast(F32),
                                      ALU.subtract).then_inc(s_lo, 1)
                for t in range(T):
                    dve.wait_ge(s_xm, t + 1)
                    if t >= 2:
                        dve.wait_ge(s_st[t % 2], 32 * (t // 2))
                    dve.tensor_scalar(out[:, t % 2, :], bank[t % 4][0:R, :], rms[:, t:t + 1], None, ALU.mult) \
                       .then_inc(s_xo, 1)

            @block.scalar
            def _(act):
                act.wait_ge(s_gain, KD)
                act.activation(wd_hi[:, :, :], wd[:, :, :], ACT.Copy).then_inc(s_whi, 1)
                act.wait_ge(s_wlr, 32)
                act.activation(wlr_hi[:, :, :], wlr[:, :, :], ACT.Copy).then_inc(s_whi, 1)
                for u, (m, c) in enumerate(units):
                    o, n = CHUNKS[c]
                    act.wait_ge(s_mm, u + 1)
                    act.activation(d_hi[:, m, o:o + n], bank[u % 4][:, 0:n], ACT.Copy).then_inc(s_hi, 1)

            @block.tensor
            def _(pe):
                pe.wait_ge(s_wlo, 1)
                for u, (m, c) in enumerate(units):
                    o, n = CHUNKS[c]
                    if u >= 4:
                        pe.wait_ge(s_lo, u - 3)
                    for k in range(KD):
                        w = slice(m * P, (m + 1) * P)
                        ins = mm3(pe, bank[u % 4][:, 0:n], (wd_hi[:, k, w], wd_lo[:, k, w]),
                                  (act_hi[:, k, o:o + n], act_lo[:, k, o:o + n]), k == 0, k == KD - 1)
                    ins.then_inc(s_mm, 1)
                pe.wait_ge(s_wlo, 2)
                pe.wait_ge(s_lo, len(units))
                for t in range(T):
                    if t >= 4:
                        pe.wait_ge(s_xo, t - 3)
                    n = slice(t * R, (t + 1) * R)
                    for k in range(KH):
                        ins = mm3(pe, bank[t % 4][0:R, :], (d_hi[:, k, n], d_lo[:, k, n]),
                                  (wlr_hi[:, k, :], wlr_lo[:, k, :]), k == 0, k == KH - 1)
                    ins.then_inc(s_xm, 1)


def edge_phase(nc, src, dst, att, xl, xr, scores, filled):
    with Phase(nc, "edge") as ph:
        idx = ph.sb("idx", [R, 3, ET], I32)
        idf = ph.sb("idf", [R, 2, ET], F32)
        now = ph.sb("now", [R, 2, 3, EB], I32)
        gl = ph.sb("gl", [R, 2, EB, HID], F32)
        gr = ph.sb("gr", [R, 2, EB, HID], F32)
        attb = ph.sb("attb", [R, HID], F32)
        e = ph.sb("e", [R, 2, EB, HEADS], F32)
        s_idx, s_att = ph.sem("idx"), ph.sem("att")
        s_loop, s_diag = ph.sems("loop", 2), ph.sem("diag")
        s_now, s_g, s_e, s_sc = ph.sem("now"), ph.sems("g", 2), ph.sem("e"), ph.sem("sc")
        s_link, s_turn = ph.sem("link"), ph.sem("turn")
        batches, loops = ET // EB, T // EB
        s_fill, fill_count = filled
        flat = scores.rearrange("s h -> (s h)")
        diag = flat[0:(N * N - 1) * HEADS].rearrange("(i x) -> i x", x=(N + 1) * HEADS)

        with nc.Block() as block:
            @block.sync
            def _(sp):
                for j, a in enumerate((src, dst)):
                    sp.dma_start(idx[:, j, :], a.rearrange("(p k) -> p k", p=R)).then_inc(s_idx, 16)
                sp.dma_start(attb[:, :], att.rearrange("(o h) d -> o (h d)", o=1).to_broadcast([R, HID])) \
                    .then_inc(s_att, 16)
                for b in range(loops):
                    rows = slice(b * EB * R, (b + 1) * EB * R)
                    for g, x in ((gl, xl), (gr, xr)):
                        sp.dma_start(g[:, b, :, :], x[rows, :].rearrange("(t p) c -> p t c", p=R)) \
                            .then_inc(s_loop[b], 16)
                sp.wait_ge(s_fill, fill_count)
                for b in range(loops):
                    sp.wait_ge(s_e, b + 1)
                    for j in range(EB):
                        first = (b * EB + j) * R
                        n = min(R, N - 1 - first)
                        sp.dma_start(diag[first:first + n, 0:HEADS], e[0:n, b, j, :]).then_inc(s_diag, 16)
                sp.dma_start(scores[N * N - 1:N * N, :], e[R - 1:R, loops - 1, EB - 1, :]).then_inc(s_diag, 16)

            @block.vector
            def _(dve):
                dve.wait_ge(s_idx, 32)
                dve.tensor_copy(idf[:, 0, :], idx[:, 0, :])
                link = Link(dve, s_link)
                link(dve.tensor_copy(idf[:, 1, :], idx[:, 1, :]))
                link(dve.scalar_tensor_tensor(idf[:, 1, :], idf[:, 1, :], float(N), idf[:, 0, :], ALU.mult, ALU.add))
                link(dve.tensor_copy(idx[:, 2, :], idf[:, 1, :]))
                linked = link.count

                def columns(b, h):
                    dve.tensor_copy(now[:, h, :, :], idx[:, :, bass.ds(b * EB, EB)]).then_inc(s_now, 1)

                def score(h, link):
                    dve_in = gl[:, h, :, :]
                    link(dve.tensor_tensor(dve_in, dve_in, gr[:, h, :, :], ALU.add))
                    link(dve.scalar_tensor_tensor(dve_in, dve_in, 0.2, dve_in, ALU.mult, ALU.max))
                    for j in range(EB):
                        ins = dve.tensor_tensor(gl[:, h, j, :], gl[:, h, j, :], attb[:, :], ALU.mult)
                    link(ins)
                    dve.tensor_reduce(e[:, h, :, :], gl[:, h, :, :].rearrange("p t (a d) -> p t a d", a=HEADS),
                                      AX.X, ALU.add).then_inc(s_e, 1)

                dve.wait_ge(s_att, 16)
                columns(0, 0)
                for b in range(loops):
                    dve.wait_ge(s_loop[b], 32)
                    score(b, link)
                linked = link.count
                dve.wait_ge(s_diag, 16 * (T + 1))
                with dve.Fori(0, batches // 2 - 1) as i:
                    link = Link(dve, s_link, linked + 6 * i)
                    for h in range(2):
                        dve.wait_ge(s_sc, 16 * EB * (2 * i + h))
                        columns(2 * i + h + 1, 1 - h)
                        dve.wait_ge(s_g[h], 32 * EB * (i + 1))
                        score(h, link)
                linked += 6 * (batches // 2 - 1)
                link = Link(dve, s_link, linked)
                for h in range(2):
                    b = batches - 2 + h
                    dve.wait_ge(s_sc, 16 * EB * b)
                    if h == 0:
                        columns(b + 1, 1)
                    dve.wait_ge(s_g[h], 32 * EB * (batches // 2))
                    score(h, link)

            @block.gpsimd
            def _(pool):
                def gather(h, j):
                    for g, x, row in ((gl, xl, 0), (gr, xr, 1)):
                        pool.indirect_dma_start(g[:, h, j, :], None, x, bass.IndirectOffsetOnAxis(
                            ap=now[:, h, row, j:j + 1].bitcast(U32), axis=0)).then_inc(s_g[h], 16)

                def scatter(b, h, j):
                    pool.wait_ge(s_sc, 16 * EB * b + 16 * j)
                    pool.sem_inc(s_turn, 1)
                    pool.indirect_dma_start(scores, bass.IndirectOffsetOnAxis(
                        ap=now[:, h, 2, j:j + 1].bitcast(U32), axis=0), e[:, h, j, :], None).then_inc(s_sc, 16)

                pool.wait_ge(s_diag, 16 * (T + 1))
                pool.wait_ge(s_now, 1)
                for j in range(EB):
                    gather(0, j)
                with pool.Fori(0, batches // 2 - 1) as i:
                    for h in range(2):
                        pool.wait_ge(s_now, 2 * i + h + 2)
                        pool.wait_ge(s_e, loops + 2 * i + h + 1)
                        for j in range(EB):
                            scatter(2 * i + h, h, j)
                            gather(1 - h, j)
                for h in range(2):
                    b = batches - 2 + h
                    if h == 0:
                        pool.wait_ge(s_now, b + 2)
                    pool.wait_ge(s_e, loops + b + 1)
                    for j in range(EB):
                        scatter(b, h, j)
                        if h == 0:
                            gather(1, j)
                pool.wait_ge(s_sc, 16 * ET)


def count_phase(nc, src, dst, ident, at, deg_inv):
    with Phase(nc, "count") as ph:
        rows_i = ph.sb("rows_i", [PAIRS, 2, 2 * R], I32)
        rows = ph.sb("rows", [PAIRS, 2, 2 * R], F32)
        ends = ph.sb("ends", [R, 2, 2, 2 * PAIRS], F32)
        local = ph.sb("local", [R, 2, 2 * PAIRS], F32)
        lim = ph.sb("lim", [PAIRS, 2], F32)
        lim_diag = ph.sb("lim_diag", [PAIRS, 2, PAIRS], F32)
        ones = ph.sb("ones", [PAIRS, T], F32)
        first = ph.sb("first", [T, 2], F32)
        tile_i = ph.sb("tile_i", [T, 1], I32)
        pair_i = ph.sb("pair_i", [T, PAIRS], I32)
        pair = ph.sb("pair", [T, PAIRS], F32)
        out_of = ph.sb("out_of", [T, 2, PAIRS], F32)
        before = ph.sb("before", [T, T], F32)
        span = ph.sb("span", [T, 4], F32)
        span_i = ph.sb("span_i", [T, 4], I32)
        node_i = ph.sb("node_i", [R, N], I32)
        node = ph.sb("node", [R, N], F32)
        hot_s = ph.sb("hot_s", [R, 2, N], BF16)
        hot_d = ph.sb("hot_d", [R, 2, R], BF16)
        nil = ph.sb("nil", [R, N], BF16)
        a_sb = ph.sb("a_sb", [R, N], F32)
        a_tr = ph.sb("a_tr", [R, T, R], F32)
        deg = ph.sb("deg", [R, T], F32)
        pa = ph.ps("pa", [R, 3, BANK])
        pt = ph.ps("pt", [R, 3, BANK])
        pm = ph.ps("pm", [P, 2, BANK])
        s_rows, s_f, s_tr, s_ends = ph.sem("rows"), ph.sem("f"), ph.sem("tr"), ph.sem("ends")
        s_iota, s_link, s_lim, s_pl = ph.sem("iota"), ph.sem("link"), ph.sem("lim"), ph.sem("pl")
        s_num, s_base, s_span = ph.sem("num"), ph.sem("base"), ph.sem("span")
        s_nil, s_const = ph.sem("nil"), ph.sem("const")
        s_hot, s_used, s_a, s_cp = ph.sem("hot"), ph.sem("used"), ph.sem("a"), ph.sem("cp")
        s_at, s_sb, s_st = ph.sem("at"), ph.sem("sb"), ph.sem("st")
        s_local = ph.sem("local")

        def spans(eng, t):
            return [eng.value_load(span_i[t:t + 1, c:c + 1], min_val=lo, max_val=hi)
                    for c, lo, hi in ((0, 0, PAIRS - 1), (2, 1, PAIRS), (3, 0, T * PAIRS))]

        with nc.Block() as block:
            @block.sync
            def _(sp):
                for j, a in enumerate((src, dst)):
                    sp.dma_start(rows_i[:, j, :], a.rearrange("(q e) -> q e", e=2 * R)).then_inc(s_rows, 16)
                for t in range(T):
                    sp.wait_ge(s_sb, t + 1)
                    sp.dma_start(at.rearrange("b p d -> p b d")[:, :, t * R:(t + 1) * R], a_tr[:, :, :]) \
                        .then_inc(s_st, 16)
                sp.wait_ge(s_st, 16 * T)

            @block.gpsimd
            def _(pool):
                pool.iota(tile_i[:, :], [[0, 1]], base=0, channel_multiplier=R).then_inc(s_iota, 1)
                pool.iota(pair_i[:, :], [[1, PAIRS]], base=0, channel_multiplier=0).then_inc(s_iota, 1)
                pool.iota(node_i[:, :], [[1, N]], base=0, channel_multiplier=0).then_inc(s_iota, 1)
                pool.memset(before[:, :], 1.0).then_inc(s_const, 1)
                pool.memset(ones[:, :], 1.0).then_inc(s_const, 1)
                pool.memset(nil[:, :], 0.0).then_inc(s_nil, 1)
                pool.wait_ge(s_const, 2)
                pool.affine_select(out=before[:, :], in_=before[:, :], compare_op=ALU.is_gt, fill=0.0,
                                   base=0, pattern=[[1, T]], channel_multiplier=-1).then_inc(s_const, 1)

            @block.vector
            def _(dve):
                link = Link(dve, s_link)
                dve.wait_ge(s_iota, 3)
                dve.tensor_copy(pair[:, :], pair_i[:, :])
                dve.tensor_copy(node[:, :], node_i[:, :])
                dve.tensor_copy(first[:, 0:1], tile_i[:, :])
                dve.tensor_scalar(first[:, 1:2], tile_i[:, :], float(R), None, ALU.add)
                dve.wait_ge(s_rows, 32)
                ins = dve.tensor_copy(rows[:, :, :], rows_i[:, :, :])
                ins.then_inc(s_f, 1)
                dve.wait_ge(s_f, 1)
                dve.tensor_reduce(lim[:, 0:1], rows[:, 1, :], AX.X, ALU.min)
                link(dve.tensor_reduce(lim[:, 1:2], rows[:, 1, :], AX.X, ALU.max))
                for j in range(2):
                    dve.tensor_scalar(lim_diag[:, j, :], ident[0:PAIRS, 0:PAIRS], lim[:, j:j + 1], None, ALU.mult) \
                       .then_inc(s_lim, 1)
                dve.wait_ge(s_tr, 4)
                dve.tensor_copy(ends[:, :, :, 0:PAIRS], pm[0:R, 0, 0:4 * PAIRS].rearrange("p (a j q) -> p a j q", a=2, j=2)) \
                   .then_inc(s_ends, 1)
                dve.wait_ge(s_pl, 1)
                low, high = pm[0:T, 1, 0:PAIRS], pm[0:T, 1, PAIRS:2 * PAIRS]
                big = float(2 * PAIRS)
                dve.tensor_scalar(out_of[:, 0, :], high, first[:, 0:1], big, ALU.is_lt, ALU.mult)
                link(dve.tensor_scalar(out_of[:, 1, :], low, first[:, 1:2], big, ALU.is_ge, ALU.mult))
                dve.tensor_tensor(out_of[:, 0, :], out_of[:, 0, :], pair[:, :], ALU.add)
                link(dve.tensor_tensor(out_of[:, 1, :], pair[:, :], out_of[:, 1, :], ALU.subtract))
                dve.tensor_reduce(span[:, 0:1], out_of[:, 0, :], AX.X, ALU.min)
                link(dve.tensor_reduce(span[:, 1:2], out_of[:, 1, :], AX.X, ALU.max))
                link(dve.tensor_scalar(span[:, 0:1], span[:, 0:1], float(PAIRS - 1), None, ALU.min))
                link(dve.tensor_tensor(span[:, 2:3], span[:, 1:2], span[:, 0:1], ALU.subtract))
                dve.tensor_scalar(span[:, 2:3], span[:, 2:3], 1.0, 1.0, ALU.add, ALU.max).then_inc(s_num, 1)
                dve.wait_ge(s_base, 1)
                link(dve.tensor_copy(span[:, 3:4], pm[0:T, 1, 2 * PAIRS:2 * PAIRS + 1]))
                dve.tensor_copy(span_i[:, :], span[:, :]).then_inc(s_span, 1)
                dve.wait_ge(s_span, 1)
                dve.wait_ge(s_ends, 1)
                for t in range(T):
                    lo, num, base = spans(dve, t)
                    if t:
                        dve.wait_ge(s_a, t)
                    dve.tensor_scalar(local[:, :, 0:PAIRS], ends[:, 1, :, 0:PAIRS], float(-R * t), None, ALU.add) \
                       .then_inc(s_local, 1)
                    dve.wait_ge(s_local, t + 1)
                    with dve.Fori(0, num) as i:
                        q = lo + i
                        for j in range(2):
                            dve.wait_ge(s_used, 2 * (base + i))
                            dve.tensor_scalar(hot_d[:, j, :], node[:, 0:R], local[:, j, bass.ds(q, 1)], None,
                                              ALU.is_equal)
                            dve.tensor_scalar(hot_s[:, j, :], node[:, :], ends[:, 0, j, bass.ds(q, 1)], None,
                                              ALU.is_equal).then_inc(s_hot, 1)
                    dve.wait_ge(s_cp, t + 1)
                    dve.tensor_reduce(deg[:, t:t + 1], a_sb[:, :], AX.X, ALU.add)
                    dve.wait_ge(s_at, t + 1)
                    if t:
                        dve.wait_ge(s_st, 16 * t)
                    for b in range(3):
                        n = min(4, T - 4 * b)
                        ins = dve.tensor_copy(a_tr[:, 4 * b:4 * b + n, :],
                                              pt[:, b, 0:n * R].rearrange("p (b r) -> p b r", r=R))
                    ins.then_inc(s_sb, 1)
                dve.wait_ge(s_sb, T)
                link(dve.tensor_scalar(deg[:, :], deg[:, :], 1.0, None, ALU.max))
                link(dve.reciprocal(deg_inv[:, :], deg[:, :]))

            @block.scalar
            def _(act):
                for t in range(T):
                    act.wait_ge(s_a, t + 1)
                    if t:
                        act.wait_ge(s_sb, t)
                    for c, (o, n) in enumerate(CHUNKS):
                        ins = act.activation(a_sb[:, o:o + n], pa[:, c, 0:n], ACT.Copy)
                    ins.then_inc(s_cp, 1)

            @block.tensor
            def _(pe):
                pe.wait_ge(s_f, 1)
                for a in range(2):
                    for j in range(2):
                        at_ = (2 * a + j) * PAIRS
                        pe.transpose(pm[0:R, 0, at_:at_ + PAIRS], rows[:, a, j * R:(j + 1) * R],
                                     ident[0:PAIRS, 0:PAIRS]).then_inc(s_tr, 1)
                pe.wait_ge(s_lim, 2)
                pe.wait_ge(s_const, 3)
                for j in range(2):
                    ins = pe.matmul(pm[0:T, 1, j * PAIRS:(j + 1) * PAIRS], ones[:, :], lim_diag[:, j, :],
                                    start=True, stop=True)
                ins.then_inc(s_pl, 1)
                pe.wait_ge(s_num, 1)
                pe.matmul(pm[0:T, 1, 2 * PAIRS:2 * PAIRS + 1], before[:, :], span[:, 2:3], start=True, stop=True) \
                  .then_inc(s_base, 1)
                pe.wait_ge(s_nil, 1)
                pe.wait_ge(s_span, 1)
                for t in range(T):
                    lo, num, base = spans(pe, t)
                    if t:
                        pe.wait_ge(s_cp, t)
                    for c, (o, n) in enumerate(CHUNKS):
                        pe.matmul(pa[:, c, 0:n], nil[:, 0:R], nil[:, 0:n], start=True, stop=False)
                    with pe.Fori(0, num) as i:
                        for j in range(2):
                            pe.wait_ge(s_hot, 2 * (base + i) + j + 1)
                            for c, (o, n) in enumerate(CHUNKS):
                                ins = pe.matmul(pa[:, c, 0:n], hot_d[:, j, :], hot_s[:, j, o:o + n],
                                                start=False, stop=False)
                            ins.then_inc(s_used, 1)
                    for c, (o, n) in enumerate(CHUNKS):
                        ins = pe.matmul(pa[:, c, 0:n], nil[:, 0:R], nil[:, 0:n], start=False, stop=True)
                    ins.then_inc(s_a, 1)
                    pe.wait_ge(s_cp, t + 1)
                    if t:
                        pe.wait_ge(s_sb, t)
                    for b in range(T):
                        ins = pe.transpose(pt[:, b // 4, (b % 4) * R:(b % 4 + 1) * R], a_sb[:, b * R:(b + 1) * R],
                                           ident[0:R, 0:R])
                    ins.then_inc(s_at, 1)


def gat_phase(nc, scores, at, xl, ident, gat):
    with Phase(nc, "gat") as ph:
        sc = ph.sb("sc", [R, 2, N, HEADS], F32)
        cnt = ph.sb("cnt", [R, 2, T, R], F32)
        vals = ph.sb("vals", [R, T, HEADS, XW], F32)
        top = ph.sb("top", [R, 2, HEADS], F32)
        prob = ph.sb("prob", [R, 2, N], F32)
        wgt = ph.sb("wgt", [R, 2, T, R], F32)
        inv = ph.sb("inv", [R, 2, HEADS], F32)
        res = ph.sb("res", [R, 2, HID], F32)
        pt = [ph.ps(f"pt{h}", [R, 3, BANK]) for h in range(2)]
        po = ph.ps("po", [R, HEADS * XW])
        pr = ph.ps("pr", [P, KH, R])
        s_x, s_one = ph.sem("x"), ph.sem("one")
        s_sc, s_cnt, s_loop, s_top = ph.sems("sc", 2), ph.sems("cnt", 2), ph.sem("loop"), ph.sem("top")
        s_p, s_pt, s_w, s_o = ph.sem("p"), ph.sem("pt"), ph.sem("w"), ph.sem("o")
        s_res, s_rt, s_hi, s_lo, s_link = ph.sem("res"), ph.sem("rt"), ph.sem("hi"), ph.sem("lo"), ph.sem("link")
        gat_hi, gat_lo = gat
        rows = scores.rearrange("(t p s) h -> t p (s h)", p=R, s=N)
        with nc.Block() as block:
            @block.sync
            def _(sp):
                for k in range(T):
                    sp.dma_start(vals[:, k, :, 0:HD], xl[k * R:(k + 1) * R, :].rearrange("p (h d) -> p h d", h=HEADS)) \
                        .then_inc(s_x, 16)
                for t in range(T):
                    if t >= 2:
                        sp.wait_ge(s_p, HEADS * (t - 1))
                        sp.wait_ge(s_w, HEADS * (t - 1))
                    sp.dma_start(sc[:, t % 2, :, :].rearrange("p s h -> p (s h)"), rows[t]).then_inc(s_sc[t % 2], 16)
                    sp.dma_start(cnt[:, t % 2, :, :], at.rearrange("b p d -> p b d")[:, :, t * R:(t + 1) * R]) \
                        .then_inc(s_cnt[t % 2], 16)

            @block.gpsimd
            def _(pool):
                pool.memset(vals[:, :, :, HD:XW], 1.0).then_inc(s_one, 1)

            @block.vector
            def _(dve):
                with dve.Fori(0, T // 2) as i:
                    link = Link(dve, s_link, 4 * i)
                    for h in range(2):
                        t = 2 * i + h
                        dve.wait_ge(s_sc[h], 16 * i + 16)
                        dve.wait_ge(s_p, HEADS * 2 * i)
                        dve.tensor_reduce(top[:, h, :], sc[:, h, :, :].rearrange("p s h -> p h s"), AX.X, ALU.max,
                                          negate=True).then_inc(s_top, 1)
                        dve.wait_ge(s_cnt[h], 16 * i + 16)
                        diag = cnt[:, h, bass.ds(t, 1), :].rearrange("p b r -> p (b r)")
                        dve.tensor_tensor(diag, diag, ident[0:R, 0:R], ALU.add).then_inc(s_loop, 1)
                        dve.wait_ge(s_loop, t + 1)
                        for a in range(HEADS):
                            n = HEADS * t + a
                            dve.wait_ge(s_pt, n + 1)
                            if a >= 2:
                                dve.wait_ge(s_o, n - 1)
                            else:
                                dve.wait_ge(s_o, HEADS * t)
                            for b in range(3):
                                m = min(4, T - 4 * b)
                                ins = dve.tensor_tensor(wgt[:, a % 2, 4 * b:4 * b + m, :],
                                                        pt[a % 2][:, b, 0:m * R].rearrange("p (b r) -> p b r", r=R),
                                                        cnt[:, h, 4 * b:4 * b + m, :], ALU.mult)
                            ins.then_inc(s_w, 1)
                        dve.wait_ge(s_o, HEADS * (t + 1))
                        acc = po[:, :].rearrange("p (h d) -> p h d", h=HEADS)
                        link(dve.tensor_scalar(inv[:, h, :], acc[:, :, HD], 1e-16, None, ALU.add))
                        link(dve.reciprocal(inv[:, h, :], inv[:, h, :]))
                        dve.wait_ge(s_rt, 2 * i)
                        for a in range(HEADS):
                            ins = dve.tensor_scalar(res[:, h, a * HD:(a + 1) * HD], acc[:, a, 0:HD],
                                                    inv[:, h, a:a + 1], None, ALU.mult)
                        ins.then_inc(s_res, 1)
                        dve.wait_ge(s_hi, t + 1)
                        at_ = bass.ds(t * R, R)
                        dve.tensor_tensor(gat_lo[:, :, at_], pr[:, :, :], gat_hi[:, :, at_].bitcast(F32),
                                          ALU.subtract).then_inc(s_lo, 1)

            @block.scalar
            def _(act):
                with act.Fori(0, T // 2) as i:
                    for h in range(2):
                        t = 2 * i + h
                        act.wait_ge(s_top, t + 1)
                        for a in range(HEADS):
                            n = HEADS * t + a
                            if a >= 2:
                                act.wait_ge(s_pt, n - 1)
                            else:
                                act.wait_ge(s_pt, HEADS * t)
                            act.activation(prob[:, a % 2, :], sc[:, h, :, a], ACT.Exp, bias=top[:, h, a:a + 1]) \
                               .then_inc(s_p, 1)
                        act.wait_ge(s_rt, t + 1)
                        act.activation(gat_hi[:, :, bass.ds(t * R, R)], pr[:, :, :], ACT.Copy).then_inc(s_hi, 1)

            @block.tensor
            def _(pe):
                pe.wait_ge(s_x, 16 * T)
                pe.wait_ge(s_one, 1)

                def spread(t, a):
                    n = HEADS * t + a
                    pe.wait_ge(s_p, n + 1)
                    if a >= 2:
                        pe.wait_ge(s_w, n - 1)
                    else:
                        pe.wait_ge(s_w, HEADS * t)
                    for b in range(T):
                        ins = pe.transpose(pt[a % 2][:, b // 4, (b % 4) * R:(b % 4 + 1) * R],
                                           prob[:, a % 2, b * R:(b + 1) * R], ident[0:R, 0:R])
                    ins.then_inc(s_pt, 1)

                with pe.Fori(0, T // 2) as i:
                    for h in range(2):
                        t = 2 * i + h
                        spread(t, 0)
                        pe.wait_ge(s_res, t)
                        for a in range(HEADS):
                            if a + 1 < HEADS:
                                spread(t, a + 1)
                            pe.wait_ge(s_w, HEADS * t + a + 1)
                            for b in range(T):
                                ins = pe.matmul(po[:, a * XW:(a + 1) * XW], wgt[:, a % 2, b, :], vals[:, b, a, :],
                                                start=b == 0, stop=b == T - 1)
                            ins.then_inc(s_o, 1)
                        pe.wait_ge(s_res, t + 1)
                        pe.wait_ge(s_lo, t)
                        for k in range(KH):
                            ins = pe.transpose(pr[:, k, :], res[:, h, k * P:(k + 1) * P], ident[0:R, 0:R])
                        ins.then_inc(s_rt, 1)
MCHUNKS = [(0, 314), (314, 312), (626, 312), (938, 312)]
GROUP = SLAB // HD


def mix_phase(nc, name, act_hi, act_lo, wq, wk, wv, biases, sum_eps, mixt):
    NM = len(MCHUNKS)
    NQ = KH * NM
    UNITS = [("k", t) for t in range(T)] + [("v", t) for t in range(T)] + \
            [("q", j) for j in range(NQ)]
    NU, NPHI = len(UNITS), T + NQ
    with Phase(nc, name) as ph:
        raw = ph.sb("raw", [P, KD, SLAB], F32)
        w = {c: [ph.sb(f"w{c}_{s}", [P, KD, SLAB], F32R) for s in ("hi", "lo")] for c in "kvq"}
        kv_part = {c: [ph.sb(f"{c}_{s}", [R, T, SLAB], F32R) for s in ("hi", "lo")] for c in "kv"}
        q = [ph.sb(f"q_{s}", [P, KH, N], F32R) for s in ("hi", "lo")]
        low = ph.sb("low", [P, 2, MCHUNKS[0][1]], F32)
        val = ph.sb("val", [P, 2, MCHUNKS[0][1]], F32)
        block_f = ph.sb("block_f", [P, 2, P], F32)
        blocks = [ph.sb(f"block_{s}", [P, KH, 2, P], F32R) for s in ("hi", "lo")]
        ones_f = ph.sb("ones_f", [R, HD], F32)
        ones = ph.sb("ones", [R, HD], F32R)
        if biases is not None:
            bias_q = ph.sb("bias_q", [P, KD], F32)
            bias_q1 = ph.sb("bias_q1", [P, KD], F32)
            bias_kv = ph.sb("bias_kv", [R, 2, SLAB], F32)
        bank = [ph.ps(f"bank{b}", [P, BANK]) for b in range(4)]
        pkv = [ph.ps(f"pkv{b}", [P, BANK]) for b in range(KH)]
        s_raw, s_whi, s_wlo = ph.sem("raw"), ph.sem("whi"), ph.sem("wlo")
        s_bq, s_bkv, s_zero, s_one, s_ones = ph.sem("bq"), ph.sem("bkv"), ph.sem("zero"), ph.sem("one"), ph.sem("ones")
        s_mm, s_low, s_exp, s_val = ph.sem("mm"), ph.sem("low"), ph.sem("exp"), ph.sem("val")
        s_hi, s_lo, s_link, s_y = ph.sem("hi"), ph.sem("lo"), ph.sem("link"), ph.sem("y")
        s_kv, s_kvf, s_kvhi, s_kvlo = ph.sem("kv"), ph.sem("kvf"), ph.sem("kvhi"), ph.sem("kvlo")
        s_nd, s_quo, s_st = ph.sem("nd"), ph.sem("quo"), ph.sems("st", 2)
        s_b1 = ph.sem("b1")
        has_y = biases is not None
        NY = 2 * T if has_y else 0

        def shape(u):
            kind, j = UNITS[u]
            return (P, MCHUNKS[j % NM][1]) if kind == "q" else (R, SLAB)

        def phi_index(u):
            return u if u < T else u - T

        with nc.Block() as block:
            @block.sync
            def _(sp):
                def store(sp, g):
                    for j in range(NQ):
                        m, (o, n) = j // NM, MCHUNKS[j % NM]
                        sp.wait_ge(s_quo, NQ * g + j + 1)
                        rows = slice((KH * g + m) * P, (KH * g + m + 1) * P)
                        sp.dma_start(mixt[rows, o:o + n], low[:, j % 2, 0:n]).then_inc(s_st[j % 2], 16)

                if has_y:
                    sp.dma_start(bias_q[:, :], biases[0].rearrange("(k p) -> p k", p=P),
                                 allow_slow_non_contiguous=True).then_inc(s_bq, 16)
                for g in range(NSLAB):
                    cols = slice(g * SLAB, (g + 1) * SLAB)
                    for j, m in enumerate((wk, wv, wq)):
                        if 3 * g + j:
                            sp.wait_ge(s_wlo, 3 * g + j)
                        sp.dma_start(raw[:, :, :], m[:, cols].rearrange("(k p) n -> p k n", p=P)).then_inc(s_raw, 16)
                        if j:
                            continue
                        if g:
                            store(sp, g - 1)
                        if has_y:
                            if g:
                                sp.wait_ge(s_lo, NU * (g - 1) + 2 * T)
                            for c, b in enumerate(biases[1:]):
                                sp.dma_start(bias_kv[:, c, :], b[cols].rearrange("(o n) -> o n", o=1)
                                             .to_broadcast([R, SLAB])).then_inc(s_bkv, 16)
                store(sp, NSLAB - 1)
                for h in range(2):
                    sp.wait_ge(s_st[h], 16 * NQ // 2 * NSLAB)

            @block.gpsimd
            def _(pool):
                pool.memset(block_f[:, :, :], 0.0).then_inc(s_zero, 1)
                pool.memset(ones_f[:, :], 1.0).then_inc(s_one, 1)

            SPLITS = {0: ("v", 1), T: ("q", 2), 2 * T: ("k", 3)}

            @block.vector
            def _(dve):
                def split(c, s):
                    dve.wait_ge(s_whi, s + 1)
                    dve.tensor_tensor(w[c][1][:, :, :], raw[:, :, :], w[c][0][:, :, :].bitcast(F32), ALU.subtract) \
                       .then_inc(s_wlo, 1)

                def lower(g, u):
                    kind, j = UNITS[u]
                    p, n = shape(u)
                    at = bank[u % 4][0:p, 0:n]
                    dve.wait_ge(s_mm, NU * g + u + 1)
                    if has_y and kind != "q":
                        dve.wait_ge(s_lo, NU * g + max(u - 1, 0))
                        b = dve.tensor_tensor(val[0:p, u % 2, 0:n], at, bias_kv[:, 0 if kind == "k" else 1, :], ALU.add)
                        b.then_inc(s_y, 1)
                        if kind == "k":
                            dve.wait_ge(s_y, NY * g + u + 1)
                            at = val[0:p, u % 2, 0:n]
                    if kind == "v":
                        return
                    if kind == "q" and has_y:
                        dve.tensor_scalar(low[0:p, u % 2, 0:n], at, bias_q[:, bass.ds(KH * g + j // NM, 1)], 0.0,
                                          ALU.add, ALU.min).then_inc(s_low, 1)
                    else:
                        if u < 2:
                            for h in range(2):
                                dve.wait_ge(s_st[h], 16 * NQ // 2 * g)
                        dve.tensor_scalar(low[0:p, u % 2, 0:n], at, 0.0, None, ALU.min).then_inc(s_low, 1)

                def phi(g, u):
                    kind, j = UNITS[u]
                    if kind == "v":
                        return
                    p, n = shape(u)
                    dve.wait_ge(s_exp, NPHI * g + phi_index(u) + 1)
                    at = val[0:p, u % 2, 0:n] if has_y and kind == "k" else bank[u % 4][0:p, 0:n]
                    one = bias_q1[:, bass.ds(KH * g + j // NM, 1)] if has_y and kind == "q" else 1.0
                    dve.scalar_tensor_tensor(val[0:p, u % 2, 0:n], at, one, low[0:p, u % 2, 0:n], ALU.add, ALU.max) \
                       .then_inc(s_val, 1)

                def rest(g, u):
                    kind, j = UNITS[u]
                    p, n = shape(u)
                    dve.wait_ge(s_hi, NU * g + u + 1)
                    if kind == "q":
                        m, (o, n) = j // NM, MCHUNKS[j % NM]
                        hi, lo = (x[:, m, o:o + n] for x in q)
                    else:
                        hi, lo = (x[:, j, :] for x in kv_part[kind])
                    whole = bank[u % 4][0:p, 0:n] if kind == "v" and not has_y else val[0:p, u % 2, 0:n]
                    dve.tensor_tensor(lo, whole, hi.bitcast(F32), ALU.subtract).then_inc(s_lo, 1)

                def pair_sums(g, m):
                    dve.wait_ge(s_kv, KH * g + m + 1)
                    if m:
                        dve.wait_ge(s_kvlo, KH * g + m)
                    for a in range(2):
                        rows = slice(HD * a, HD * a + HD)
                        dve.tensor_copy(block_f[rows, 0, rows], pkv[m][rows, (2 * m + a) * HD:(2 * m + a + 1) * HD])
                        ins = dve.tensor_scalar(block_f[rows, 1, rows], pkv[m][rows, SLAB:SLAB + HD], sum_eps, None,
                                                ALU.add)
                    ins.then_inc(s_kvf, 1)
                    dve.wait_ge(s_kvhi, KH * g + m + 1)
                    dve.tensor_tensor(blocks[1][:, m, :, :], block_f[:, :, :], blocks[0][:, m, :, :].bitcast(F32),
                                      ALU.subtract).then_inc(s_kvlo, 1)

                def quotient(g, j, link):
                    n = MCHUNKS[j % NM][1]
                    num, den = (bank[2 * (j % 2) + x][:, 0:n] for x in range(2))
                    dve.wait_ge(s_nd, NQ * g + j + 1)
                    link(dve.tensor_scalar(val[:, j % 2, 0:n], den, 1e-6, None, ALU.add))
                    link(dve.reciprocal(val[:, j % 2, 0:n], val[:, j % 2, 0:n]))
                    if j < 2:
                        dve.wait_ge(s_exp, NPHI * (g + 1))
                    dve.wait_ge(s_st[j % 2], 16 * (NQ // 2 * g + j // 2))
                    dve.tensor_tensor(low[:, j % 2, 0:n], num, val[:, j % 2, 0:n], ALU.mult).then_inc(s_quo, 1)

                def slab(g, last):
                    link = Link(dve, s_link, 2 * NQ * g)
                    for u in range(NU + 2):
                        if u in SPLITS and not (last and u == 2 * T):
                            split(SPLITS[u][0], 3 * g + SPLITS[u][1])
                        if u >= 2:
                            rest(g, u - 2)
                        if u < NU:
                            lower(g, u)
                        if 1 <= u <= NU:
                            phi(g, u - 1)
                    for m in range(KH):
                        pair_sums(g, m)
                    for j in range(NQ):
                        quotient(g, j, link)

                dve.wait_ge(s_one, 1)
                dve.tensor_copy(ones[:, :], ones_f[:, :]).then_inc(s_ones, 1)
                if has_y:
                    dve.wait_ge(s_bq, 16)
                    dve.tensor_scalar(bias_q1[:, :], bias_q[:, :], 1.0, None, ALU.add).then_inc(s_b1, 1)
                    dve.wait_ge(s_b1, 1)
                split("k", 0)
                dve.wait_ge(s_zero, 1)
                with dve.Fori(0, NSLAB - 1) as g:
                    if has_y:
                        dve.wait_ge(s_bkv, 32 * g + 32)
                    slab(g, False)
                if has_y:
                    dve.wait_ge(s_bkv, 32 * NSLAB)
                slab(NSLAB - 1, True)

            @block.scalar
            def _(act):
                def split(c, s):
                    act.wait_ge(s_raw, 16 * s + 16)
                    act.activation(w[c][0][:, :, :], raw[:, :, :], ACT.Copy).then_inc(s_whi, 1)

                def exp(g, u):
                    if UNITS[u][0] == "v":
                        return
                    p, n = shape(u)
                    act.wait_ge(s_low, NPHI * g + phi_index(u) + 1)
                    act.activation(low[0:p, u % 2, 0:n], low[0:p, u % 2, 0:n], ACT.Exp).then_inc(s_exp, 1)

                def high(g, u):
                    kind, j = UNITS[u]
                    p, n = shape(u)
                    whole = val[0:p, u % 2, 0:n]
                    if kind != "v":
                        act.wait_ge(s_val, NPHI * g + phi_index(u) + 1)
                    elif has_y:
                        act.wait_ge(s_y, NY * g + u + 1)
                    else:
                        act.wait_ge(s_mm, NU * g + u + 1)
                        whole = bank[u % 4][0:p, 0:n]
                    if kind == "q":
                        m, (o, n) = j // NM, MCHUNKS[j % NM]
                        hi = q[0][:, m, o:o + n]
                    else:
                        hi = kv_part[kind][0][:, j, :]
                    act.activation(hi, whole, ACT.Copy).then_inc(s_hi, 1)

                def slab(g, last):
                    for u in range(NU + 1):
                        if u in SPLITS and not (last and u == 2 * T):
                            split(SPLITS[u][0], 3 * g + SPLITS[u][1])
                        if u < NU:
                            exp(g, u)
                        if u >= 1:
                            high(g, u - 1)
                    for m in range(KH):
                        act.wait_ge(s_kvf, KH * g + m + 1)
                        act.activation(blocks[0][:, m, :, :], block_f[:, :, :], ACT.Copy).then_inc(s_kvhi, 1)

                split("k", 0)
                with act.Fori(0, NSLAB - 1) as g:
                    slab(g, False)
                    act.wait_ge(s_nd, NQ * g + NQ)
                slab(NSLAB - 1, True)

            @block.tensor
            def _(pe):
                def project(g, u):
                    kind, j = UNITS[u]
                    p, n = shape(u)
                    out = bank[u % 4][0:p, 0:n]
                    if u in (0, T, 2 * T):
                        pe.wait_ge(s_wlo, 3 * g + u // T + 1)
                    if u < 4:
                        pe.wait_ge(s_quo, NQ * g)
                    else:
                        b = u - 4
                        if has_y and UNITS[b][0] != "q":
                            pe.wait_ge(s_y, NY * g + b + 1)
                        elif UNITS[b][0] == "v":
                            pe.wait_ge(s_lo, NU * g + b + 1)
                        else:
                            pe.wait_ge(s_val, NPHI * g + phi_index(b) + 1)
                    for k in range(KD):
                        if kind == "q":
                            m, (o, n) = j // NM, MCHUNKS[j % NM]
                            ins = mm3(pe, out, [x[:, k, m * P:(m + 1) * P] for x in w["q"]],
                                      (act_hi[:, k, o:o + n], act_lo[:, k, o:o + n]), k == 0, k == KD - 1)
                        else:
                            rows = slice(j * R, (j + 1) * R)
                            ins = mm3(pe, out, (act_hi[:, k, rows], act_lo[:, k, rows]),
                                      [x[:, k, :] for x in w[kind]], k == 0, k == KD - 1)
                    ins.then_inc(s_mm, 1)

                def slab(g):
                    for u in range(NU):
                        project(g, u)
                    pe.wait_ge(s_lo, NU * g + 2 * T)
                    for m in range(KH):
                        pair = slice(m * P, (m + 1) * P)
                        for t in range(T):
                            mm3(pe, pkv[m][:, 0:SLAB], [x[:, t, pair] for x in kv_part["k"]],
                                [x[:, t, :] for x in kv_part["v"]], t == 0, t == T - 1)
                        for t in range(T):
                            for s, x in enumerate(kv_part["k"]):
                                ins = pe.matmul(pkv[m][:, SLAB:SLAB + HD], x[:, t, pair], ones[:, :],
                                                start=(t, s) == (0, 0), stop=(t, s) == (T - 1, 1))
                        ins.then_inc(s_kv, 1)
                    pe.wait_ge(s_lo, NU * g + NU)
                    for j in range(NQ):
                        m, (o, n) = j // NM, MCHUNKS[j % NM]
                        if j % NM == 0:
                            pe.wait_ge(s_kvlo, KH * g + m + 1)
                        if j >= 2:
                            pe.wait_ge(s_quo, NQ * g + j - 1)
                        for x in range(2):
                            ins = mm3(pe, bank[2 * (j % 2) + x][:, 0:n], [b[:, m, x, :] for b in blocks],
                                      [y[:, m, o:o + n] for y in q], True, True)
                        ins.then_inc(s_nd, 1)

                pe.wait_ge(s_ones, 1)
                with pe.Fori(0, NSLAB - 1) as g:
                    slab(g)
                slab(NSLAB - 1)


def output_phase(nc, name, act_hi, act_lo, mixt, wo, bias, extra, resid, dst):
    KX = KH if extra is not None else 0
    KT = KD + KX
    with Phase(nc, name) as ph:
        part = ph.sb("part", [P, 2, N], F32)
        raw = ph.sb("raw", [P, KT, SLAB], F32)
        w = [[ph.sb(f"w{h}_{s}", [P, KT, SLAB], F32R) for s in ("hi", "lo")] for h in range(2)]
        res = ph.sb("res", [R, 2, T, SLAB], F32)
        if bias is not None:
            bb = ph.sb("bias", [R, D], F32)
        bank = [ph.ps(f"bank{b}", [P, BANK]) for b in range(4)]
        s_part, s_phi, s_plo = ph.sems("part", 2), ph.sem("phi"), ph.sem("plo")
        s_raw, s_whi, s_wlo = ph.sem("raw"), ph.sem("whi"), ph.sem("wlo")
        s_res, s_bias, s_add = ph.sems("res", 2), ph.sem("bias"), ph.sem("add")
        s_mm, s_out, s_st = ph.sem("mm"), ph.sem("out"), ph.sems("st", 2)
        n_raw = 32 if extra is not None else 16
        with nc.Block() as block:
            @block.sync
            def _(sp):
                def slab(g):
                    cols = slice(g * SLAB, (g + 1) * SLAB)
                    if g:
                        sp.wait_ge(s_wlo, g)
                    sp.dma_start(raw[:, 0:KD, :], wo[:, cols].rearrange("(k p) n -> p k n", p=P)).then_inc(s_raw, 16)
                    if extra is not None:
                        sp.dma_start(raw[:, KD:KT, :], extra[2][:, cols].rearrange("(k p) n -> p k n", p=P)) \
                            .then_inc(s_raw, 16)
                    if g >= 2:
                        sp.wait_ge(s_st[g % 2], 16 * (g // 2))
                    sp.dma_start(res[:, g % 2, :, :], resid[:, cols].rearrange("(t p) n -> p t n", p=R)) \
                        .then_inc(s_res[g % 2], 16)

                slab(0)
                if bias is not None:
                    sp.dma_start(bb[:, :], bias.rearrange("(o n) -> o n", o=1).to_broadcast([R, D])).then_inc(s_bias, 16)
                for k in range(KD):
                    if k >= 2:
                        sp.wait_ge(s_plo, k - 1)
                    sp.dma_start(part[:, k % 2, :], mixt[k * P:(k + 1) * P, :]).then_inc(s_part[k % 2], 16)
                for g in range(NSLAB):
                    if g + 1 < NSLAB:
                        slab(g + 1)
                    sp.wait_ge(s_out, T * (g + 1))
                    cols = slice(g * SLAB, (g + 1) * SLAB)
                    sp.dma_start(dst[:, cols].rearrange("(t p) n -> p t n", p=R), res[:, g % 2, :, :]) \
                        .then_inc(s_st[g % 2], 16)
                for h in range(2):
                    sp.wait_ge(s_st[h], 16 * NSLAB // 2)

            @block.gpsimd
            def _(pool):
                if bias is not None:
                    pool.wait_ge(s_bias, 16)
                    for g in range(NSLAB):
                        pool.wait_ge(s_res[g % 2], 16 * (g // 2 + 1))
                        for t in range(T):
                            ins = pool.tensor_tensor(res[:, g % 2, t, :], res[:, g % 2, t, :],
                                                     bb[:, g * SLAB:(g + 1) * SLAB], ALU.add)
                        ins.then_inc(s_add, 1)

            @block.vector
            def _(dve):
                def split(g, h):
                    dve.wait_ge(s_whi, g + 1)
                    dve.tensor_tensor(w[h][1][:, :, :], raw[:, :, :], w[h][0][:, :, :].bitcast(F32), ALU.subtract) \
                       .then_inc(s_wlo, 1)

                split(0, 0)
                for k in range(KD):
                    dve.wait_ge(s_phi, k + 1)
                    dve.tensor_tensor(act_lo[:, k, :], part[:, k % 2, :], act_hi[:, k, :].bitcast(F32), ALU.subtract) \
                       .then_inc(s_plo, 1)
                for g in range(NSLAB):
                    h = g % 2
                    if g + 1 < NSLAB:
                        split(g + 1, 1 - h)
                    if bias is not None:
                        dve.wait_ge(s_add, g + 1)
                    else:
                        dve.wait_ge(s_res[h], 16 * (g // 2 + 1))
                    for t in range(T):
                        u = T * g + t
                        dve.wait_ge(s_mm, u + 1)
                        dve.tensor_tensor(res[:, h, t, :], bank[u % 4][0:R, 0:SLAB], res[:, h, t, :], ALU.add) \
                           .then_inc(s_out, 1)

            @block.scalar
            def _(act):
                def split(g, h):
                    act.wait_ge(s_raw, n_raw * (g + 1))
                    if g >= 2:
                        act.wait_ge(s_mm, T * (g - 1))
                    act.activation(w[h][0][:, :, :], raw[:, :, :], ACT.Copy).then_inc(s_whi, 1)

                split(0, 0)
                for k in range(KD):
                    act.wait_ge(s_part[k % 2], 16 * (k // 2 + 1))
                    act.activation(act_hi[:, k, :], part[:, k % 2, :], ACT.Copy).then_inc(s_phi, 1)
                for g in range(1, NSLAB):
                    split(g, g % 2)

            @block.tensor
            def _(pe):
                pe.wait_ge(s_plo, KD)
                for g in range(NSLAB):
                    pe.wait_ge(s_wlo, g + 1)
                    for t in range(T):
                        u = T * g + t
                        if u >= 4:
                            pe.wait_ge(s_out, u - 3)
                        rows = slice(t * R, (t + 1) * R)
                        for k in range(KT):
                            lhs = (act_hi[:, k, rows], act_lo[:, k, rows]) if k < KD else \
                                  (extra[0][:, k - KD, rows], extra[1][:, k - KD, rows])
                            ins = mm3(pe, bank[u % 4][0:R, 0:SLAB], lhs, [x[:, k, :] for x in w[g % 2]],
                                      k == 0, k == KT - 1)
                        ins.then_inc(s_mm, 1)


E_N = 8
CAP0 = 2 * N // E_N
LIST = 3
CAPR = CAP0 // LIST
H0 = 512
KH0 = H0 // P
CAP1 = N // E_N
PAD1 = -CAP1 % 8
H1 = 256
KH1 = H1 // P
BLOCKS = N // P + E_N
TOPW = N + 8


def exact_exp(dve, link, x, whole, rest, poly):
    every = (slice(None),) * 3
    n, bits = whole[:, 0, :, :], whole[:, 1, :, :]
    link(dve.tensor_scalar(x[every], x[every], -87.0, None, ALU.max))
    link(dve.tensor_scalar(n, x[every], 1.0 / math.log(2.0), None, ALU.mult))
    link(dve.tensor_copy(poly[every], n))
    ln2 = 0.693359375
    dve.tensor_scalar(bits, poly[every], 127.0, None, ALU.add)
    link(dve.scalar_tensor_tensor(rest[every], poly[every], -ln2, x[every], ALU.mult, ALU.add))
    link(dve.scalar_tensor_tensor(rest[every], poly[every], ln2 - math.log(2.0), rest[every], ALU.mult, ALU.add))
    dve.tensor_scalar(bits, bits, 23, None, ALU.logical_shift_left)
    link(dve.tensor_scalar(poly[every], rest[every], 1.0 / math.factorial(10), None, ALU.mult))
    for k in range(9, 0, -1):
        link(dve.scalar_tensor_tensor(poly[every], poly[every], 1.0 / math.factorial(k), rest[every], ALU.add, ALU.mult))
    link(dve.scalar_tensor_tensor(x[every], poly[every], 1.0, bits.bitcast(F32), ALU.add, ALU.mult))


def gate_steps(ph, nc):
    gate = ph.sb("gate", [P, KD, E_N], F32)
    g_hi, g_lo = (ph.sb(f"gate_{s}", [P, KD, E_N], F32R) for s in ("hi", "lo"))
    prob = ph.sb("prob", [R, T, E_N], F32)
    top = ph.sb("gtop", [R, T], F32)
    ps = ph.ps("gates", [R, T, E_N])
    whole = ph.sb("whole", [R, 2, T, E_N], I32)
    rest = ph.sb("rest", [R, T, E_N], F32)
    poly = ph.sb("poly", [R, T, E_N], F32)
    s_g, s_ghi, s_glo, s_mm = ph.sem("g_in"), ph.sem("g_hi"), ph.sem("g_lo"), ph.sem("g_mm")
    s_prob, s_l = ph.sem("g_prob"), ph.sem("g_link")

    def sync(sp, w):
        sp.dma_start(gate[:, :, :], w.rearrange("(k p) e -> p k e", p=P)).then_inc(s_g, 16)

    def scalar(act):
        act.wait_ge(s_g, 16)
        act.activation(g_hi[:, :, :], gate[:, :, :], ACT.Copy).then_inc(s_ghi, 1)

    def tensor(pe, act_hi, act_lo):
        pe.wait_ge(s_glo, 1)
        for t in range(T):
            rows = slice(t * R, (t + 1) * R)
            for k in range(KD):
                ins = mm3(pe, ps[:, t, :], (act_hi[:, k, rows], act_lo[:, k, rows]),
                          (g_hi[:, k, :], g_lo[:, k, :]), k == 0, k == KD - 1)
        ins.then_inc(s_mm, 1)

    def vector(dve):
        link = Link(dve, s_l)
        wide = top[:, :].unsqueeze(2).to_broadcast([R, T, E_N])
        dve.wait_ge(s_ghi, 1)
        dve.tensor_tensor(g_lo[:, :, :], gate[:, :, :], g_hi[:, :, :].bitcast(F32), ALU.subtract).then_inc(s_glo, 1)
        dve.wait_ge(s_mm, 1)
        link(dve.tensor_reduce(top[:, :], ps[:, :, :], AX.X, ALU.max))
        link(dve.tensor_tensor(prob[:, :, :], ps[:, :, :], wide, ALU.subtract))
        exact_exp(dve, link, prob, whole, rest, poly)
        link(dve.tensor_reduce(top[:, :], prob[:, :, :], AX.X, ALU.add))
        link(dve.reciprocal(top[:, :], top[:, :]))
        dve.tensor_tensor(prob[:, :, :], prob[:, :, :], wide, ALU.mult).then_inc(s_prob, 1)

    return prob, s_prob, sync, scalar, tensor, vector


def spread_nodes(pe, pt, x, ident):
    for t in range(T):
        ins = pe.transpose(pt[:, t // 4, (t % 4) * R:(t % 4 + 1) * R], x[:, t, :], ident[0:R, 0:R])
    return ins


def gather_nodes(dve, out, pt):
    for b in range(3):
        n = min(4, T - 4 * b) * R
        ins = dve.tensor_copy(out[:, 4 * b * R:4 * b * R + n], pt[:, b, 0:n])
    return ins


def choose_phase(nc, act_hi, act_lo, gate_w, ident, chosen, share):
    with Phase(nc, "choose") as ph:
        prob, s_prob, g_sync, g_scalar, g_tensor, g_vector = gate_steps(ph, nc)
        work = ph.sb("work", [E_N, N], F32)
        best = ph.sb("best", [E_N, 2, CAP0], F32)
        place = ph.sb("place", [E_N, CAP0], U32)
        pt = ph.ps("pt", [E_N, 3, BANK])
        pc = ph.ps("pc", [CAPR, 2, LIST, E_N])
        s_tr, s_link, s_best, s_cols, s_got = ph.sem("tr"), ph.sem("link"), ph.sem("best"), ph.sem("cols"), ph.sem("got")
        with nc.Block() as block:
            @block.sync
            def _(sp):
                g_sync(sp, gate_w)

            @block.scalar
            def _(act):
                g_scalar(act)

            @block.tensor
            def _(pe):
                g_tensor(pe, act_hi, act_lo)
                pe.wait_ge(s_prob, 1)
                spread_nodes(pe, pt, prob, ident).then_inc(s_tr, 1)
                pe.wait_ge(s_best, 1)
                for a in range(2):
                    for j in range(LIST):
                        ins = pe.transpose(pc[:, a, j, :], best[:, a, j * CAPR:(j + 1) * CAPR], ident[0:E_N, 0:E_N])
                ins.then_inc(s_cols, 1)

            @block.vector
            def _(dve):
                g_vector(dve)
                dve.wait_ge(s_tr, 1)
                link = Link(dve, s_link)
                link(gather_nodes(dve, work, pt))
                for i in range(CAP0 // 8):
                    at = slice(8 * i, 8 * i + 8)
                    link(dve.max(best[:, 1, at], work[:, :]))
                    link(dve.max_index(place[:, at], best[:, 1, at], work[:, :]))
                    link(dve.match_replace(work[:, :], best[:, 1, at], work[:, :], -1.0))
                dve.tensor_copy(best[:, 0, :], place[:, :]).then_inc(s_best, 1)
                dve.wait_ge(s_cols, 1)
                dve.tensor_copy(chosen[:, :, :], pc[:, 0, :, :])
                dve.tensor_copy(share[:, :, :], pc[:, 1, :, :]).then_inc(s_got, 1)
                dve.wait_ge(s_got, 1)


def expert_phase(nc, y, chosen, share, w1, w2, ident, dst):
    with Phase(nc, "expert") as ph:
        now = ph.sb("now", [CAPR, 2, LIST], I32)
        rows = ph.sb("rows", [CAPR, 2, LIST, D], F32)
        x = [ph.sb(f"x_{s}", [P, KD, CAP0], F32R) for s in ("hi", "lo")]
        hid_f = ph.sb("hid_f", [P, 2, CAP0], F32)
        hid = [ph.sb(f"hid_{s}", [P, KH0, CAP0], F32R) for s in ("hi", "lo")]
        raw = ph.sb("raw", [P, 2, KD * H0], F32)
        a = [ph.sb(f"w1_{s}", [P, KD, H0], F32R) for s in ("hi", "lo")]
        b = [ph.sb(f"w2_{s}", [P, KH0, D], F32R) for s in ("hi", "lo")]
        out = ph.sb("out", [CAPR, LIST, D], F32)
        px = [ph.ps(f"px{i}", [P, BANK]) for i in range(4)]
        po = [ph.ps(f"po{i}", [P, BANK]) for i in range(4)]
        s_now, s_rows, s_raw = ph.sem("now"), ph.sems("rows", 2), ph.sems("raw", 2)
        s_ahi, s_alo, s_bhi, s_blo = ph.sem("ahi"), ph.sem("alo"), ph.sem("bhi"), ph.sem("blo")
        s_tr, s_xhi, s_xlo = ph.sem("tr"), ph.sem("xhi"), ph.sem("xlo")
        s_h, s_gelu, s_hhi, s_hlo = ph.sem("h"), ph.sem("gelu"), ph.sem("hhi"), ph.sem("hlo")
        s_o, s_out, s_add = ph.sem("o"), ph.sem("out"), ph.sem("add")
        OUTS = [(j, c) for j in range(LIST) for c in range(D // BANK)]
        NO = len(OUTS)
        with nc.Block() as block:
            @block.sync
            def _(sp):
                for e in range(E_N):
                    if e:
                        sp.wait_ge(s_alo, e)
                    sp.dma_start(raw[:, 0, :].rearrange("p (k h) -> p k h", h=H0),
                                 w1[e].rearrange("(k p) h -> p k h", p=P)).then_inc(s_raw[0], 16)
                    if e:
                        sp.wait_ge(s_blo, e)
                    sp.dma_start(raw[:, 1, :].rearrange("p (k d) -> p k d", d=D),
                                 w2[e].rearrange("(k p) d -> p k d", p=P)).then_inc(s_raw[1], 16)

            @block.gpsimd
            def _(pool):
                def gather(h):
                    for j in range(LIST):
                        pool.indirect_dma_start(rows[:, h, j, :], None, y, bass.IndirectOffsetOnAxis(
                            ap=now[:, h, j:j + 1].bitcast(U32), axis=0)).then_inc(s_rows[h], 16)

                pool.wait_ge(s_now, 1)
                gather(0)
                for e in range(E_N):
                    if e + 1 < E_N:
                        pool.wait_ge(s_now, e + 2)
                        gather((e + 1) % 2)
                    pool.wait_ge(s_add, 16 * LIST * e)
                    for j in range(LIST):
                        pool.wait_ge(s_out, NO * e + 2 * (j + 1))
                        pool.indirect_dma_start(dst, bass.IndirectOffsetOnAxis(
                            ap=now[:, e % 2, j:j + 1].bitcast(U32), axis=0), out[:, j, :], None,
                            compute_op=ALU.add).then_inc(s_add, 16)
                pool.wait_ge(s_add, 16 * LIST * E_N)

            @block.vector
            def _(dve):
                def list_of(e, h):
                    dve.tensor_copy(now[:, h, :], chosen[:, :, bass.ds(e, 1)].rearrange("p j o -> p (j o)")) \
                       .then_inc(s_now, 1)

                def split(e):
                    dve.wait_ge(s_ahi, e + 1)
                    dve.tensor_tensor(a[1][:, :, :].rearrange("p k h -> p (k h)"), raw[:, 0, :],
                                      a[0][:, :, :].rearrange("p k h -> p (k h)").bitcast(F32), ALU.subtract) \
                       .then_inc(s_alo, 1)

                def expert(e, h, last=False):
                    if not last:
                        dve.wait_ge(s_add, 16 * LIST * e)
                        list_of(e + 1, 1 - h)
                    for k in range(KD):
                        dve.wait_ge(s_xhi, KD * e + k + 1)
                        dve.tensor_tensor(x[1][:, k, :], px[k % 4][:, 0:CAP0], x[0][:, k, :].bitcast(F32),
                                          ALU.subtract).then_inc(s_xlo, 1)
                    dve.wait_ge(s_bhi, e + 1)
                    dve.tensor_tensor(b[1][:, :, :].rearrange("p k d -> p (k d)"), raw[:, 1, :],
                                      b[0][:, :, :].rearrange("p k d -> p (k d)").bitcast(F32), ALU.subtract) \
                       .then_inc(s_blo, 1)
                    for m in range(KH0):
                        dve.wait_ge(s_hhi, KH0 * e + m + 1)
                        dve.tensor_tensor(hid[1][:, m, :], hid_f[:, m % 2, :], hid[0][:, m, :].bitcast(F32),
                                          ALU.subtract).then_inc(s_hlo, 1)
                    if not last:
                        split(e + 1)
                    dve.wait_ge(s_add, 16 * LIST * e)
                    for i, (j, c) in enumerate(OUTS):
                        dve.wait_ge(s_o, NO * e + i + 1)
                        dve.tensor_scalar(out[:, j, c * BANK:(c + 1) * BANK], po[i % 4][0:CAPR, :],
                                          share[:, j, bass.ds(e, 1)], None, ALU.mult).then_inc(s_out, 1)

                list_of(0, 0)
                split(0)
                with dve.Fori(0, E_N // 2 - 1) as i:
                    for h in range(2):
                        expert(2 * i + h, h)
                expert(E_N - 2, 0)
                expert(E_N - 1, 1, last=True)

            @block.scalar
            def _(act):
                def split(e):
                    act.wait_ge(s_raw[0], 16 * e + 16)
                    act.activation(a[0][:, :, :].rearrange("p k h -> p (k h)"), raw[:, 0, :], ACT.Copy).then_inc(s_ahi, 1)

                def expert(e, last=False):
                    for k in range(KD):
                        act.wait_ge(s_tr, KD * e + k + 1)
                        act.activation(x[0][:, k, :], px[k % 4][:, 0:CAP0], ACT.Copy).then_inc(s_xhi, 1)
                    act.wait_ge(s_raw[1], 16 * e + 16)
                    act.activation(b[0][:, :, :].rearrange("p k d -> p (k d)"), raw[:, 1, :], ACT.Copy).then_inc(s_bhi, 1)
                    for m in range(KH0):
                        act.wait_ge(s_h, KH0 * e + m + 1)
                        if m >= 2:
                            act.wait_ge(s_hlo, KH0 * e + m - 1)
                        act.activation(hid_f[:, m % 2, :], px[m % 4][:, 0:CAP0], ACT.Gelu).then_inc(s_gelu, 1)
                        act.wait_ge(s_gelu, KH0 * e + m + 1)
                        act.activation(hid[0][:, m, :], hid_f[:, m % 2, :], ACT.Copy).then_inc(s_hhi, 1)
                    if not last:
                        split(e + 1)
                    act.wait_ge(s_o, NO * e + NO)

                split(0)
                with act.Fori(0, E_N - 1) as e:
                    expert(e)
                expert(E_N - 1, last=True)

            @block.tensor
            def _(pe):
                def expert(e, h, turn):
                    pe.wait_ge(s_rows[h], 16 * LIST * turn)
                    for k in range(KD):
                        if k >= 4:
                            pe.wait_ge(s_xlo, KD * e + k - 3)
                        for j in range(LIST):
                            ins = pe.transpose(px[k % 4][:, j * CAPR:(j + 1) * CAPR],
                                               rows[:, h, j, k * P:(k + 1) * P], ident[0:CAPR, 0:CAPR])
                        ins.then_inc(s_tr, 1)
                    pe.wait_ge(s_xlo, KD * (e + 1))
                    pe.wait_ge(s_alo, e + 1)
                    for m in range(KH0):
                        cols = slice(m * P, (m + 1) * P)
                        for k in range(KD):
                            ins = mm3(pe, px[m % 4][:, 0:CAP0], [w[:, k, cols] for w in a], [v[:, k, :] for v in x],
                                      k == 0, k == KD - 1)
                        ins.then_inc(s_h, 1)
                    pe.wait_ge(s_blo, e + 1)
                    pe.wait_ge(s_hlo, KH0 * (e + 1))
                    for i, (j, c) in enumerate(OUTS):
                        if i < 4:
                            pe.wait_ge(s_out, NO * e)
                        else:
                            pe.wait_ge(s_out, NO * e + i - 3)
                        toks, cols = slice(j * CAPR, (j + 1) * CAPR), slice(c * BANK, (c + 1) * BANK)
                        for k in range(KH0):
                            ins = mm3(pe, po[i % 4][0:CAPR, :], [v[:, k, toks] for v in hid], [w[:, k, cols] for w in b],
                                      k == 0, k == KH0 - 1)
                        ins.then_inc(s_o, 1)

                with pe.Fori(0, E_N // 2) as i:
                    for h in range(2):
                        expert(2 * i + h, h, i + 1)


def sage_phase(nc, name, act_hi, act_lo, at, deg_inv, w_self, w_neigh, bias, resid, dst):
    with Phase(nc, name) as ph:
        cnt = ph.sb("cnt", [R, T, N], F32R)
        raw = ph.sb("raw", [P, KD, SLAB], F32)
        w = [[ph.sb(f"w{c}_{s}", [P, KD, SLAB], F32R) for s in ("hi", "lo")] for c in "ns"]
        z = [ph.sb(f"z_{s}", [R, T, SLAB], F32R) for s in ("hi", "lo")]
        add = ph.sb("add", [R, 2, SLAB], F32)
        bb = ph.sb("bias", [R, D], F32)
        own = ph.sb("own", [R, 2, SLAB], F32)
        out = ph.sb("out", [R, 2, SLAB], F32)
        pz = [ph.ps(f"pz{i}", [R, BANK]) for i in range(4)]
        pown = [ph.ps(f"pown{i}", [R, BANK]) for i in range(2)]
        pagg = [ph.ps(f"pagg{i}", [R, BANK]) for i in range(2)]
        s_cnt, s_bias, s_raw, s_whi, s_wlo = ph.sem("cnt"), ph.sem("bias"), ph.sem("raw"), ph.sem("whi"), ph.sem("wlo")
        s_zm, s_zhi, s_zlo = ph.sem("zm"), ph.sem("zhi"), ph.sem("zlo")
        s_add, s_sum, s_own, s_agg = ph.sems("add", 2), ph.sem("sum"), ph.sem("own"), ph.sem("agg")
        s_part, s_tot, s_out, s_st = ph.sem("part"), ph.sem("tot"), ph.sem("out"), ph.sems("st", 2)
        tiles = NSLAB * T

        def store(sp, u):
            g, t = u // T, u % T
            sp.wait_ge(s_out, u + 1)
            sp.dma_start(dst[t * R:(t + 1) * R, g * SLAB:(g + 1) * SLAB], out[:, u % 2, :]).then_inc(s_st[u % 2], 16)

        with nc.Block() as block:
            @block.sync
            def _(sp):
                def slab(s):
                    if s:
                        sp.wait_ge(s_wlo, s)
                    m = (w_neigh, w_self)[s % 2]
                    sp.dma_start(raw[:, :, :], m[:, s // 2 * SLAB:(s // 2 + 1) * SLAB].rearrange("(k p) n -> p k n", p=P)) \
                        .then_inc(s_raw, 16)

                slab(0)
                sp.dma_start(bb[:, :], bias.rearrange("(o n) -> o n", o=1).to_broadcast([R, D])).then_inc(s_bias, 16)
                for k in range(T):
                    sp.dma_start(cnt[:, k, :].bitcast(F32), at[k]).then_inc(s_cnt, 16)
                slab(1)
                for u in range(tiles):
                    g, t = u // T, u % T
                    rows, cols = slice(t * R, (t + 1) * R), slice(g * SLAB, (g + 1) * SLAB)
                    if t == 4 and g + 1 < NSLAB:
                        slab(2 * g + 2)
                    if t == 9 and g + 1 < NSLAB:
                        slab(2 * g + 3)
                    if resid is not None:
                        if u >= 2:
                            sp.wait_ge(s_part, u - 1)
                        sp.dma_start(add[:, u % 2, :], resid[rows, cols]).then_inc(s_add[u % 2], 16)
                    if u:
                        store(sp, u - 1)
                store(sp, tiles - 1)
                for h in range(2):
                    sp.wait_ge(s_st[h], 16 * tiles // 2)

            @block.gpsimd
            def _(pool):
                if resid is not None:
                    pool.wait_ge(s_bias, 16)
                    for u in range(tiles):
                        g = u // T
                        pool.wait_ge(s_add[u % 2], 16 * (u // 2 + 1))
                        pool.tensor_tensor(add[:, u % 2, :], add[:, u % 2, :], bb[:, g * SLAB:(g + 1) * SLAB], ALU.add) \
                            .then_inc(s_sum, 1)

            @block.vector
            def _(dve):
                def split(s):
                    dve.wait_ge(s_whi, s + 1)
                    dve.tensor_tensor(w[s % 2][1][:, :, :], raw[:, :, :], w[s % 2][0][:, :, :].bitcast(F32), ALU.subtract) \
                       .then_inc(s_wlo, 1)

                split(0)
                split(1)
                dve.wait_ge(s_bias, 16)
                for g in range(NSLAB):
                    for t in range(T):
                        u = T * g + t
                        dve.wait_ge(s_zhi, u + 1)
                        dve.tensor_tensor(z[1][:, t, :], pz[u % 4][:, 0:SLAB], z[0][:, t, :].bitcast(F32), ALU.subtract) \
                           .then_inc(s_zlo, 1)
                    for t in range(T):
                        u = T * g + t
                        if t == 5 and g + 1 < NSLAB:
                            split(2 * g + 2)
                        dve.wait_ge(s_own, u + 1)
                        if resid is not None:
                            dve.wait_ge(s_sum, u + 1)
                            more = add[:, u % 2, :]
                        else:
                            more = bb[:, g * SLAB:(g + 1) * SLAB]
                        dve.tensor_tensor(own[:, u % 2, :], pown[u % 2][:, 0:SLAB], more, ALU.add).then_inc(s_part, 1)
                        dve.wait_ge(s_part, u + 1)
                        dve.wait_ge(s_agg, u + 1)
                        if u >= 2:
                            dve.wait_ge(s_st[u % 2], 16 * (u // 2))
                        whole = out if resid is not None else own
                        dve.scalar_tensor_tensor(whole[:, u % 2, :], pagg[u % 2][:, 0:SLAB], deg_inv[:, t:t + 1],
                                                 own[:, u % 2, :], ALU.mult, ALU.add).then_inc(s_tot, 1)
                        if resid is None:
                            dve.wait_ge(s_tot, u + 1)
                            dve.tensor_scalar(out[:, u % 2, :], own[:, u % 2, :], 0.0, None, ALU.max).then_inc(s_out, 1)
                        else:
                            dve.wait_ge(s_tot, u + 1)
                            dve.sem_inc(s_out, 1)
                    if g + 1 < NSLAB:
                        split(2 * g + 3)

            @block.scalar
            def _(act):
                def split(s):
                    act.wait_ge(s_raw, 16 * (s + 1))
                    act.activation(w[s % 2][0][:, :, :], raw[:, :, :], ACT.Copy).then_inc(s_whi, 1)

                split(0)
                split(1)
                for g in range(NSLAB):
                    for t in range(T):
                        u = T * g + t
                        act.wait_ge(s_zm, u + 1)
                        act.activation(z[0][:, t, :], pz[u % 4][:, 0:SLAB], ACT.Copy).then_inc(s_zhi, 1)
                    if g + 1 < NSLAB:
                        split(2 * g + 2)
                        act.wait_ge(s_own, T * (g + 1))
                        split(2 * g + 3)
                        act.wait_ge(s_agg, T * (g + 1))

            @block.tensor
            def _(pe):
                for g in range(NSLAB):
                    pe.wait_ge(s_wlo, 2 * g + 1)
                    for t in range(T):
                        u = T * g + t
                        if u >= 4:
                            pe.wait_ge(s_zlo, u - 3)
                        rows = slice(t * R, (t + 1) * R)
                        for k in range(KD):
                            ins = mm3(pe, pz[u % 4][:, 0:SLAB], (act_hi[:, k, rows], act_lo[:, k, rows]),
                                      [x[:, k, :] for x in w[0]], k == 0, k == KD - 1)
                        ins.then_inc(s_zm, 1)
                    pe.wait_ge(s_wlo, 2 * g + 2)
                    if not g:
                        pe.wait_ge(s_cnt, 16 * T)
                    for t in range(T):
                        u = T * g + t
                        if u >= 2:
                            pe.wait_ge(s_tot, u - 1)
                        rows = slice(t * R, (t + 1) * R)
                        for k in range(KD):
                            ins = mm3(pe, pown[u % 2][:, 0:SLAB], (act_hi[:, k, rows], act_lo[:, k, rows]),
                                      [x[:, k, :] for x in w[1]], k == 0, k == KD - 1)
                        ins.then_inc(s_own, 1)
                        if not t:
                            pe.wait_ge(s_zlo, T * (g + 1))
                        for k in range(T):
                            for s in range(2):
                                ins = pe.matmul(pagg[u % 2][:, 0:SLAB], cnt[:, k, rows], z[s][:, k, :],
                                                start=(k, s) == (0, 0), stop=(k, s) == (T - 1, 1))
                        ins.then_inc(s_agg, 1)


def assign_phase(nc, act_hi, act_lo, gate_w, ident, slots, expert_of):
    with Phase(nc, "assign") as ph:
        prob, s_prob, g_sync, g_scalar, g_tensor, g_vector = gate_steps(ph, nc)
        work = ph.sb("work", [E_N, TOPW], F32)
        best = ph.sb("best", [E_N, 8], F32)
        picked = ph.sb("picked", [E_N, N], F32)
        pick = ph.sb("pick", [R, T, E_N], F32)
        score = ph.sb("score", [R, T, E_N], F32)
        one = ph.sb("one", [R, T], F32)
        hot = ph.sb("hot", [R, T, E_N], F32)
        num_i = ph.sb("num_i", [R, E_N], I32)
        num = ph.sb("num", [R, E_N], F32)
        first = ph.sb("first", [R, T], F32)
        hot_e = ph.sb("hot_e", [E_N, N], F32)
        rank = ph.sb("rank", [E_N, N], F32)
        size = ph.sb("size", [E_N, 4], F32)
        size_i = ph.sb("size_i", [E_N, 2], I32)
        before = ph.sb("before", [E_N, E_N], F32)
        ones = ph.sb("ones", [E_N, 2], F32)
        block_i = ph.sb("block_i", [E_N, BLOCKS], I32)
        ends = ph.sb("ends", [E_N, BLOCKS], F32)
        slot = ph.sb("slot", [R, T], I32)
        node = ph.sb("node", [R, T], I32)
        row = ph.sb("row", [R, T, 2], F32)
        free = ph.sb("free", [P, BLOCKS, 2], F32)
        pt = ph.ps("pt", [E_N, 3, BANK])
        pp = ph.ps("pp", [R, T, E_N])
        ps = ph.ps("ps", [R, BANK])
        pe_of = ph.ps("pe_of", [1, BANK])
        s_tr, s_link, s_pick, s_back, s_hot, s_he = (ph.sem(x) for x in ("tr", "link", "pick", "back", "hot", "he"))
        s_iota, s_const, s_size, s_start = (ph.sem(x) for x in ("iota", "const", "size", "start"))
        s_val, s_slot, s_ends, s_ex, s_row = (ph.sem(x) for x in ("val", "slot", "ends", "ex", "row"))
        s_free, s_fill, s_put, s_done = (ph.sem(x) for x in ("free", "fill", "put", "done"))
        with nc.Block() as block:
            @block.sync
            def _(sp):
                g_sync(sp, gate_w)
                sp.wait_ge(s_free, 2)
                sp.dma_start(slots.rearrange("(b p) c -> p b c", p=P), free[:, :, :]).then_inc(s_fill, 16)

            @block.gpsimd
            def _(pool):
                pool.iota(num_i[:, :], [[1, E_N]], base=0, channel_multiplier=0).then_inc(s_iota, 1)
                pool.iota(block_i[:, :], [[1, BLOCKS]], base=0, channel_multiplier=0).then_inc(s_iota, 1)
                pool.iota(node[:, :], [[R, T]], base=0, channel_multiplier=1).then_inc(s_iota, 1)
                pool.iota(free[:, :, 0].bitcast(I32), [[0, BLOCKS]], base=N, channel_multiplier=0).then_inc(s_free, 1)
                pool.memset(free[:, :, 1], 0.0).then_inc(s_free, 1)
                pool.memset(ones[:, :], 1.0).then_inc(s_const, 1)
                pool.memset(before[:, :], 1.0).then_inc(s_const, 1)
                pool.wait_ge(s_const, 2)
                pool.affine_select(out=before[:, :], in_=before[:, :], compare_op=ALU.is_gt, fill=0.0,
                                   base=0, pattern=[[1, E_N]], channel_multiplier=-1).then_inc(s_const, 1)
                pool.wait_ge(s_fill, 16)
                pool.wait_ge(s_row, 1)
                for t in range(T):
                    pool.indirect_dma_start(slots, bass.IndirectOffsetOnAxis(ap=slot[:, t:t + 1].bitcast(U32), axis=0),
                                            row[:, t, :], None).then_inc(s_put, 16)
                pool.wait_ge(s_put, 16 * T)

            @block.scalar
            def _(act):
                g_scalar(act)

            @block.tensor
            def _(pe):
                g_tensor(pe, act_hi, act_lo)
                pe.wait_ge(s_prob, 1)
                spread_nodes(pe, pt, prob, ident).then_inc(s_tr, 1)
                pe.wait_ge(s_pick, 1)
                for t in range(T):
                    ins = pe.transpose(pp[:, t, :], picked[:, t * R:(t + 1) * R], ident[0:E_N, 0:E_N])
                ins.then_inc(s_back, 1)
                pe.wait_ge(s_hot, 1)
                spread_nodes(pe, pt, hot, ident).then_inc(s_tr, 1)
                pe.wait_ge(s_const, 3)
                pe.wait_ge(s_size, 1)
                pe.matmul(ps[0:E_N, 0:2], before[:, :], size[:, 2:4], start=True, stop=True).then_inc(s_start, 1)
                pe.wait_ge(s_val, 1)
                for t in range(T):
                    ins = pe.matmul(ps[:, 2 + t:3 + t], rank[:, t * R:(t + 1) * R], ones[:, 0:1], start=True, stop=True)
                ins.then_inc(s_slot, 1)
                pe.wait_ge(s_ends, 1)
                pe.matmul(pe_of[0:1, 0:BLOCKS], ones[:, 0:1], ends[:, :], start=True, stop=True).then_inc(s_ex, 1)

            @block.vector
            def _(dve):
                g_vector(dve)
                link = Link(dve, s_link)
                dve.wait_ge(s_tr, 1)
                dve.memset(work[:, N:N + PAD1], 2.0)
                dve.memset(work[:, N + PAD1:TOPW], -2.0)
                link(gather_nodes(dve, work, pt))
                for i in range((CAP1 + PAD1) // 8):
                    link(dve.max(best[:, :], work[:, :]))
                    link(dve.match_replace(work[:, :], best[:, :], work[:, :], -1.0))
                dve.tensor_scalar(picked[:, :], work[:, 0:N], 0.0, None, ALU.is_lt).then_inc(s_pick, 1)
                dve.wait_ge(s_back, 1)
                dve.wait_ge(s_iota, 3)
                dve.tensor_copy(num[:, :], num_i[:, :])
                link(dve.tensor_reduce(one[:, :], pp[:, :, :], AX.X, ALU.max))
                link(dve.tensor_scalar(one[:, :], one[:, :], -1.0, 1.0, ALU.mult, ALU.add))
                wide = one[:, :].unsqueeze(2).to_broadcast([R, T, E_N])
                link(dve.tensor_tensor(pick[:, :, :], pp[:, :, :], wide, ALU.add))
                link(dve.tensor_tensor(score[:, :, :], prob[:, :, :], pick[:, :, :], ALU.mult))
                link(dve.tensor_scalar(pick[:, :, :], pick[:, :, :], -1.0, None, ALU.add))
                link(dve.tensor_tensor(score[:, :, :], score[:, :, :], pick[:, :, :], ALU.add))
                link(dve.tensor_reduce(one[:, :], score[:, :, :], AX.X, ALU.max))
                dve.tensor_copy(row[:, :, 1], one[:, :])
                link(dve.tensor_tensor(pick[:, :, :], score[:, :, :], wide, ALU.is_lt))
                numbers = num[:, :].unsqueeze(1).to_broadcast([R, T, E_N])
                link(dve.scalar_tensor_tensor(pick[:, :, :], pick[:, :, :], float(E_N), numbers, ALU.mult, ALU.add))
                link(dve.tensor_reduce(first[:, :], pick[:, :, :], AX.X, ALU.min))
                dve.tensor_tensor(hot[:, :, :], pick[:, :, :], first[:, :].unsqueeze(2).to_broadcast([R, T, E_N]),
                                  ALU.is_equal).then_inc(s_hot, 1)
                dve.tensor_copy(row[:, :, 0].bitcast(I32), node[:, :])
                dve.wait_ge(s_tr, 2)
                link(gather_nodes(dve, hot_e, pt))
                link(dve.tensor_tensor_scan(rank[:, :], hot_e[:, :], hot_e[:, :], 0.0, ALU.add, ALU.max))
                link(dve.tensor_scalar(size_i[:, 0:1], rank[:, N - 1:N], float(P - 1), None, ALU.add))
                link(dve.tensor_scalar(size_i[:, 1:2], size_i[:, 0:1], P.bit_length() - 1, None, ALU.arith_shift_right))
                dve.tensor_copy(size[:, 2:3], size_i[:, 1:2])
                dve.tensor_copy(size[:, 3:4], size_i[:, 1:2]).then_inc(s_size, 1)
                dve.wait_ge(s_start, 1)
                link(dve.tensor_scalar(size[:, 0:1], ps[0:E_N, 0:1], float(P), -1.0, ALU.mult, ALU.add))
                link(dve.tensor_tensor(size[:, 1:2], ps[0:E_N, 0:1], size[:, 2:3], ALU.add))
                dve.scalar_tensor_tensor(rank[:, :], rank[:, :], size[:, 0:1], hot_e[:, :], ALU.add, ALU.mult) \
                   .then_inc(s_val, 1)
                dve.tensor_scalar(ends[:, :], block_i[:, :], size[:, 1:2], None, ALU.is_ge).then_inc(s_ends, 1)
                dve.wait_ge(s_slot, 1)
                dve.tensor_copy(slot[:, :], ps[:, 2:2 + T]).then_inc(s_row, 1)
                dve.wait_ge(s_ex, 1)
                dve.tensor_scalar(expert_of[:, :], pe_of[0:1, 0:BLOCKS], float(E_N - 1), None, ALU.min) \
                   .then_inc(s_done, 1)
                dve.wait_ge(s_done, 1)


def block_phase(nc, y, x, slots, expert_of, w1, w2, ident, dst):
    with Phase(nc, "block") as ph:
        now = ph.sb("now", [P, 2, 2], F32)
        rows = ph.sb("rows", [P, 2, D], F32)
        keep = ph.sb("keep", [P, 2, D], F32)
        out = ph.sb("out", [P, 2, D], F32)
        t_ = [ph.sb(f"t_{s}", [P, 2, KD, P], F32R) for s in ("hi", "lo")]
        act_f = ph.sb("act_f", [P, 2, H1], F32)
        hid = [ph.sb(f"hid_{s}", [P, 2, KH1, P], F32R) for s in ("hi", "lo")]
        raw = ph.sb("raw", [P, 2, 2, KD * H1], F32)
        a = [ph.sb(f"w1_{s}", [P, 2, KD, H1], F32R) for s in ("hi", "lo")]
        b = [ph.sb(f"w2_{s}", [P, 2, KH1, D], F32R) for s in ("hi", "lo")]
        px = ph.ps("px", [P, 2, BANK])
        phid = ph.ps("phid", [P, BANK])
        pht = ph.ps("pht", [P, KH1, P])
        po = [ph.ps(f"po{i}", [P, 2, BANK]) for i in range(2)]
        s_now, s_rows, s_keep, s_raw = ph.sems("now", 2), ph.sems("rows", 2), ph.sems("keep", 2), ph.sems("raw", 2)
        s_zero, s_whi, s_wlo = ph.sem("zero"), ph.sem("whi"), ph.sem("wlo")
        s_tr, s_thi, s_tlo = ph.sem("tr"), ph.sem("thi"), ph.sem("tlo")
        s_h, s_gelu, s_ht, s_hhi, s_hlo = ph.sem("h"), ph.sem("gelu"), ph.sem("ht"), ph.sem("hhi"), ph.sem("hlo")
        s_o, s_out, s_st = ph.sem("o"), ph.sem("out"), ph.sems("st", 2)
        with nc.Block() as block:
            @block.sync
            def _(sp):
                for n in range(BLOCKS):
                    h = n % 2
                    if n >= 2:
                        sp.wait_ge(s_st[h], 16 * (n // 2))
                    sp.dma_start(now[:, h, :], slots[n * P:(n + 1) * P, :]).then_inc(s_now[h], 16)
                    if n >= 2:
                        sp.wait_ge(s_wlo, n - 1)
                    e = sp.value_load(expert_of[0:1, n:n + 1], min_val=0, max_val=E_N - 1)
                    sp.dma_start(raw[:, h, 0, :].rearrange("p (k h) -> p k h", h=H1),
                                 w1[bass.ds(e, 1)].rearrange("e (k p) h -> p (e k) h", p=P)).then_inc(s_raw[h], 16)
                    sp.dma_start(raw[:, h, 1, :].rearrange("p (k d) -> p k d", d=D),
                                 w2[bass.ds(e, 1)].rearrange("e (k p) d -> p (e k) d", p=P)).then_inc(s_raw[h], 16)

            @block.gpsimd
            def _(pool):
                def offset(h):
                    return bass.IndirectOffsetOnAxis(ap=now[:, h, 0:1].bitcast(U32), axis=0)

                def gather(n):
                    h = n % 2
                    pool.wait_ge(s_now[h], 16 * (n // 2 + 1))
                    if n >= 2:
                        pool.wait_ge(s_tr, n - 1)
                        pool.wait_ge(s_out, n - 1)
                    for buf, src, sem in ((rows, y, s_rows[h]), (keep, x, s_keep[h])):
                        pool.indirect_dma_start(buf[:, h, :], None, src, offset(h), bounds_check=N - 1,
                                                oob_is_err=False).then_inc(sem, 16)

                for buf in (rows, keep):
                    pool.memset(buf[:, :, :], 0.0).then_inc(s_zero, 1)
                pool.wait_ge(s_zero, 2)
                gather(0)
                for n in range(BLOCKS):
                    if n + 1 < BLOCKS:
                        gather(n + 1)
                    pool.wait_ge(s_out, n + 1)
                    pool.indirect_dma_start(dst, offset(n % 2), out[:, n % 2, :], None, bounds_check=N - 1,
                                            oob_is_err=False).then_inc(s_st[n % 2], 16)
                pool.wait_ge(s_st[0], 16 * ((BLOCKS + 1) // 2))
                pool.wait_ge(s_st[1], 16 * (BLOCKS // 2))

            @block.scalar
            def _(act):
                def prepare(n):
                    h = n % 2
                    act.wait_ge(s_raw[h], 32 * (n // 2 + 1))
                    if n >= 2:
                        act.wait_ge(s_o, n - 1)
                    act.activation(a[0][:, h, :, :].rearrange("p k c -> p (k c)"), raw[:, h, 0, :], ACT.Copy)
                    act.activation(b[0][:, h, :, :].rearrange("p k c -> p (k c)"), raw[:, h, 1, :], ACT.Copy) \
                       .then_inc(s_whi, 1)
                    act.wait_ge(s_tr, n + 1)
                    for c in range(2):
                        ins = act.activation(t_[0][:, h, 4 * c:4 * c + 4, :].rearrange("p k r -> p (k r)"),
                                             px[:, c, :], ACT.Copy)
                    ins.then_inc(s_thi, 1)

                prepare(0)
                for n in range(BLOCKS):
                    h = n % 2
                    if n + 1 < BLOCKS:
                        prepare(n + 1)
                    act.wait_ge(s_h, n + 1)
                    act.activation(act_f[:, h, :], phid[:, 0:H1], ACT.Gelu).then_inc(s_gelu, 1)
                    act.wait_ge(s_ht, n + 1)
                    act.activation(hid[0][:, h, :, :], pht[:, :, :], ACT.Copy).then_inc(s_hhi, 1)

            @block.vector
            def _(dve):
                def prepare(n):
                    h = n % 2
                    dve.wait_ge(s_whi, n + 1)
                    dve.tensor_tensor(a[1][:, h, :, :].rearrange("p k c -> p (k c)"), raw[:, h, 0, :],
                                      a[0][:, h, :, :].rearrange("p k c -> p (k c)").bitcast(F32), ALU.subtract)
                    dve.tensor_tensor(b[1][:, h, :, :].rearrange("p k c -> p (k c)"), raw[:, h, 1, :],
                                      b[0][:, h, :, :].rearrange("p k c -> p (k c)").bitcast(F32), ALU.subtract) \
                       .then_inc(s_wlo, 1)
                    dve.wait_ge(s_thi, n + 1)
                    for c in range(2):
                        part = [t_[s][:, h, 4 * c:4 * c + 4, :].rearrange("p k r -> p (k r)") for s in range(2)]
                        ins = dve.tensor_tensor(part[1], px[:, c, :], part[0].bitcast(F32), ALU.subtract)
                    ins.then_inc(s_tlo, 1)

                prepare(0)
                for n in range(BLOCKS):
                    h = n % 2
                    if n + 1 < BLOCKS:
                        prepare(n + 1)
                    dve.wait_ge(s_hhi, n + 1)
                    dve.tensor_tensor(hid[1][:, h, :, :], pht[:, :, :], hid[0][:, h, :, :].bitcast(F32), ALU.subtract) \
                       .then_inc(s_hlo, 1)
                    dve.wait_ge(s_o, n + 1)
                    dve.wait_ge(s_keep[h], 16 * (n // 2 + 1))
                    if n >= 2:
                        dve.wait_ge(s_st[h], 16 * (n // 2))
                    for c in range(2):
                        cols = slice(c * BANK, (c + 1) * BANK)
                        ins = dve.scalar_tensor_tensor(out[:, h, cols], po[h][:, c, :], now[:, h, 1:2],
                                                       keep[:, h, cols], ALU.mult, ALU.add)
                    ins.then_inc(s_out, 1)

            @block.tensor
            def _(pe):
                def flip(n):
                    h = n % 2
                    pe.wait_ge(s_rows[h], 16 * (n // 2 + 1))
                    if n:
                        pe.wait_ge(s_tlo, n)
                    for k in range(KD):
                        ins = pe.transpose(px[:, k // 4, (k % 4) * P:(k % 4 + 1) * P], rows[:, h, k * P:(k + 1) * P],
                                           ident[:, :])
                    ins.then_inc(s_tr, 1)

                flip(0)
                for n in range(BLOCKS):
                    h = n % 2
                    pe.wait_ge(s_tlo, n + 1)
                    pe.wait_ge(s_wlo, n + 1)
                    if n:
                        pe.wait_ge(s_gelu, n)
                    for k in range(KD):
                        ins = mm3(pe, phid[:, 0:H1], [v[:, h, k, :] for v in t_], [w[:, h, k, :] for w in a],
                                  k == 0, k == KD - 1)
                    ins.then_inc(s_h, 1)
                    if n + 1 < BLOCKS:
                        flip(n + 1)
                    pe.wait_ge(s_gelu, n + 1)
                    if n:
                        pe.wait_ge(s_hlo, n)
                    for k in range(KH1):
                        ins = pe.transpose(pht[:, k, :], act_f[:, h, k * P:(k + 1) * P], ident[:, :])
                    ins.then_inc(s_ht, 1)
                    pe.wait_ge(s_hlo, n + 1)
                    if n >= 2:
                        pe.wait_ge(s_out, n - 1)
                    for c in range(2):
                        for k in range(KH1):
                            ins = mm3(pe, po[h][:, c, :], [v[:, h, k, :] for v in hid],
                                      [w[:, h, k, c * BANK:(c + 1) * BANK] for w in b], k == 0, k == KH1 - 1)
                    ins.then_inc(s_o, 1)


def gps_kernel(nc, x, src, dst, rms_w, w_down, wl, wr, att, w_up, wq, bq, wk, bk, wv, bv, wo, bo,
               gate0_w, w1_0, w2_0, w_self0, w_neigh0, b0, w_self1, w_neigh1, b1, w_qkv, w_o,
               gate1_w, w1_1, w2_1, out):
    def dram(name, shape):
        return nc.dram_tensor(name, shape, F32, kind="Internal").ap()

    scores, at = dram("scores", (N * N, HEADS)), dram("at", (T, R, N))
    wt = dram("wt", (4, D, D))
    xl, xr = dram("xl", (N, HID)), dram("xr", (N, HID))
    mixt = [dram(f"mixt{i}", (D, N)) for i in range(2)]
    xs = [dram(f"x{i}", (N, D)) for i in range(2)]
    y = [dram(f"y{i}", (N, D)) for i in range(2)]
    hidden, resid = dram("hidden", (N, D)), dram("resid", (N, D))
    slots = dram("slots", (BLOCKS * P, 2))

    with Phase(nc, "all") as keep:
        ident = keep.sb("ident", [P, P], F32)
        deg_inv = keep.sb("deg_inv", [R, T], F32)
        expert_of = keep.sb("expert_of", [1, BLOCKS], I32)

        def activations(ph):
            return [ph.sb(f"act_{s}", [P, KD, N], F32R) for s in ("hi", "lo")]

        with Phase(nc, "ffn0") as ffn0:
            chosen = ffn0.sb("chosen", [CAPR, LIST, E_N], I32)
            share = ffn0.sb("share", [CAPR, LIST, E_N], F32)
            with Phase(nc, "layer0") as layer:
                act = activations(layer)
                with Phase(nc, "front") as front:
                    hole = front.sb("hole", [R, N], F32)
                    rms = front.sb("rms", [R, T], F32)
                    filled = constants_phase(nc, ident, hole, scores)
                    norm_phase(nc, "norm0", x, *act, ident, rms=rms)
                    weights_phase(nc, [wq, wk, wv, wo], wt, ident)
                    gat_project_phase(nc, *act, rms, rms_w, w_down, wl, wr, xl, xr)
                    edge_phase(nc, src, dst, att, xl, xr, scores, filled)
                mix_phase(nc, "mix0", *act, wt[0], wt[1], wt[2], [bq, bk, bv], 1e-6, mixt[0])
                with Phase(nc, "gnn0") as gnn:
                    gat = [gnn.sb(f"gat_{s}", [P, KH, N], F32R) for s in ("hi", "lo")]
                    count_phase(nc, src, dst, ident, at, deg_inv)
                    gat_phase(nc, scores, at, xl, ident, gat)
                    output_phase(nc, "out0", *act, mixt[0], wt[3], bo, (*gat, w_up), x, xs[0])
                norm_phase(nc, "norm1", xs[0], *act, ident, dst=y[0])
                choose_phase(nc, *act, gate0_w, ident, chosen, share)
            expert_phase(nc, y[0], chosen, share, w1_0, w2_0, ident, xs[0])

        with Phase(nc, "layer1") as layer:
            act = activations(layer)
            norm_phase(nc, "norm2", xs[0], *act, ident)
            mix_phase(nc, "mix1", *act, w_qkv[:, 0:D], w_qkv[:, D:2 * D], w_qkv[:, 2 * D:3 * D], None, 0.0, mixt[1])
            sage_phase(nc, "sage0", *act, at, deg_inv, w_self0, w_neigh0, b0, None, hidden)
            norm_phase(nc, "flip", hidden, *act, ident, normalize=False)
            sage_phase(nc, "sage1", *act, at, deg_inv, w_self1, w_neigh1, b1, xs[0], resid)
            output_phase(nc, "out1", *act, mixt[1], w_o, None, None, resid, xs[1])
            norm_phase(nc, "norm3", xs[1], *act, ident, dst=y[1])
            assign_phase(nc, *act, gate1_w, ident, slots, expert_of)
        block_phase(nc, y[1], xs[1], slots, expert_of, w1_1, w2_1, ident, out)


_INS = ['x', 'src', 'dst', 'L0_gnn_rms_w', 'L0_gnn_W_down', 'L0_gnn_Wl', 'L0_gnn_Wr', 'L0_gnn_att', 'L0_gnn_W_up',
        'L0_mix_Wq', 'L0_mix_bq', 'L0_mix_Wk', 'L0_mix_bk', 'L0_mix_Wv', 'L0_mix_bv', 'L0_mix_Wo', 'L0_mix_bo',
        'L0_ffn_gate_w', 'L0_ffn_w1', 'L0_ffn_w2', 'L1_gnn_W_self0', 'L1_gnn_W_neigh0', 'L1_gnn_b0',
        'L1_gnn_W_self1', 'L1_gnn_W_neigh1', 'L1_gnn_b1', 'L1_mix_w_qkv', 'L1_mix_w_o',
        'L1_ffn_Wg', 'L1_ffn_W1', 'L1_ffn_W2']
_OUTS = [((N, D), 'float32')]


def kernel(**inputs):
    import numpy as _np
    import concourse.bacc as _bacc
    from concourse import mybir as _mybir
    from concourse.bass_utils import run_bass_kernel_spmd as _run

    nc = _bacc.Bacc("TRN2", target_bir_lowering=False, num_devices=1)
    arrays, args = {}, []
    for name in _INS:
        a = _np.ascontiguousarray(inputs[name])
        arrays[f"in_{name}_dram"] = a
        args.append(nc.dram_tensor(f"in_{name}_dram", a.shape, _mybir.dt.from_np(a.dtype), kind="ExternalInput").ap())
    for i, (shape, dtype) in enumerate(_OUTS):
        dt = _mybir.dt.from_np(_np.dtype(dtype))
        args.append(nc.dram_tensor(f"out_{i}_dram", shape, dt, kind="ExternalOutput").ap())
    gps_kernel(nc, *args)
    r = _run(nc, [arrays], core_ids=[0])
    got = tuple(r.results[0][f"out_{i}_dram"] for i in range(len(_OUTS)))
    return got[0]
```

```python
import math
import concourse.bass as bass
from concourse import mybir
from contextlib import ExitStack

F32 = mybir.dt.float32
F32R = mybir.dt.float32r
BF16 = mybir.dt.bfloat16
F16 = mybir.dt.float16
I32 = mybir.dt.int32
U32 = mybir.dt.uint32
ALU = mybir.AluOpType
ACT = mybir.ActivationFunctionType
AX = mybir.AxisListType

N = 1250
D = 1024
P = 128
R = 125
T = N // R
KD = D // P
CHUNKS = [(0, 418), (418, 416), (834, 416)]
SLAB = 256
NSLAB = D // SLAB
BANK = 512
NEG = -1.0e30


class Link:

    def __init__(self, eng, sem, base=0):
        self.eng, self.sem, self.base, self.count = eng, sem, base, 0

    def __call__(self, ins):
        self.count += 1
        ins.then_inc(self.sem, 1)
        self.eng.wait_ge(self.sem, self.base + self.count)


class Phase:

    def __init__(self, nc, name):
        self.nc, self.name, self.ctx, self.held = nc, name, ExitStack(), []

    def __enter__(self):
        return self

    def __exit__(self, *exc):
        if self.held:
            self.nc.clear_and_free_semaphores(self.held)
            self.nc.all_engine_barrier()
        return self.ctx.__exit__(*exc)

    def sb(self, name, shape, dt):
        return self.ctx.enter_context(self.nc.sbuf_tensor(f"{self.name}_{name}", shape, dt))

    def ps(self, name, shape, dt=F32):
        return self.ctx.enter_context(self.nc.psum_tensor(f"{self.name}_{name}", shape, dt))

    def sem(self, name):
        self.held.append(self.nc.alloc_semaphore(f"{self.name}_{name}"))
        return self.held[-1]

    def sems(self, name, n):
        return [self.sem(f"{name}{i}") for i in range(n)]


def constants_phase(nc, ident, hole, scores):
    with Phase(nc, "const") as ph:
        s_zero, s_id, s_hole = ph.sem("zero"), ph.sem("id"), ph.sem("hole")
        s_fill = nc.alloc_semaphore("scores_filled")
        rows = scores.rearrange("(t p s) h -> t p (s h)", p=R, s=N)
        with nc.Block() as block:
            @block.gpsimd
            def _(pool):
                pool.memset(ident[:, :], 0.0).then_inc(s_zero, 1)
                pool.memset(hole[:, :], NEG).then_inc(s_hole, 1)
                pool.wait_ge(s_zero, 1)
                pool.affine_select(out=ident[:, :], in_=ident[:, :], compare_op=ALU.not_equal, fill=1.0,
                                   base=0, pattern=[[-1, P]], channel_multiplier=1).then_inc(s_id, 1)

            @block.sync
            def _(sp):
                sp.wait_ge(s_hole, 1)
                for t in range(T):
                    for h in range(4):
                        sp.dma_start(rows[t][:, h * N:(h + 1) * N], hole[:, :]).then_inc(s_fill, 16)
        return s_fill, 16 * 4 * T


def norm_phase(nc, name, src, act_hi, act_lo, ident, dst=None, rms=None, normalize=True):
    with Phase(nc, name) as ph:
        x = ph.sb("x", [R, 2, D], F32)
        y = ph.sb("y", [R, 2, D], F32)
        stats = ph.sb("stats", [R, 2, 2, 6], F32)
        mv = ph.sb("mv", [R, 2, 2], F32)
        dev = ph.sb("dev", [R, 2, 2], F32)
        rstd = ph.sb("rstd", [R, 2, 1], F32)
        square = ph.sb("square", [R, D], F32)
        sumsq = ph.sb("sumsq", [R, T], F32)
        pt = [ph.ps(f"pt{h}", [P, 2, BANK]) for h in range(2)]
        s_x = ph.sems("x_in", 2)
        s_var, s_dev, s_y = ph.sem("var"), ph.sem("dev"), ph.sem("y")
        s_tr, s_hi, s_lo = ph.sem("tr"), ph.sem("hi"), ph.sem("lo")
        s_out = ph.sems("out", 2)
        s_link, s_sq, s_rms, s_rdev = ph.sem("link"), ph.sem("sq"), ph.sem("rms"), ph.sem("rdev")
        rows = src.rearrange("(t p) c -> t p c", p=R)
        out_rows = dst.rearrange("(t p) c -> t p c", p=R) if dst is not None else None
        feed = y if normalize else x

        with nc.Block() as block:
            @block.sync
            def _(sp):
                def load(t):
                    if t >= 2:
                        sp.wait_ge(s_y if normalize else s_tr, t - 1 if normalize else t)
                    sp.dma_start(x[:, t % 2, :], rows[t]).then_inc(s_x[t % 2], 16)

                if dst is not None:
                    for h in range(2):
                        sp.sem_inc(s_out[h], 16)
                load(0)
                for t in range(T):
                    if t + 1 < T:
                        load(t + 1)
                    if dst is not None:
                        sp.wait_ge(s_y, t + 1)
                        sp.dma_start(out_rows[t], y[:, t % 2, :]).then_inc(s_out[t % 2], 16)
                if dst is not None:
                    for h in range(2):
                        sp.wait_ge(s_out[h], 16 * (T // 2) + 16)

            @block.vector
            def _(dve):
                dve.sem_inc(s_lo, 1)
                with dve.Fori(0, T // 2) as i:
                    link = Link(dve, s_link, 2 * 6 * i)
                    if normalize:
                        for h in range(2):
                            dve.wait_ge(s_x[h], 16 * i + 16)
                            for half in range(2):
                                ins = dve.bn_stats(stats[:, h, half, :], x[:, h, half * BANK:(half + 1) * BANK])
                            link(ins)
                            dve.memset(dev[:, h, 0:1], 0.0)
                            link(dve.bn_aggr(mv[:, h, :], stats[:, h, :, :].rearrange("p a b -> p (a b)")))
                            dve.tensor_scalar(dev[:, h, 0:1], mv[:, h, 1:2], 1e-5, None, ALU.add).then_inc(s_var, 1)
                            dve.wait_ge(s_dev, 2 * i + h + 1)
                            link(dve.reciprocal(rstd[:, h, :], dev[:, h, 1:2]))
                            link(dve.tensor_scalar(dev[:, h, 1:2], rstd[:, h, :], rstd[:, h, :], dev[:, h, 0:1],
                                                   ALU.mult, ALU.mult))
                            link(dve.tensor_scalar(dev[:, h, 1:2], dev[:, h, 1:2], -0.5, 1.5, ALU.mult, ALU.add))
                            link(dve.tensor_tensor(rstd[:, h, :], rstd[:, h, :], dev[:, h, 1:2], ALU.mult))
                            dve.wait_ge(s_tr, 2 * i + 1)
                            if dst is not None:
                                dve.wait_ge(s_out[h], 16 * i + 16)
                            if rms is not None:
                                dve.wait_ge(s_sq, 2 * i + 1)
                            dve.tensor_scalar(y[:, h, :], x[:, h, :], mv[:, h, 0:1], rstd[:, h, :],
                                              ALU.subtract, ALU.mult).then_inc(s_y, 1)
                    for h in range(2):
                        dve.wait_ge(s_hi, 2 * i + h + 1)
                        for b in range(2):
                            cols = slice(4 * b, 4 * b + 4)
                            at = bass.ds(2 * R * i + R * h, R)
                            ins = dve.tensor_tensor(
                                act_lo[:, cols, at], pt[h][:, b, 0:4 * R].rearrange("p (k r) -> p k r", k=4),
                                act_hi[:, cols, at].bitcast(F32), ALU.subtract)
                        ins.then_inc(s_lo, 1)
                if rms is not None:
                    dve.wait_ge(s_sq, T + 1)
                    dve.tensor_scalar(rms[:, :], sumsq[:, :], 1.0 / D, 1e-6, ALU.mult, ALU.add).then_inc(s_rms, 1)
                    dve.wait_ge(s_rdev, 1)
                    dve.reciprocal(rms[:, :], sumsq[:, :]).then_inc(s_rms, 1)
                    dve.wait_ge(s_rms, 2)

            @block.scalar
            def _(act):
                act.sem_inc(s_sq, 1)
                with act.Fori(0, T // 2) as i:
                    if normalize:
                        for h in range(2):
                            act.wait_ge(s_var, 2 * i + h + 1)
                            act.activation(dev[:, h, 1:2], dev[:, h, 0:1], ACT.Sqrt).then_inc(s_dev, 1)
                    for h in range(2):
                        if rms is not None:
                            act.wait_ge(s_y, 2 * i + h + 1)
                            act.wait_ge(s_sq, 2 * i + h + 1)
                            act.activation(square[:, :], y[:, h, :], ACT.Square,
                                           accum_out=sumsq[:, bass.ds(2 * i + h, 1)]).then_inc(s_sq, 1)
                        act.wait_ge(s_tr, 2 * i + h + 2)
                        for b in range(2):
                            ins = act.activation(act_hi[:, 4 * b:4 * b + 4, bass.ds(2 * R * i + R * h, R)],
                                                 pt[h][:, b, 0:4 * R].rearrange("p (k r) -> p k r", k=4), ACT.Copy)
                        ins.then_inc(s_hi, 1)
                if rms is not None:
                    act.wait_ge(s_rms, 1)
                    act.activation(sumsq[:, :], rms[:, :], ACT.Sqrt).then_inc(s_rdev, 1)

            @block.tensor
            def _(pe):
                pe.sem_inc(s_tr, 1)
                with pe.Fori(0, T // 2) as i:
                    for h in range(2):
                        if normalize:
                            pe.wait_ge(s_y, 2 * i + h + 1)
                        else:
                            pe.wait_ge(s_x[h], 16 * i + 16)
                        pe.wait_ge(s_lo, 2 * i + 1)
                        for k in range(KD):
                            ins = pe.transpose(pt[h][:, k // 4, (k % 4) * R:(k % 4 + 1) * R],
                                               feed[:, h, k * P:(k + 1) * P], ident[0:R, 0:R])
                        ins.then_inc(s_tr, 1)
HID = 256
HEADS = 4
HD = HID // HEADS
EDGES = 21250
ET = EDGES // R
EB = 2
BATCHES = ET // EB
RING = 4
AHEAD = 3
MIX_BATCHES = 2 * RING * (D // (2 * HD))
PAIRS = ET // 2
KH = HID // P
XW = HD + 2


def mm3(pe, out, lhs, rhs, first, last):
    pe.matmul(out, lhs[0], rhs[0], start=first, stop=False)
    pe.matmul(out, lhs[0], rhs[1], start=False, stop=False)
    return pe.matmul(out, lhs[1], rhs[0], start=False, stop=last)


def gat_project_phase(nc, act_hi, act_lo, rms, rms_w, w_down, wl, wr, att, xl, xr, loops):
    with Phase(nc, "proj") as ph:
        wd = ph.sb("wd", [P, KD, HID], F32)
        wd_hi, wd_lo = (ph.sb(f"wd_{s}", [P, KD, HID], F32R) for s in ("hi", "lo"))
        gain = ph.sb("gain", [P, KD], F32)
        wlr = ph.sb("wlr", [P, KH, 2 * HID], F32)
        wlr_hi, wlr_lo = (ph.sb(f"wlr_{s}", [P, KH, 2 * HID], F32R) for s in ("hi", "lo"))
        d_hi, d_lo = (ph.sb(f"down_{s}", [P, KH, N], F32R) for s in ("hi", "lo"))
        out = ph.sb("out", [R, 2, 2 * HID], F32)
        attb = ph.sb("attb", [R, HID], F32)
        self_ = ph.sb("self", [R, HID], F32)
        s_att, s_link = ph.sem("att"), ph.sem("link")
        bank = [ph.ps(f"bank{b}", [P, BANK]) for b in range(4)]
        s_w, s_wlr, s_gain = ph.sem("w"), ph.sem("wlr"), ph.sem("scaled")
        s_whi, s_wlo = ph.sem("whi"), ph.sem("wlo")
        s_mm, s_hi, s_lo = ph.sem("mm"), ph.sem("hi"), ph.sem("lo")
        s_xm, s_xo, s_st = ph.sem("xm"), ph.sem("xo"), ph.sems("st", 2)
        units = [(m, c) for m in range(KH) for c in range(len(CHUNKS))]
        with nc.Block() as block:
            @block.sync
            def _(sp):
                sp.dma_start(wd[:, :, :], w_down.rearrange("(k p) n -> p k n", p=P)).then_inc(s_w, 16)
                sp.dma_start(gain[:, :], rms_w.rearrange("(k p) -> p k", p=P),
                             allow_slow_non_contiguous=True).then_inc(s_w, 16)
                for j, w in enumerate((wl, wr)):
                    sp.dma_start(wlr[:, :, j * HID:(j + 1) * HID], w.rearrange("(k p) n -> p k n", p=P)) \
                        .then_inc(s_wlr, 16)
                sp.dma_start(attb[:, :], att.rearrange("(o h) d -> o (h d)", o=1).to_broadcast([R, HID])) \
                    .then_inc(s_att, 16)
                for t in range(T):
                    sp.wait_ge(s_xo, t + 1)
                    for j, x in enumerate((xl, xr)):
                        sp.dma_start(x[t * R:(t + 1) * R, :], out[:, t % 2, j * HID:(j + 1) * HID]) \
                            .then_inc(s_st[t % 2], 16)
                for h in range(2):
                    sp.wait_ge(s_st[h], 32 * T // 2)

            @block.vector
            def _(dve):
                dve.wait_ge(s_w, 32)
                for k in range(KD):
                    dve.tensor_scalar(wd[:, k, :], wd[:, k, :], gain[:, k:k + 1], None, ALU.mult).then_inc(s_gain, 1)
                dve.wait_ge(s_whi, 1)
                dve.tensor_tensor(wd_lo[:, :, :], wd[:, :, :], wd_hi[:, :, :].bitcast(F32), ALU.subtract) \
                   .then_inc(s_wlo, 1)
                dve.wait_ge(s_whi, 2)
                dve.tensor_tensor(wlr_lo[:, :, :], wlr[:, :, :], wlr_hi[:, :, :].bitcast(F32), ALU.subtract) \
                   .then_inc(s_wlo, 1)
                for u, (m, c) in enumerate(units):
                    o, n = CHUNKS[c]
                    dve.wait_ge(s_hi, u + 1)
                    dve.tensor_tensor(d_lo[:, m, o:o + n], bank[u % 4][:, 0:n], d_hi[:, m, o:o + n].bitcast(F32),
                                      ALU.subtract).then_inc(s_lo, 1)
                link = Link(dve, s_link)
                dve.wait_ge(s_att, 16)
                for t in range(T):
                    dve.wait_ge(s_xm, t + 1)
                    if t >= 2:
                        dve.wait_ge(s_st[t % 2], 32 * (t // 2))
                    dve.tensor_scalar(out[:, t % 2, :], bank[t % 4][0:R, :], rms[:, t:t + 1], None, ALU.mult) \
                       .then_inc(s_xo, 1)
                    dve.wait_ge(s_xo, t + 1)
                    link(dve.tensor_tensor(self_[:, :], out[:, t % 2, 0:HID], out[:, t % 2, HID:], ALU.add))
                    link(dve.scalar_tensor_tensor(self_[:, :], self_[:, :], 0.2, self_[:, :], ALU.mult, ALU.max))
                    link(dve.tensor_tensor(self_[:, :], self_[:, :], attb[:, :], ALU.mult))
                    link(dve.tensor_reduce(loops[:, t, :], self_[:, :].rearrange("p (a d) -> p a d", a=HEADS), AX.X, ALU.add))

            @block.scalar
            def _(act):
                act.wait_ge(s_gain, KD)
                act.activation(wd_hi[:, :, :], wd[:, :, :], ACT.Copy).then_inc(s_whi, 1)
                act.wait_ge(s_wlr, 32)
                act.activation(wlr_hi[:, :, :], wlr[:, :, :], ACT.Copy).then_inc(s_whi, 1)
                for u, (m, c) in enumerate(units):
                    o, n = CHUNKS[c]
                    act.wait_ge(s_mm, u + 1)
                    act.activation(d_hi[:, m, o:o + n], bank[u % 4][:, 0:n], ACT.Copy).then_inc(s_hi, 1)

            @block.tensor
            def _(pe):
                pe.wait_ge(s_wlo, 1)
                for u, (m, c) in enumerate(units):
                    o, n = CHUNKS[c]
                    if u >= 4:
                        pe.wait_ge(s_lo, u - 3)
                    for k in range(KD):
                        w = slice(m * P, (m + 1) * P)
                        ins = mm3(pe, bank[u % 4][:, 0:n], (wd_hi[:, k, w], wd_lo[:, k, w]),
                                  (act_hi[:, k, o:o + n], act_lo[:, k, o:o + n]), k == 0, k == KD - 1)
                    ins.then_inc(s_mm, 1)
                pe.wait_ge(s_wlo, 2)
                pe.wait_ge(s_lo, len(units))
                for t in range(T):
                    if t >= 4:
                        pe.wait_ge(s_xo, t - 3)
                    n = slice(t * R, (t + 1) * R)
                    for k in range(KH):
                        ins = mm3(pe, bank[t % 4][0:R, :], (d_hi[:, k, n], d_lo[:, k, n]),
                                  (wlr_hi[:, k, :], wlr_lo[:, k, :]), k == 0, k == KH - 1)
                    ins.then_inc(s_xm, 1)


class Edges:

    def __init__(self, ph, src, dst, att, xl, xr, scores, loops, filled):
        self.src, self.dst, self.att, self.xl, self.xr = src, dst, att, xl, xr
        self.scores, self.loops, self.filled = scores, loops, filled
        self.idx = ph.sb("idx", [R, 3, ET], I32)
        self.idf = ph.sb("idf", [R, 2, ET], F32)
        self.now = ph.sb("now", [R, 2 * RING, 3, EB], I32)
        self.gl = ph.sb("gl", [R, RING, EB, HID], F32)
        self.gr = ph.sb("gr", [R, RING, EB, HID], F32)
        self.attb = ph.sb("attb", [R, HID], F32)
        self.e = ph.sb("e", [R, RING, EB, HEADS], F32)
        self.s_idx, self.s_att = ph.sem("idx"), ph.sem("att")
        self.s_now, self.s_e, self.s_sc = ph.sem("now"), ph.sem("e"), ph.sem("sc")
        self.s_g, self.s_link, self.s_turn = ph.sems("g", RING), ph.sem("link"), ph.sem("turn")

    def stored(self, b, j=0):
        return 16 * (T + 1) + 16 * (EB * b + j)

    def sync(self, sp):
        for j, a in enumerate((self.src, self.dst)):
            sp.dma_start(self.idx[:, j, :], a.rearrange("(p k) -> p k", p=R)).then_inc(self.s_idx, 16)
        sp.dma_start(self.attb[:, :], self.att.rearrange("(o h) d -> o (h d)", o=1).to_broadcast([R, HID])) \
          .then_inc(self.s_att, 16)

    def columns(self, dve, b, slot):
        dve.tensor_copy(self.now[:, slot, :, :], self.idx[:, :, bass.ds(b * EB, EB)]).then_inc(self.s_now, 1)

    def vector(self, dve):
        idx, idf = self.idx, self.idf
        link = Link(dve, self.s_link)
        dve.wait_ge(self.s_idx, 32)
        dve.tensor_copy(idf[:, 0, :], idx[:, 0, :])
        link(dve.tensor_copy(idf[:, 1, :], idx[:, 1, :]))
        link(dve.scalar_tensor_tensor(idf[:, 1, :], idf[:, 1, :], float(N), idf[:, 0, :], ALU.mult, ALU.add))
        link(dve.tensor_copy(idx[:, 2, :], idf[:, 1, :]))
        for b in range(AHEAD):
            self.columns(dve, b, b)
        dve.wait_ge(self.s_att, 16)

    def turns(self, dve, g):
        return EdgeTurns(self, dve, g)

    def gather(self, pool, b, slot, wide_slot, j):
        for buf, x, row in ((self.gl, self.xl, 0), (self.gr, self.xr, 1)):
            pool.indirect_dma_start(buf[:, slot, j, :], None, x, bass.IndirectOffsetOnAxis(
                ap=self.now[:, wide_slot, row, j:j + 1].bitcast(U32), axis=0)).then_inc(self.s_g[slot], 16)

    def gpsimd(self, pool, first, end):
        def batch(b, u, last=False):
            if not last:
                pool.wait_ge(self.s_now, b + 3)
            pool.wait_ge(self.s_e, b + 1)
            for j in range(EB):
                pool.wait_ge(self.s_sc, self.stored(b, j))
                pool.sem_inc(self.s_turn, 1)
                pool.indirect_dma_start(self.scores, bass.IndirectOffsetOnAxis(
                    ap=self.now[:, u % (2 * RING), 2, j:j + 1].bitcast(U32), axis=0),
                    self.e[:, u % RING, j, :], None).then_inc(self.s_sc, 16)
                if not last:
                    self.gather(pool, b + 2, (u + 2) % RING, (u + 2) % (2 * RING), j)

        if first == 0:
            pool.sem_inc(self.s_turn, EB * RING)
            for b in range(2):
                pool.wait_ge(self.s_now, b + 1)
                for j in range(EB):
                    self.gather(pool, b, b, b, j)
            pool.wait_ge(*self.filled)
            flat = self.scores.rearrange("s h -> (s h)")
            diag = flat[0:(N * N - 1) * HEADS].rearrange("(i x) -> i x", x=(N + 1) * HEADS)
            for t in range(T):
                n = min(R, N - 1 - t * R)
                pool.dma_start(diag[t * R:t * R + n, 0:HEADS], self.loops[0:n, t, :]).then_inc(self.s_sc, 16)
            pool.dma_start(self.scores[N * N - 1:N * N, :], self.loops[R - 1:R, T - 1, :]).then_inc(self.s_sc, 16)
        whole = (min(end, BATCHES - 2) - first) // (2 * RING)
        with pool.Fori(0, whole) as i:
            for u in range(2 * RING):
                batch(2 * RING * i + first + u, u)
        for b in range(first + 2 * RING * whole, end):
            batch(b, b, last=b + 2 >= BATCHES)
        pool.wait_ge(self.s_sc, self.stored(end))


class EdgeTurns:
    def __init__(self, edges, dve, g):
        self.edges, self.dve, self.g = edges, dve, g
        self.u = 0 if g is not None else MIX_BATCHES

    def left(self):
        return self.u < BATCHES

    def step(self):
        e, dve, u = self.edges, self.dve, self.u
        b = u if self.g is None else self.g * (2 * RING) + u
        slot = u % RING
        link = Link(dve, e.s_link, 3 * b + 3)
        dve.wait_ge(e.s_turn, EB * RING + EB * (b - RING + 1) + 1)
        if self.g is not None or u + AHEAD < BATCHES:
            e.columns(dve, b + AHEAD, (u + AHEAD) % (2 * RING))
        gl, gr = e.gl[:, slot, :, :], e.gr[:, slot, :, :]
        turn = b // RING if self.g is None else self.g * 2 + u // RING
        dve.wait_ge(e.s_g[slot], 32 * EB * (turn + 1))
        link(dve.tensor_tensor(gl, gl, gr, ALU.add))
        link(dve.scalar_tensor_tensor(gl, gl, 0.2, gl, ALU.mult, ALU.max))
        link(dve.tensor_tensor(gl, gl, e.attb[:, :].unsqueeze(1).to_broadcast([R, EB, HID]), ALU.mult))
        dve.tensor_reduce(e.e[:, slot, :, :], gl.rearrange("p t (a d) -> p t a d", a=HEADS), AX.X, ALU.add) \
           .then_inc(e.s_e, 1)
        self.u += 1


def count_phase(nc, src, dst, ident, at, deg_inv):
    with Phase(nc, "count") as ph:
        rows_i = ph.sb("rows_i", [PAIRS, 2, 2 * R], I32)
        rows = ph.sb("rows", [PAIRS, 2, 2 * R], F32)
        ends = ph.sb("ends", [R, 2, 2, 2 * PAIRS], F32)
        local = ph.sb("local", [R, 2, 2 * PAIRS], F32)
        lim = ph.sb("lim", [PAIRS, 2], F32)
        lim_diag = ph.sb("lim_diag", [PAIRS, 2, PAIRS], F32)
        ones = ph.sb("ones", [PAIRS, T], F32)
        first = ph.sb("first", [T, 2], F32)
        tile_i = ph.sb("tile_i", [T, 1], I32)
        pair_i = ph.sb("pair_i", [T, PAIRS], I32)
        pair = ph.sb("pair", [T, PAIRS], F32)
        out_of = ph.sb("out_of", [T, 2, PAIRS], F32)
        before = ph.sb("before", [T, T], F32)
        span = ph.sb("span", [T, 4], F32)
        span_i = ph.sb("span_i", [T, 4], I32)
        node_i = ph.sb("node_i", [R, N], I32)
        node = ph.sb("node", [R, N], F16)
        hot_s = ph.sb("hot_s", [R, 2, N], BF16)
        hot_d = ph.sb("hot_d", [R, 2, R], BF16)
        nil = ph.sb("nil", [R, N], BF16)
        a_sb = ph.sb("a_sb", [R, N], F32)
        a_tr = ph.sb("a_tr", [R, T, R], F32)
        deg = ph.sb("deg", [R, T], F32)
        pa = ph.ps("pa", [R, 3, BANK])
        pt = ph.ps("pt", [R, 3, BANK])
        pm = ph.ps("pm", [P, 2, BANK])
        s_rows, s_f, s_tr, s_ends = ph.sem("rows"), ph.sem("f"), ph.sem("tr"), ph.sem("ends")
        s_iota, s_link, s_lim, s_pl = ph.sem("iota"), ph.sem("link"), ph.sem("lim"), ph.sem("pl")
        s_num, s_base, s_span = ph.sem("num"), ph.sem("base"), ph.sem("span")
        s_nil, s_const = ph.sem("nil"), ph.sem("const")
        s_hot, s_used, s_a, s_cp = ph.sem("hot"), ph.sem("used"), ph.sem("a"), ph.sem("cp")
        s_at, s_sb, s_st = ph.sem("at"), ph.sem("sb"), ph.sem("st")
        s_local = ph.sem("local")

        def spans(eng, t):
            return [eng.value_load(span_i[t:t + 1, c:c + 1], min_val=lo, max_val=hi)
                    for c, lo, hi in ((0, 0, PAIRS - 1), (2, 1, PAIRS), (3, 0, T * PAIRS))]

        with nc.Block() as block:
            @block.sync
            def _(sp):
                for j, a in enumerate((src, dst)):
                    sp.dma_start(rows_i[:, j, :], a.rearrange("(q e) -> q e", e=2 * R)).then_inc(s_rows, 16)
                for t in range(T):
                    sp.wait_ge(s_sb, t + 1)
                    sp.dma_start(at.rearrange("b p d -> p b d")[:, :, t * R:(t + 1) * R], a_tr[:, :, :]) \
                        .then_inc(s_st, 16)
                sp.wait_ge(s_st, 16 * T)

            @block.gpsimd
            def _(pool):
                pool.iota(tile_i[:, :], [[0, 1]], base=0, channel_multiplier=R).then_inc(s_iota, 1)
                pool.iota(pair_i[:, :], [[1, PAIRS]], base=0, channel_multiplier=0).then_inc(s_iota, 1)
                pool.iota(node_i[:, :], [[1, N]], base=0, channel_multiplier=0).then_inc(s_iota, 1)
                pool.memset(before[:, :], 1.0).then_inc(s_const, 1)
                pool.memset(ones[:, :], 1.0).then_inc(s_const, 1)
                pool.memset(nil[:, :], 0.0).then_inc(s_nil, 1)
                pool.wait_ge(s_const, 2)
                pool.affine_select(out=before[:, :], in_=before[:, :], compare_op=ALU.is_gt, fill=0.0,
                                   base=0, pattern=[[1, T]], channel_multiplier=-1).then_inc(s_const, 1)

            @block.vector
            def _(dve):
                link = Link(dve, s_link)
                dve.wait_ge(s_iota, 3)
                dve.tensor_copy(pair[:, :], pair_i[:, :])
                dve.tensor_copy(node[:, :], node_i[:, :])
                dve.tensor_copy(first[:, 0:1], tile_i[:, :])
                dve.tensor_scalar(first[:, 1:2], tile_i[:, :], float(R), None, ALU.add)
                dve.wait_ge(s_rows, 32)
                ins = dve.tensor_copy(rows[:, :, :], rows_i[:, :, :])
                ins.then_inc(s_f, 1)
                dve.wait_ge(s_f, 1)
                dve.tensor_reduce(lim[:, 0:1], rows[:, 1, :], AX.X, ALU.min)
                link(dve.tensor_reduce(lim[:, 1:2], rows[:, 1, :], AX.X, ALU.max))
                for j in range(2):
                    dve.tensor_scalar(lim_diag[:, j, :], ident[0:PAIRS, 0:PAIRS], lim[:, j:j + 1], None, ALU.mult) \
                       .then_inc(s_lim, 1)
                dve.wait_ge(s_tr, 4)
                dve.tensor_copy(ends[:, :, :, 0:PAIRS], pm[0:R, 0, 0:4 * PAIRS].rearrange("p (a j q) -> p a j q", a=2, j=2)) \
                   .then_inc(s_ends, 1)
                dve.wait_ge(s_pl, 1)
                low, high = pm[0:T, 1, 0:PAIRS], pm[0:T, 1, PAIRS:2 * PAIRS]
                big = float(2 * PAIRS)
                dve.tensor_scalar(out_of[:, 0, :], high, first[:, 0:1], big, ALU.is_lt, ALU.mult)
                link(dve.tensor_scalar(out_of[:, 1, :], low, first[:, 1:2], big, ALU.is_ge, ALU.mult))
                dve.tensor_tensor(out_of[:, 0, :], out_of[:, 0, :], pair[:, :], ALU.add)
                link(dve.tensor_tensor(out_of[:, 1, :], pair[:, :], out_of[:, 1, :], ALU.subtract))
                dve.tensor_reduce(span[:, 0:1], out_of[:, 0, :], AX.X, ALU.min)
                link(dve.tensor_reduce(span[:, 1:2], out_of[:, 1, :], AX.X, ALU.max))
                link(dve.tensor_scalar(span[:, 0:1], span[:, 0:1], float(PAIRS - 1), None, ALU.min))
                link(dve.tensor_tensor(span[:, 2:3], span[:, 1:2], span[:, 0:1], ALU.subtract))
                dve.tensor_scalar(span[:, 2:3], span[:, 2:3], 1.0, 1.0, ALU.add, ALU.max).then_inc(s_num, 1)
                dve.wait_ge(s_base, 1)
                link(dve.tensor_copy(span[:, 3:4], pm[0:T, 1, 2 * PAIRS:2 * PAIRS + 1]))
                dve.tensor_copy(span_i[:, :], span[:, :]).then_inc(s_span, 1)
                dve.wait_ge(s_span, 1)
                dve.wait_ge(s_ends, 1)
                for t in range(T):
                    lo, num, base = spans(dve, t)
                    if t:
                        dve.wait_ge(s_a, t)
                    dve.tensor_scalar(local[:, :, 0:PAIRS], ends[:, 1, :, 0:PAIRS], float(-R * t), None, ALU.add) \
                       .then_inc(s_local, 1)
                    dve.wait_ge(s_local, t + 1)
                    with dve.Fori(0, num) as i:
                        q = lo + i
                        for j in range(2):
                            dve.wait_ge(s_used, 2 * (base + i) + j + 1)
                            dve.tensor_scalar(hot_d[:, j, :], node[:, 0:R], local[:, j, bass.ds(q, 1)], None,
                                              ALU.is_equal)
                            dve.tensor_scalar(hot_s[:, j, :], node[:, :], ends[:, 0, j, bass.ds(q, 1)], None,
                                              ALU.is_equal).then_inc(s_hot, 1)
                    dve.wait_ge(s_cp, t + 1)
                    dve.tensor_reduce(deg[:, t:t + 1], a_sb[:, :], AX.X, ALU.add)
                    dve.wait_ge(s_at, t + 1)
                    if t:
                        dve.wait_ge(s_st, 16 * t)
                    for b in range(3):
                        n = min(4, T - 4 * b)
                        ins = dve.tensor_copy(a_tr[:, 4 * b:4 * b + n, :],
                                              pt[:, b, 0:n * R].rearrange("p (b r) -> p b r", r=R))
                    ins.then_inc(s_sb, 1)
                dve.wait_ge(s_sb, T)
                link(dve.tensor_scalar(deg[:, :], deg[:, :], 1.0, None, ALU.max))
                link(dve.reciprocal(deg_inv[:, :], deg[:, :]))

            @block.scalar
            def _(act):
                for t in range(T):
                    act.wait_ge(s_a, t + 1)
                    if t:
                        act.wait_ge(s_sb, t)
                    for c, (o, n) in enumerate(CHUNKS):
                        ins = act.activation(a_sb[:, o:o + n], pa[:, c, 0:n], ACT.Copy)
                    ins.then_inc(s_cp, 1)

            @block.tensor
            def _(pe):
                pe.wait_ge(s_f, 1)
                for a in range(2):
                    for j in range(2):
                        at_ = (2 * a + j) * PAIRS
                        pe.transpose(pm[0:R, 0, at_:at_ + PAIRS], rows[:, a, j * R:(j + 1) * R],
                                     ident[0:PAIRS, 0:PAIRS]).then_inc(s_tr, 1)
                pe.wait_ge(s_lim, 2)
                pe.wait_ge(s_const, 3)
                for j in range(2):
                    ins = pe.matmul(pm[0:T, 1, j * PAIRS:(j + 1) * PAIRS], ones[:, :], lim_diag[:, j, :],
                                    start=True, stop=True)
                ins.then_inc(s_pl, 1)
                pe.wait_ge(s_num, 1)
                pe.matmul(pm[0:T, 1, 2 * PAIRS:2 * PAIRS + 1], before[:, :], span[:, 2:3], start=True, stop=True) \
                  .then_inc(s_base, 1)
                pe.sem_inc(s_used, 2)
                pe.wait_ge(s_nil, 1)
                pe.wait_ge(s_span, 1)
                for t in range(T):
                    lo, num, base = spans(pe, t)
                    if t:
                        pe.wait_ge(s_cp, t)
                    for c, (o, n) in enumerate(CHUNKS):
                        pe.matmul(pa[:, c, 0:n], nil[:, 0:R], nil[:, 0:n], start=True, stop=False)
                    with pe.Fori(0, num) as i:
                        for j in range(2):
                            pe.wait_ge(s_hot, 2 * (base + i) + j + 1)
                            for c, (o, n) in enumerate(CHUNKS):
                                ins = pe.matmul(pa[:, c, 0:n], hot_d[:, j, :], hot_s[:, j, o:o + n],
                                                start=False, stop=False)
                            ins.then_inc(s_used, 1)
                    for c, (o, n) in enumerate(CHUNKS):
                        ins = pe.matmul(pa[:, c, 0:n], nil[:, 0:R], nil[:, 0:n], start=False, stop=True)
                    ins.then_inc(s_a, 1)
                    pe.wait_ge(s_cp, t + 1)
                    if t:
                        pe.wait_ge(s_sb, t)
                    for b in range(T):
                        ins = pe.transpose(pt[:, b // 4, (b % 4) * R:(b % 4 + 1) * R], a_sb[:, b * R:(b + 1) * R],
                                           ident[0:R, 0:R])
                    ins.then_inc(s_at, 1)


def gat_phase(nc, scores, at, xl, ident, w_up, bias, part, dst):
    with Phase(nc, "gat") as ph:
        sc = ph.sb("sc", [R, 2, N, HEADS], F32)
        cnt = ph.sb("cnt", [R, 2, T, R], F32)
        vals = ph.sb("vals", [R, T, HEADS, XW], F32)
        top = ph.sb("top", [R, 2, HEADS], F32)
        prob = ph.sb("prob", [R, 2, N], F32)
        wgt = ph.sb("wgt", [R, 2, T, R], F32)
        inv = ph.sb("inv", [R, 2, HEADS], F32)
        res = ph.sb("res", [R, 2, HID], F32)
        gat = [ph.sb(f"gat_{s}", [P, KH, R], F32R) for s in ("hi", "lo")]
        raw = ph.sb("raw", [P, KH, D], F32)
        up = [ph.sb(f"up_{s}", [P, KH, D], F32R) for s in ("hi", "lo")]
        bb = ph.sb("bias", [R, D], F32)
        rows_sb = ph.sb("rows", [R, 2, D], F32)
        pt = [ph.ps(f"pt{h}", [R, 3, BANK]) for h in range(2)]
        po = ph.ps("po", [R, BANK])
        pr = ph.ps("pr", [P, BANK])
        s_x, s_one = ph.sem("x"), ph.sem("one")
        s_sc, s_cnt, s_loop, s_top = ph.sems("sc", 2), ph.sems("cnt", 2), ph.sem("loop"), ph.sem("top")
        s_p, s_pt, s_w, s_o = ph.sem("p"), ph.sem("pt"), ph.sem("w"), ph.sem("o")
        s_res, s_rt, s_hi, s_lo, s_link = ph.sem("res"), ph.sem("rt"), ph.sem("hi"), ph.sem("lo"), ph.sem("link")
        s_raw, s_uhi, s_ulo, s_bias = ph.sem("raw"), ph.sem("uhi"), ph.sem("ulo"), ph.sem("bias")
        s_rows, s_biased, s_up, s_add, s_st = ph.sems("rows", 2), ph.sem("biased"), ph.sem("up"), ph.sem("add"), ph.sems("st", 2)
        scored = scores.rearrange("(t p s) h -> t p (s h)", p=R, s=N)
        at_cols = at.rearrange("b p d -> p b d")
        turned = pr[:, 0:KH * R].rearrange("p (k r) -> p k r", r=R)

        def heads_at(t, a):
            return HEADS * t + HEADS + a

        with nc.Block() as block:
            @block.sync
            def _(sp):
                def tile(t):
                    if t >= 2:
                        sp.wait_ge(s_p, heads_at(t - 1, 0))
                        sp.wait_ge(s_w, heads_at(t - 1, 0))
                    sp.dma_start(sc[:, t % 2, :, :].rearrange("p s h -> p (s h)"), scored[t]).then_inc(s_sc[t % 2], 16)
                    sp.dma_start(cnt[:, t % 2, :, :], at_cols[:, :, t * R:(t + 1) * R]).then_inc(s_cnt[t % 2], 16)
                    if t >= 2:
                        sp.wait_ge(s_st[t % 2], 16 * (t // 2))
                    sp.dma_start(rows_sb[:, t % 2, :], part[t * R:(t + 1) * R, :]).then_inc(s_rows[t % 2], 16)

                def store(t):
                    sp.wait_ge(s_add, t + 2)
                    sp.dma_start(dst[t * R:(t + 1) * R, :], rows_sb[:, t % 2, :]).then_inc(s_st[t % 2], 16)

                tile(0)
                sp.dma_start(bb[:, :], bias.rearrange("(o n) -> o n", o=1).to_broadcast([R, D])).then_inc(s_bias, 16)
                for k in range(T):
                    sp.dma_start(vals[:, k, :, 0:HD], xl[k * R:(k + 1) * R, :].rearrange("p (h d) -> p h d", h=HEADS)) \
                        .then_inc(s_x, 16)
                tile(1)
                sp.dma_start(raw[:, :, :], w_up.rearrange("(k p) n -> p k n", p=P)).then_inc(s_raw, 16)
                for t in range(T):
                    store(t)
                    if t + 2 < T:
                        tile(t + 2)
                for h in range(2):
                    sp.wait_ge(s_st[h], 16 * T // 2)

            @block.gpsimd
            def _(pool):
                pool.memset(vals[:, :, :, HD:XW], 1.0).then_inc(s_one, 1)
                pool.wait_ge(s_bias, 16)
                for t in range(T):
                    pool.wait_ge(s_rows[t % 2], 16 * (t // 2 + 1))
                    pool.tensor_tensor(rows_sb[:, t % 2, :], rows_sb[:, t % 2, :], bb[:, :], ALU.add).then_inc(s_biased, 1)

            @block.vector
            def _(dve):
                for s, n in ((s_w, HEADS), (s_res, 1), (s_lo, 1), (s_add, 1)):
                    dve.sem_inc(s, n)
                dve.wait_ge(s_uhi, 1)
                dve.tensor_tensor(up[1][:, :, :], raw[:, :, :], up[0][:, :, :].bitcast(F32), ALU.subtract).then_inc(s_ulo, 1)
                with dve.Fori(0, T // 2) as i:
                    link = Link(dve, s_link, 4 * i)
                    for h in range(2):
                        t = 2 * i + h
                        dve.wait_ge(s_sc[h], 16 * i + 16)
                        dve.wait_ge(s_p, heads_at(2 * i, 0))
                        dve.tensor_reduce(top[:, h, :], sc[:, h, :, :].rearrange("p s h -> p h s"), AX.X, ALU.max,
                                          negate=True).then_inc(s_top, 1)
                        dve.wait_ge(s_cnt[h], 16 * i + 16)
                        diag = cnt[:, h, bass.ds(t, 1), :].rearrange("p b r -> p (b r)")
                        dve.tensor_tensor(diag, diag, ident[0:R, 0:R], ALU.add).then_inc(s_loop, 1)
                        dve.wait_ge(s_loop, t + 1)
                        for a in range(HEADS):
                            dve.wait_ge(s_pt, heads_at(t, a + 1))
                            dve.wait_ge(s_o, heads_at(t, max(a - 1, 0)))
                            for b in range(3):
                                m = min(4, T - 4 * b)
                                ins = dve.tensor_tensor(wgt[:, a % 2, 4 * b:4 * b + m, :],
                                                        pt[a % 2][:, b, 0:m * R].rearrange("p (b r) -> p b r", r=R),
                                                        cnt[:, h, 4 * b:4 * b + m, :], ALU.mult)
                            ins.then_inc(s_w, 1)
                        dve.wait_ge(s_o, heads_at(t, HEADS))
                        acc = po[:, 0:HEADS * XW].rearrange("p (h d) -> p h d", h=HEADS)
                        link(dve.tensor_scalar(inv[:, h, :], acc[:, :, HD], 1e-16, None, ALU.add))
                        link(dve.reciprocal(inv[:, h, :], inv[:, h, :]))
                        dve.wait_ge(s_rt, 2 * i + 1)
                        for a in range(HEADS):
                            ins = dve.tensor_scalar(res[:, h, a * HD:(a + 1) * HD], acc[:, a, 0:HD],
                                                    inv[:, h, a:a + 1], None, ALU.mult)
                        ins.then_inc(s_res, 1)
                        dve.wait_ge(s_hi, t + 1)
                        dve.tensor_tensor(gat[1][:, :, :], turned, gat[0][:, :, :].bitcast(F32), ALU.subtract) \
                           .then_inc(s_lo, 1)
                        dve.wait_ge(s_biased, t + 1)
                        dve.wait_ge(s_up, t + 1)
                        for c, v in enumerate((pr[0:R, :], po[:, :])):
                            ins = dve.tensor_tensor(rows_sb[:, h, c * BANK:(c + 1) * BANK], v,
                                                    rows_sb[:, h, c * BANK:(c + 1) * BANK], ALU.add)
                        ins.then_inc(s_add, 1)

            @block.scalar
            def _(act):
                act.sem_inc(s_p, HEADS)
                act.wait_ge(s_raw, 16)
                act.activation(up[0][:, :, :], raw[:, :, :], ACT.Copy).then_inc(s_uhi, 1)
                with act.Fori(0, T // 2) as i:
                    for h in range(2):
                        t = 2 * i + h
                        act.wait_ge(s_top, t + 1)
                        for a in range(HEADS):
                            act.wait_ge(s_pt, heads_at(t, max(a - 1, 0)))
                            act.activation(prob[:, a % 2, :], sc[:, h, :, a], ACT.Exp, bias=top[:, h, a:a + 1]) \
                               .then_inc(s_p, 1)
                        act.wait_ge(s_rt, t + 2)
                        act.activation(gat[0][:, :, :], turned, ACT.Copy).then_inc(s_hi, 1)

            @block.tensor
            def _(pe):
                for s, n in ((s_pt, HEADS), (s_o, HEADS), (s_rt, 1)):
                    pe.sem_inc(s, n)
                pe.wait_ge(s_x, 16 * T)
                pe.wait_ge(s_one, 1)
                pe.wait_ge(s_ulo, 1)

                def spread(t, a):
                    pe.wait_ge(s_p, heads_at(t, a + 1))
                    pe.wait_ge(s_w, heads_at(t, max(a - 1, 0)))
                    for b in range(T):
                        ins = pe.transpose(pt[a % 2][:, b // 4, (b % 4) * R:(b % 4 + 1) * R],
                                           prob[:, a % 2, b * R:(b + 1) * R], ident[0:R, 0:R])
                    ins.then_inc(s_pt, 1)

                with pe.Fori(0, T // 2) as i:
                    for h in range(2):
                        t = 2 * i + h
                        spread(t, 0)
                        pe.wait_ge(s_add, t + 1)
                        for a in range(HEADS):
                            if a + 1 < HEADS:
                                spread(t, a + 1)
                            pe.wait_ge(s_w, heads_at(t, a + 1))
                            for b in range(T):
                                ins = pe.matmul(po[:, a * XW:(a + 1) * XW], wgt[:, a % 2, b, :], vals[:, b, a, :],
                                                start=b == 0, stop=b == T - 1)
                            ins.then_inc(s_o, 1)
                        pe.wait_ge(s_res, t + 2)
                        for k in range(KH):
                            ins = pe.transpose(turned[:, k, :], res[:, h, k * P:(k + 1) * P], ident[0:R, 0:R])
                        ins.then_inc(s_rt, 1)
                        pe.wait_ge(s_lo, t + 2)
                        for c, v in enumerate((pr[0:R, :], po[:, :])):
                            for k in range(KH):
                                ins = mm3(pe, v, [x[:, k, :] for x in gat], [x[:, k, c * BANK:(c + 1) * BANK] for x in up],
                                          k == 0, k == KH - 1)
                        ins.then_inc(s_up, 1)


PAIR = 2 * HD
SLABS = D // PAIR
MHEADS = D // HD
NC = len(CHUNKS)
QW = CHUNKS[0][1]
WCHUNKS = 6
EDGE_STEPS = {10 + 3 + 6 + 1 + 3: (1, 3, 5, 7, 9, 11, 14, 18), 10 + 3 + 1 + 3: (1, 3, 5, 7, 9, 10, 11, 13)}


def mix_phase(nc, name, act_hi, act_lo, wq, wk, wv, biases, sum_eps, flip, ident, mixt, z, edges=None):
    steps = [("kv", t) for t in range(T)] + \
            [("q", 0), ("w", 0), ("w", 1), ("q", 1), ("w", 2), ("w", 3), ("pair", 0), ("q", 2), ("w", 4), ("w", 5)] + \
            [("n", j) for j in range(NC)]
    last_steps = [s for s in steps if s[0] != "w"]
    NU = T + NC
    has_y = biases is not None
    W3 = 3 * PAIR
    with Phase(nc, name) as ph:
        raw = ph.sb("raw", [P, 3 * D], F32)
        w_kv = [ph.sb(f"wkv_{s}", [P, KD, 2 * PAIR], F32R) for s in ("hi", "lo")]
        w_q = [ph.sb(f"wq_{s}", [P, KD, PAIR], F32R) for s in ("hi", "lo")]
        kv = [ph.sb(f"kv_{s}", [R, T, W3], F32R) for s in ("hi", "lo")]
        q = [ph.sb(f"q_{s}", [P, N], F32R) for s in ("hi", "lo")]
        y = ph.sb("y", [P, 3, QW], F32)
        neg = ph.sb("neg", [P, 2, QW], F32)
        ex = ph.sb("ex", [P, 2, QW], F32)
        num = ph.sb("num", [P, NC, QW], F32)
        sums_f = ph.sb("sums_f", [P, PAIR + MHEADS], F32)
        sums = [ph.sb(f"sums_{s}", [P, PAIR + MHEADS], F32R) for s in ("hi", "lo")]
        one = ph.sb("one", [R, PAIR], F32)
        nil = ph.sb("nil", [P, QW], BF16)
        if has_y:
            bias_q = ph.sb("bias_q", [P, SLABS], F32)
            bias_now = ph.sb("bias_now", [P, 2], F32)
            bias_kv = ph.sb("bias_kv", [R, 2 * PAIR], F32)
        bank = [ph.ps(f"bank{b}", [P, BANK]) for b in range(4)]
        pkv = ph.ps("pkv", [P, BANK])
        den = ph.ps("den", [MHEADS, NC, BANK])
        s_raw, s_bias, s_bq = ph.sems("raw", 3), ph.sem("bias"), ph.sem("bq")
        s_kv, s_q, s_n, s_w, s_pair = (ph.sem(x) for x in ("kv", "q", "n", "w", "pair"))
        s_exp, s_hi, s_whi, s_num, s_shi = (ph.sem(x) for x in ("exp", "hi", "whi", "num", "shi"))
        s_y, s_val, s_lo, s_wlo, s_sum, s_slo = (ph.sem(x) for x in ("y", "val", "lo", "wlo", "sum", "slo"))
        s_neg = ph.sem("neg")
        s_st, s_nil, s_one, s_zero = ph.sems("st", NC), ph.sem("nil"), ph.sem("one"), ph.sem("zero")
        s_den, s_z, s_zhi, s_col, s_bnow = (ph.sem(x) for x in ("den", "z", "zhi", "col", "bnow"))

        def unit(kind, j):
            return j if kind == "kv" else T + j

        def val_at(g, n):
            return NU * g + NU + n

        lo_at = val_at

        def num_at(g, n):
            return NC * g + NC + n

        def w_at(g, c):
            return WCHUNKS * g + c

        def width(kind, j):
            return (R, 2 * PAIR) if kind == "kv" else (P, CHUNKS[j][1])

        def w_part(c):
            if c >= 4:
                return [x[:, 4 * (c - 4):4 * (c - 4) + 4, :] for x in w_q]
            if flip:
                return [x[:, 4 * (c % 2):4 * (c % 2) + 4, (c // 2) * PAIR:(c // 2 + 1) * PAIR] for x in w_kv]
            return [x[:, 2 * c:2 * c + 2, :] for x in w_kv]

        def w_raw(c, b):
            if flip:
                return bank[b][:, :].rearrange("p (k n) -> p k n", n=PAIR)
            return raw[:, BANK * c:BANK * c + BANK].rearrange("p (k n) -> p k n", n=PAIR if c >= 4 else 2 * PAIR)

        def banks(seq):
            out, used = {}, []
            for s in seq:
                if s[0] == "pair" or (s[0] == "w" and not flip):
                    continue
                out[s] = (len(used) % 4, used[-4] if len(used) >= 4 else None)
                used.append(s)
            return out

        z_f = num[0:MHEADS, :, :].rearrange("p j n -> p (j n)")[:, 0:N]

        with nc.Block() as block:
            @block.sync
            def _(sp):
                def load(g):
                    cols = slice(g * PAIR, (g + 1) * PAIR)
                    for j, m in enumerate((wk, wv, wq)):
                        if flip:
                            if g:
                                sp.wait_ge(s_w, w_at(g - 1, 2 * j + 2))
                            sp.dma_start(raw[:, j * D:(j + 1) * D], m[cols, :]).then_inc(s_raw[j], 16)
                            continue
                        if g and j != 1:
                            sp.wait_ge(s_wlo, w_at(g - 1, 4 if j == 0 else 6))
                        to = raw[:, 2 * D:].rearrange("p (k n) -> p k n", n=PAIR) if j == 2 else \
                            raw[:, 0:2 * D].rearrange("p (k n) -> p k n", n=2 * PAIR)[:, :, j * PAIR:(j + 1) * PAIR]
                        sp.dma_start(to, m[:, cols].rearrange("(k p) n -> p k n", p=P)).then_inc(s_raw[j], 16)

                def bias(g):
                    if g:
                        sp.wait_ge(s_y, T * g)
                    for j, b in enumerate(biases[1:]):
                        sp.dma_start(bias_kv[:, j * PAIR:(j + 1) * PAIR], b[g * PAIR:(g + 1) * PAIR]
                                     .rearrange("(o n) -> o n", o=1).to_broadcast([R, PAIR])).then_inc(s_bias, 16)

                for j in range(NC):
                    sp.sem_inc(s_st[j], 16)
                load(0)
                if edges is not None:
                    edges.sync(sp)
                if has_y:
                    sp.dma_start(bias_q[:, :], biases[0].rearrange("(k p) -> p k", p=P),
                                 allow_slow_non_contiguous=True).then_inc(s_bq, 16)
                    bias(0)
                load(1)
                for g in range(SLABS):
                    if has_y and g + 1 < SLABS:
                        bias(g + 1)
                    if g + 2 < SLABS:
                        load(g + 2)
                    for j, (o, n) in enumerate(CHUNKS):
                        sp.wait_ge(s_num, num_at(g, j + 1))
                        sp.dma_start(mixt[g * P:(g + 1) * P, o:o + n], num[:, j, 0:n]).then_inc(s_st[j], 16)
                for j in range(NC):
                    sp.wait_ge(s_st[j], 16 * SLABS + 16)

            @block.gpsimd
            def _(pool):
                pool.memset(nil[:, :], 0.0).then_inc(s_nil, 1)
                pool.memset(one[:, :], 1.0).then_inc(s_one, 1)
                pool.memset(sums_f[:, :], 0.0).then_inc(s_zero, 1)
                if edges is not None:
                    edges.gpsimd(pool, 0, MIX_BATCHES)

            @block.vector
            def _(dve):
                def start(g, kind, j):
                    if kind == "kv" and has_y:
                        dve.wait_ge(s_kv, T * g + j + 1)
                        dve.wait_ge(s_lo, lo_at(g, max(j - 2, 0)))
                        dve.tensor_tensor(y[0:R, j % 3, 0:2 * PAIR], bank[at[kind, j][0]][0:R, 0:2 * PAIR],
                                          bias_kv[:, :], ALU.add).then_inc(s_y, 1)

                def middle(g, kind, j):
                    if kind in ("kv", "q"):
                        u, (p, n) = unit(kind, j), width(kind, j)
                        n = PAIR if kind == "kv" else n
                        dve.wait_ge(s_exp, NU * g + u + 1)
                        from_, more = bank[at[kind, j][0]][0:p, 0:n], 1.0
                        if kind == "kv" and has_y:
                            from_ = y[0:R, u % 3, 0:n]
                        else:
                            dve.wait_ge(s_lo, lo_at(g, max(u - 2, 0)))
                        if kind == "q" and has_y:
                            dve.wait_ge(s_bnow, g + 1)
                            more = bias_now[:, 1:2]
                        dve.scalar_tensor_tensor(y[0:p, u % 3, 0:n], from_, more, ex[0:p, u % 2, 0:n],
                                                 ALU.add, ALU.max).then_inc(s_val, 1)
                    elif kind == "w":
                        weights(w_at(g + 1, j + 1), j, at.get((kind, j), (0,))[0])
                    elif kind == "pair":
                        dve.wait_ge(s_pair, g + 1)
                        dve.wait_ge(s_slo, g + 1)
                        dve.memset(sums_f[:, PAIR:], 0.0).then_inc(s_col, 1)
                        for a in range(2):
                            rows = slice(HD * a, HD * a + HD)
                            dve.tensor_copy(sums_f[rows, rows], pkv[rows, rows])
                        dve.wait_ge(s_col, g + 1)
                        for a in range(2):
                            rows = slice(HD * a, HD * a + HD)
                            ins = dve.tensor_scalar(sums_f[rows, bass.ds(PAIR + 2 * g + a, 1)],
                                                    pkv[rows, PAIR:PAIR + 1], sum_eps, None, ALU.add)
                        ins.then_inc(s_sum, 1)

                def finish(g, kind, j):
                    if kind in ("kv", "q"):
                        u, (p, n) = unit(kind, j), width(kind, j)
                        dve.wait_ge(s_hi, NU * g + u + 1)
                        if kind == "q":
                            o = CHUNKS[j][0]
                            dve.tensor_tensor(q[1][:, o:o + n], y[:, u % 3, 0:n], q[0][:, o:o + n].bitcast(F32),
                                              ALU.subtract).then_inc(s_lo, 1)
                        elif has_y:
                            dve.tensor_tensor(kv[1][:, j, 0:n], y[0:R, u % 3, 0:n], kv[0][:, j, 0:n].bitcast(F32),
                                              ALU.subtract).then_inc(s_lo, 1)
                        else:
                            dve.tensor_tensor(kv[1][:, j, 0:PAIR], y[0:R, u % 3, 0:PAIR],
                                              kv[0][:, j, 0:PAIR].bitcast(F32), ALU.subtract)
                            dve.tensor_tensor(kv[1][:, j, PAIR:n], bank[at[kind, j][0]][0:R, PAIR:n],
                                              kv[0][:, j, PAIR:n].bitcast(F32), ALU.subtract).then_inc(s_lo, 1)
                    elif kind == "pair":
                        dve.wait_ge(s_shi, g + 1)
                        dve.tensor_tensor(sums[1][:, :], sums_f[:, :], sums[0][:, :].bitcast(F32), ALU.subtract) \
                           .then_inc(s_slo, 1)

                def weights(count, c, b):
                    dve.wait_ge(s_whi, count)
                    hi, lo = w_part(c)
                    dve.tensor_tensor(lo, w_raw(c, b), hi.bitcast(F32), ALU.subtract).then_inc(s_wlo, 1)

                def slab(g, seq):
                    if has_y:
                        dve.wait_ge(s_bias, 32 * g + 32)
                    todo = edges.turns(dve, g) if edges is not None else None
                    for i in range(len(seq) + 2):
                        if has_y and i == T // 2:
                            dve.wait_ge(s_val, val_at(g, 1))
                            dve.tensor_scalar(bias_now[:, 0:1], bias_q[:, bass.ds(g, 1)], -1.0, None, ALU.mult)
                            dve.tensor_scalar(bias_now[:, 1:2], bias_q[:, bass.ds(g, 1)], 1.0, None, ALU.add) \
                               .then_inc(s_bnow, 1)
                        if i < len(seq):
                            start(g, *seq[i])
                        if 1 <= i <= len(seq):
                            middle(g, *seq[i - 1])
                        if i >= 2:
                            finish(g, *seq[i - 2])
                        if todo is not None and i in EDGE_STEPS[len(seq)]:
                            todo.step()

                dve.sem_inc(s_val, NU)
                dve.sem_inc(s_lo, NU)
                dve.sem_inc(s_slo, 1)
                dve.wait_ge(s_one, 1)
                dve.tensor_copy(kv[0][:, :, 2 * PAIR:], one[:, :].unsqueeze(1).to_broadcast([R, T, PAIR]))
                dve.tensor_scalar(kv[1][:, :, 2 * PAIR:], one[:, :].unsqueeze(1).to_broadcast([R, T, PAIR]), 0.0, None,
                                  ALU.mult)
                if edges is not None:
                    edges.vector(dve)
                if has_y:
                    dve.wait_ge(s_bq, 16)
                at = {}
                for c in range(WCHUNKS):
                    weights(c + 1, c, c % 4)
                dve.wait_ge(s_zero, 1)
                at = banks(steps)
                with dve.Fori(0, SLABS - 1) as g:
                    slab(g, steps)
                at = banks(last_steps)
                slab(SLABS - 1, last_steps)
                dve.wait_ge(s_den, 1)
                for j in range(NC):
                    dve.wait_ge(s_st[j], 16 * SLABS + 16)
                for j, (o, n) in enumerate(CHUNKS):
                    ins = dve.tensor_scalar(z_f[:, o:o + n], den[:, j, 0:n], 1e-6, None, ALU.add)
                ins.then_inc(s_z, 1)
                dve.wait_ge(s_z, 1)
                dve.reciprocal(z_f[:, :], z_f[:, :]).then_inc(s_z, 1)
                dve.wait_ge(s_zhi, 1)
                dve.tensor_tensor(z[1][:, :], z_f[:, :], z[0][:, :].bitcast(F32), ALU.subtract)

            @block.scalar
            def _(act):
                def start(g, kind, j):
                    if kind in ("kv", "q"):
                        u, (p, n) = unit(kind, j), width(kind, j)
                        from_, more = bank[at[kind, j][0]][0:p, 0:n], {}
                        if kind == "q":
                            act.wait_ge(s_q, NC * g + j + 1)
                            if has_y:
                                act.wait_ge(s_bnow, g + 1)
                                more = {"bias": bias_now[:, 0:1]}
                        else:
                            n = PAIR
                            if has_y:
                                act.wait_ge(s_y, T * g + j + 1)
                                from_ = y[0:R, u % 3, 0:n]
                            else:
                                act.wait_ge(s_kv, T * g + j + 1)
                                from_ = from_[:, 0:n]
                        act.wait_ge(s_val, val_at(g, max(u - 1, 0)))
                        act.activation(neg[0:p, u % 2, 0:n], from_, ACT.Relu, scale=-1.0, **more).then_inc(s_neg, 1)
                        act.wait_ge(s_neg, NU * g + u + 1)
                        act.activation(ex[0:p, u % 2, 0:n], neg[0:p, u % 2, 0:n], ACT.Exp, scale=-1.0).then_inc(s_exp, 1)
                    elif kind == "w":
                        if not flip:
                            if j < 4:
                                act.wait_ge(s_kv, T * g + T)
                            else:
                                act.wait_ge(s_q, NC * g + NC)
                            for x in ((0, 1) if j < 4 else (2,)):
                                act.wait_ge(s_raw[x], 16 * g + 32)
                        weights(w_at(g + 1, j + 1), j, at.get((kind, j), (0,))[0])
                    elif kind == "n":
                        n = CHUNKS[j][1]
                        act.wait_ge(s_n, NC * g + j + 1)
                        act.wait_ge(s_st[j], 16 * g + 16)
                        act.activation(num[:, j, 0:n], bank[at[kind, j][0]][:, 0:n], ACT.Copy).then_inc(s_num, 1)

                def finish(g, kind, j):
                    if kind in ("kv", "q"):
                        u, (p, n) = unit(kind, j), width(kind, j)
                        act.wait_ge(s_val, val_at(g, u + 1))
                        if kind == "q":
                            o = CHUNKS[j][0]
                            act.activation(q[0][:, o:o + n], y[:, u % 3, 0:n], ACT.Copy).then_inc(s_hi, 1)
                        elif has_y:
                            act.activation(kv[0][:, j, 0:n], y[0:R, u % 3, 0:n], ACT.Copy).then_inc(s_hi, 1)
                        else:
                            act.activation(kv[0][:, j, 0:PAIR], y[0:R, u % 3, 0:PAIR], ACT.Copy)
                            act.activation(kv[0][:, j, PAIR:n], bank[at[kind, j][0]][0:R, PAIR:n], ACT.Copy) \
                               .then_inc(s_hi, 1)
                    elif kind == "pair":
                        act.wait_ge(s_sum, g + 1)
                        act.activation(sums[0][:, :], sums_f[:, :], ACT.Copy).then_inc(s_shi, 1)

                def weights(count, c, b):
                    if flip:
                        act.wait_ge(s_w, count)
                    act.activation(w_part(c)[0], w_raw(c, b), ACT.Copy).then_inc(s_whi, 1)

                def slab(g, seq):
                    for i in range(len(seq) + 1):
                        late = i < len(seq) and seq[i][0] == "n"
                        if i < len(seq) and not late:
                            start(g, *seq[i])
                        if i >= 1:
                            finish(g, *seq[i - 1])
                        if late:
                            start(g, *seq[i])

                act.sem_inc(s_num, NC)
                for j in range(3):
                    act.wait_ge(s_raw[j], 16)
                at = {}
                for c in range(WCHUNKS):
                    weights(c + 1, c, c % 4)
                at = banks(steps)
                with act.Fori(0, SLABS - 1) as g:
                    slab(g, steps)
                at = banks(last_steps)
                slab(SLABS - 1, last_steps)
                act.wait_ge(s_z, 2)
                act.activation(z[0][:, :], z_f[:, :], ACT.Copy).then_inc(s_zhi, 1)

            @block.tensor
            def _(pe):
                def free(g, before):
                    if before is None:
                        return
                    kind, j = before
                    if kind == "kv" and has_y:
                        pe.wait_ge(s_y, T * g + j + 1)
                    elif kind == "kv":
                        pe.wait_ge(s_lo, lo_at(g, j + 1))
                    elif kind == "q":
                        pe.wait_ge(s_val, val_at(g, T + j + 1))
                    elif kind == "w":
                        pe.wait_ge(s_wlo, w_at(g + 1, j + 1))
                    else:
                        pe.wait_ge(s_num, num_at(g, j + 1))

                def transpose(c, b):
                    for i in range(4):
                        k = 4 * (c % 2) + i
                        ins = pe.transpose(bank[b][:, i * P:(i + 1) * P],
                                           raw[:, (c // 2) * D + k * P:(c // 2) * D + (k + 1) * P], ident[:, :])
                    ins.then_inc(s_w, 1)

                def slab(g, seq, at):
                    pe.wait_ge(s_wlo, w_at(g, WCHUNKS))
                    pe.wait_ge(s_num, num_at(g, 0))
                    for kind, j in seq:
                        if (kind, j) in at:
                            b, before = at[kind, j]
                            out = bank[b]
                            free(g, before)
                        if kind == "kv":
                            rows = slice(j * R, (j + 1) * R)
                            for k in range(KD):
                                ins = mm3(pe, out[0:R, 0:2 * PAIR], (act_hi[:, k, rows], act_lo[:, k, rows]),
                                          [x[:, k, :] for x in w_kv], k == 0, k == KD - 1)
                            ins.then_inc(s_kv, 1)
                        elif kind == "q":
                            o, n = CHUNKS[j]
                            for k in range(KD):
                                ins = mm3(pe, out[:, 0:n], [x[:, k, :] for x in w_q],
                                          (act_hi[:, k, o:o + n], act_lo[:, k, o:o + n]), k == 0, k == KD - 1)
                            ins.then_inc(s_q, 1)
                        elif kind == "w" and flip:
                            if j % 2 == 0:
                                pe.wait_ge(s_raw[j // 2], 16 * g + 32)
                            transpose(j, b)
                        elif kind == "pair":
                            pe.wait_ge(s_lo, lo_at(g, T))
                            for t in range(T):
                                ins = mm3(pe, pkv[:, 0:2 * PAIR], [x[:, t, 0:PAIR] for x in kv],
                                          [x[:, t, PAIR:] for x in kv], t == 0, t == T - 1)
                            ins.then_inc(s_pair, 1)
                        elif kind == "n":
                            o, n = CHUNKS[j]
                            if j == 0:
                                pe.wait_ge(s_slo, g + 2)
                                pe.wait_ge(s_lo, lo_at(g, NU))
                            mm3(pe, out[:, 0:n], [x[:, 0:PAIR] for x in sums], [x[:, o:o + n] for x in q], True, True) \
                                .then_inc(s_n, 1)
                            for a, b_ in ((0, 0), (0, 1), (1, 0)):
                                pe.matmul(den[:, j, 0:n], sums[a][:, PAIR:], q[b_][:, o:o + n], start=False, stop=False)

                if flip:
                    for c in range(WCHUNKS):
                        if c % 2 == 0:
                            pe.wait_ge(s_raw[c // 2], 16)
                        if c >= 4:
                            pe.wait_ge(s_wlo, c - 3)
                        transpose(c, c % 4)
                pe.wait_ge(s_nil, 1)
                for j, (o, n) in enumerate(CHUNKS):
                    pe.matmul(den[:, j, 0:n], nil[:, 0:MHEADS], nil[:, 0:n], start=True, stop=False)
                with pe.Fori(0, SLABS - 1) as g:
                    slab(g, steps, banks(steps))
                slab(SLABS - 1, last_steps, banks(last_steps))
                for j, (o, n) in enumerate(CHUNKS):
                    ins = pe.matmul(den[:, j, 0:n], nil[:, 0:MHEADS], nil[:, 0:n], start=False, stop=True)
                ins.then_inc(s_den, 1)


def output_phase(nc, name, act_hi, act_lo, mixt, z, wo, flip, ident, resid, dst, edges=None):
    WC = 4
    with Phase(nc, name) as ph:
        part = ph.sb("part", [P, 2, N], F32)
        head_f = ph.sb("head_f", [MHEADS, D], F32)
        head = ph.sb("head", [MHEADS, D], F32R)
        raw = ph.sb("raw", [P, 2 * D], F32)
        w = [[ph.sb(f"w{h}_{s}", [P, KD, SLAB], F32R) for s in ("hi", "lo")] for h in range(2)]
        res = ph.sb("res", [R, 2, T, SLAB], F32)
        bank = [ph.ps(f"bank{b}", [P, BANK]) for b in range(4)]
        wide = [ph.ps(f"wide{b}", [P, BANK]) for b in range(NC)]
        s_part, s_scaled, s_phi, s_plo = ph.sems("part", 2), ph.sem("scaled"), ph.sem("phi"), ph.sem("plo")
        s_one, s_head, s_zb = ph.sem("one"), ph.sem("head"), ph.sem("zb")
        s_raw, s_w, s_whi, s_wlo = ph.sem("raw"), ph.sem("w"), ph.sem("whi"), ph.sem("wlo")
        s_res, s_mm, s_out, s_st = ph.sems("res", 2), ph.sem("mm"), ph.sem("out"), ph.sems("st", 2)

        def chunk(c, h):
            if flip:
                i, half = c // 2, c % 2
                return wide[c % NC][:, :].rearrange("p (k n) -> p k n", n=P), \
                    [x[:, 4 * half:4 * half + 4, i * P:(i + 1) * P] for x in w[h]]
            return raw[:, c * BANK:(c + 1) * BANK].rearrange("p (k n) -> p k n", n=SLAB), \
                [x[:, 2 * c:2 * c + 2, :] for x in w[h]]

        with nc.Block() as block:
            @block.sync
            def _(sp):
                def slab(g):
                    cols = slice(g * SLAB, (g + 1) * SLAB)
                    if g:
                        if flip:
                            sp.wait_ge(s_w, WC * g)
                        else:
                            sp.wait_ge(s_wlo, WC * g)
                    if flip:
                        sp.dma_start(raw[:, :].rearrange("p (i k) -> p i k", i=2),
                                     wo[cols, :].rearrange("(i p) k -> p i k", p=P)).then_inc(s_raw, 16)
                    else:
                        sp.dma_start(raw[:, :].rearrange("p (k n) -> p k n", n=SLAB),
                                     wo[:, cols].rearrange("(k p) n -> p k n", p=P)).then_inc(s_raw, 16)

                def rows(g):
                    cols = slice(g * SLAB, (g + 1) * SLAB)
                    if g >= 2:
                        sp.wait_ge(s_st[g % 2], 16 * (g // 2))
                    sp.dma_start(res[:, g % 2, :, :], resid[:, cols].rearrange("(t p) n -> p t n", p=R)) \
                        .then_inc(s_res[g % 2], 16)

                for k in range(KD):
                    if k >= 2:
                        sp.wait_ge(s_plo, k - 1)
                    sp.dma_start(part[:, k % 2, :], mixt[k * P:(k + 1) * P, :]).then_inc(s_part[k % 2], 16)
                    if k == 0:
                        slab(0)
                rows(0)
                for g in range(NSLAB):
                    if g + 1 < NSLAB:
                        slab(g + 1)
                        rows(g + 1)
                    sp.wait_ge(s_out, T * (g + 1))
                    cols = slice(g * SLAB, (g + 1) * SLAB)
                    sp.dma_start(dst[:, cols].rearrange("(t p) n -> p t n", p=R), res[:, g % 2, :, :]) \
                        .then_inc(s_st[g % 2], 16)
                for h in range(2):
                    sp.wait_ge(s_st[h], 16 * NSLAB // 2)

            @block.gpsimd
            def _(pool):
                pool.memset(head_f[:, :], 1.0).then_inc(s_one, 1)
                pool.wait_ge(s_one, 1)
                pool.affine_select(out=head_f[:, :], in_=head_f[:, :], compare_op=ALU.is_ge, fill=0.0,
                                   base=0, pattern=[[1, D]], channel_multiplier=-HD).then_inc(s_one, 1)
                pool.wait_ge(s_one, 2)
                pool.affine_select(out=head_f[:, :], in_=head_f[:, :], compare_op=ALU.is_ge, fill=0.0,
                                   base=HD - 1, pattern=[[-1, D]], channel_multiplier=HD).then_inc(s_one, 1)
                if edges is not None:
                    edges.gpsimd(pool, MIX_BATCHES, BATCHES)

            @block.vector
            def _(dve):
                def split(g, c):
                    dve.wait_ge(s_whi, WC * g + c + 1)
                    whole, (hi, lo) = chunk(c, g % 2)
                    dve.tensor_tensor(lo, whole, hi.bitcast(F32), ALU.subtract).then_inc(s_wlo, 1)

                dve.wait_ge(s_one, 3)
                dve.tensor_copy(head[:, :], head_f[:, :]).then_inc(s_head, 1)
                for c in range(WC):
                    split(0, c)
                for k in range(KD + 1):
                    if k < KD:
                        dve.wait_ge(s_part[k % 2], 16 * (k // 2 + 1))
                        dve.wait_ge(s_zb, k + 1)
                        for j, (o, n) in enumerate(CHUNKS):
                            ins = dve.tensor_tensor(part[:, k % 2, o:o + n], part[:, k % 2, o:o + n], wide[j][:, 0:n],
                                                    ALU.mult)
                        ins.then_inc(s_scaled, 1)
                    if k:
                        dve.wait_ge(s_phi, k)
                        dve.tensor_tensor(act_lo[:, k - 1, :], part[:, (k - 1) % 2, :], act_hi[:, k - 1, :].bitcast(F32),
                                          ALU.subtract).then_inc(s_plo, 1)
                todo = edges.turns(dve, None) if edges is not None else None
                for g in range(NSLAB):
                    for t in range(T):
                        u = T * g + t
                        if g + 1 < NSLAB and t in (2, 4, 6, 8):
                            split(g + 1, t // 2 - 1)
                        if t == 0:
                            dve.wait_ge(s_res[g % 2], 16 * (g // 2 + 1))
                        dve.wait_ge(s_mm, u + 1)
                        dve.tensor_tensor(res[:, g % 2, t, :], bank[u % 4][0:R, 0:SLAB], res[:, g % 2, t, :], ALU.add) \
                           .then_inc(s_out, 1)
                        if todo is not None and u % 2 and todo.left():
                            todo.step()
                while todo is not None and todo.left():
                    todo.step()

            @block.scalar
            def _(act):
                def split(g, c):
                    if flip:
                        act.wait_ge(s_w, WC * g + c + 1)
                    else:
                        act.wait_ge(s_raw, 16 * (g + 1))
                        if g >= 2:
                            act.wait_ge(s_mm, T * (g - 1))
                    whole, (hi, lo) = chunk(c, g % 2)
                    act.activation(hi, whole, ACT.Copy).then_inc(s_whi, 1)

                for c in range(WC):
                    split(0, c)
                for k in range(KD):
                    act.wait_ge(s_scaled, k + 1)
                    act.activation(act_hi[:, k, :], part[:, k % 2, :], ACT.Copy).then_inc(s_phi, 1)
                for g in range(1, NSLAB):
                    for c in range(WC):
                        split(g, c)

            @block.tensor
            def _(pe):
                def transpose(g, c):
                    pe.wait_ge(s_raw, 16 * (g + 1))
                    n = WC * g + c
                    if c >= NC:
                        pe.wait_ge(s_wlo, n - NC + 1)
                    elif g:
                        pe.wait_ge(s_wlo, WC * g)
                    i, half = c // 2, c % 2
                    for k in range(4):
                        at = i * D + (4 * half + k) * P
                        ins = pe.transpose(wide[c % NC][:, k * P:(k + 1) * P], raw[:, at:at + P], ident[:, :])
                    ins.then_inc(s_w, 1)

                if flip:
                    for c in range(WC):
                        transpose(0, c)
                    pe.wait_ge(s_wlo, WC)
                pe.wait_ge(s_head, 1)
                for k in range(KD):
                    if k:
                        pe.wait_ge(s_scaled, k)
                    for j, (o, n) in enumerate(CHUNKS):
                        for s in range(2):
                            ins = pe.matmul(wide[j][:, 0:n], head[:, k * P:(k + 1) * P], z[s][:, o:o + n],
                                            start=s == 0, stop=s == 1)
                    ins.then_inc(s_zb, 1)
                pe.wait_ge(s_plo, KD)
                for g in range(NSLAB):
                    pe.wait_ge(s_wlo, WC * (g + 1))
                    for t in range(T):
                        u = T * g + t
                        if flip and g + 1 < NSLAB and t in (1, 3, 5, 7):
                            transpose(g + 1, t // 2)
                        if u >= 4:
                            pe.wait_ge(s_out, u - 3)
                        rows = slice(t * R, (t + 1) * R)
                        for k in range(KD):
                            ins = mm3(pe, bank[u % 4][0:R, 0:SLAB], (act_hi[:, k, rows], act_lo[:, k, rows]),
                                      [x[:, k, :] for x in w[g % 2]], k == 0, k == KD - 1)
                        ins.then_inc(s_mm, 1)


E_N = 8
CAP0 = 2 * N // E_N
LIST = 3
CAPR = CAP0 // LIST
H0 = 512
KH0 = H0 // P
CAP1 = N // E_N
PAD1 = -CAP1 % 8
H1 = 256
KH1 = H1 // P
BLOCKS = N // P + E_N
TOPW = N + 8


def exact_exp(dve, link, x, whole, rest, poly):
    every = (slice(None),) * 3
    n, bits = whole[:, 0, :, :], whole[:, 1, :, :]
    link(dve.tensor_scalar(x[every], x[every], -87.0, None, ALU.max))
    link(dve.tensor_scalar(n, x[every], 1.0 / math.log(2.0), None, ALU.mult))
    link(dve.tensor_copy(poly[every], n))
    ln2 = 0.693359375
    dve.tensor_scalar(bits, poly[every], 127.0, None, ALU.add)
    link(dve.scalar_tensor_tensor(rest[every], poly[every], -ln2, x[every], ALU.mult, ALU.add))
    link(dve.scalar_tensor_tensor(rest[every], poly[every], ln2 - math.log(2.0), rest[every], ALU.mult, ALU.add))
    dve.tensor_scalar(bits, bits, 23, None, ALU.logical_shift_left)
    link(dve.tensor_scalar(poly[every], rest[every], 1.0 / math.factorial(10), None, ALU.mult))
    for k in range(9, 0, -1):
        link(dve.scalar_tensor_tensor(poly[every], poly[every], 1.0 / math.factorial(k), rest[every], ALU.add, ALU.mult))
    link(dve.scalar_tensor_tensor(x[every], poly[every], 1.0, bits.bitcast(F32), ALU.add, ALU.mult))


def gate_steps(ph, nc):
    gate = ph.sb("gate", [P, KD, E_N], F32)
    g_hi, g_lo = (ph.sb(f"gate_{s}", [P, KD, E_N], F32R) for s in ("hi", "lo"))
    prob = ph.sb("prob", [R, T, E_N], F32)
    top = ph.sb("gtop", [R, T], F32)
    ps = ph.ps("gates", [R, T, E_N])
    whole = ph.sb("whole", [R, 2, T, E_N], I32)
    rest = ph.sb("rest", [R, T, E_N], F32)
    poly = ph.sb("poly", [R, T, E_N], F32)
    s_g, s_ghi, s_glo, s_mm = ph.sem("g_in"), ph.sem("g_hi"), ph.sem("g_lo"), ph.sem("g_mm")
    s_prob, s_l = ph.sem("g_prob"), ph.sem("g_link")

    def sync(sp, w):
        sp.dma_start(gate[:, :, :], w.rearrange("(k p) e -> p k e", p=P)).then_inc(s_g, 16)

    def scalar(act):
        act.wait_ge(s_g, 16)
        act.activation(g_hi[:, :, :], gate[:, :, :], ACT.Copy).then_inc(s_ghi, 1)

    def tensor(pe, act_hi, act_lo):
        pe.wait_ge(s_glo, 1)
        for t in range(T):
            rows = slice(t * R, (t + 1) * R)
            for k in range(KD):
                ins = mm3(pe, ps[:, t, :], (act_hi[:, k, rows], act_lo[:, k, rows]),
                          (g_hi[:, k, :], g_lo[:, k, :]), k == 0, k == KD - 1)
        ins.then_inc(s_mm, 1)

    def vector(dve):
        link = Link(dve, s_l)
        wide = top[:, :].unsqueeze(2).to_broadcast([R, T, E_N])
        dve.wait_ge(s_ghi, 1)
        dve.tensor_tensor(g_lo[:, :, :], gate[:, :, :], g_hi[:, :, :].bitcast(F32), ALU.subtract).then_inc(s_glo, 1)
        dve.wait_ge(s_mm, 1)
        link(dve.tensor_reduce(top[:, :], ps[:, :, :], AX.X, ALU.max))
        link(dve.tensor_tensor(prob[:, :, :], ps[:, :, :], wide, ALU.subtract))
        exact_exp(dve, link, prob, whole, rest, poly)
        link(dve.tensor_reduce(top[:, :], prob[:, :, :], AX.X, ALU.add))
        link(dve.reciprocal(top[:, :], top[:, :]))
        dve.tensor_tensor(prob[:, :, :], prob[:, :, :], wide, ALU.mult).then_inc(s_prob, 1)

    return prob, s_prob, sync, scalar, tensor, vector


def spread_nodes(pe, pt, x, ident):
    for t in range(T):
        ins = pe.transpose(pt[:, t // 4, (t % 4) * R:(t % 4 + 1) * R], x[:, t, :], ident[0:R, 0:R])
    return ins


def gather_nodes(dve, out, pt):
    for b in range(3):
        n = min(4, T - 4 * b) * R
        ins = dve.tensor_copy(out[:, 4 * b * R:4 * b * R + n], pt[:, b, 0:n])
    return ins


def choose_phase(nc, act_hi, act_lo, gate_w, ident, chosen, share):
    with Phase(nc, "choose") as ph:
        prob, s_prob, g_sync, g_scalar, g_tensor, g_vector = gate_steps(ph, nc)
        work = ph.sb("work", [E_N, N], F32)
        best = ph.sb("best", [E_N, 2, CAP0], F32)
        place = ph.sb("place", [E_N, CAP0], U32)
        pt = ph.ps("pt", [E_N, 3, BANK])
        pc = ph.ps("pc", [CAPR, 2, LIST, E_N])
        s_tr, s_link, s_best, s_cols, s_got = ph.sem("tr"), ph.sem("link"), ph.sem("best"), ph.sem("cols"), ph.sem("got")
        with nc.Block() as block:
            @block.sync
            def _(sp):
                g_sync(sp, gate_w)

            @block.scalar
            def _(act):
                g_scalar(act)

            @block.tensor
            def _(pe):
                g_tensor(pe, act_hi, act_lo)
                pe.wait_ge(s_prob, 1)
                spread_nodes(pe, pt, prob, ident).then_inc(s_tr, 1)
                pe.wait_ge(s_best, 1)
                for a in range(2):
                    for j in range(LIST):
                        ins = pe.transpose(pc[:, a, j, :], best[:, a, j * CAPR:(j + 1) * CAPR], ident[0:E_N, 0:E_N])
                ins.then_inc(s_cols, 1)

            @block.vector
            def _(dve):
                g_vector(dve)
                dve.wait_ge(s_tr, 1)
                link = Link(dve, s_link)
                link(gather_nodes(dve, work, pt))
                for i in range(CAP0 // 8):
                    at = slice(8 * i, 8 * i + 8)
                    link(dve.max(best[:, 1, at], work[:, :]))
                    link(dve.max_index(place[:, at], best[:, 1, at], work[:, :]))
                    link(dve.match_replace(work[:, :], best[:, 1, at], work[:, :], -1.0))
                dve.tensor_copy(best[:, 0, :], place[:, :]).then_inc(s_best, 1)
                dve.wait_ge(s_cols, 1)
                dve.tensor_copy(chosen[:, :, :], pc[:, 0, :, :])
                dve.tensor_copy(share[:, :, :], pc[:, 1, :, :]).then_inc(s_got, 1)
                dve.wait_ge(s_got, 1)


def expert_phase(nc, y, chosen, share, w1, w2, ident, dst):
    with Phase(nc, "expert") as ph:
        now = ph.sb("now", [CAPR, 2, LIST], I32)
        rows = ph.sb("rows", [CAPR, 2, LIST, D], F32)
        x = [ph.sb(f"x_{s}", [P, KD, CAP0], F32R) for s in ("hi", "lo")]
        hid_f = ph.sb("hid_f", [P, 2, CAP0], F32)
        hid = [ph.sb(f"hid_{s}", [P, KH0, CAP0], F32R) for s in ("hi", "lo")]
        raw = ph.sb("raw", [P, 2, KD * H0], F32)
        a = [ph.sb(f"w1_{s}", [P, KD, H0], F32R) for s in ("hi", "lo")]
        b = [ph.sb(f"w2_{s}", [P, KH0, D], F32R) for s in ("hi", "lo")]
        out = ph.sb("out", [CAPR, LIST, D], F32)
        px = [ph.ps(f"px{i}", [P, BANK]) for i in range(4)]
        po = [ph.ps(f"po{i}", [P, BANK]) for i in range(4)]
        s_now, s_rows, s_raw = ph.sem("now"), ph.sems("rows", 2), ph.sems("raw", 2)
        s_ahi, s_alo, s_bhi, s_blo = ph.sem("ahi"), ph.sem("alo"), ph.sem("bhi"), ph.sem("blo")
        s_tr, s_xhi, s_xlo = ph.sem("tr"), ph.sem("xhi"), ph.sem("xlo")
        s_h, s_gelu, s_hhi, s_hlo = ph.sem("h"), ph.sem("gelu"), ph.sem("hhi"), ph.sem("hlo")
        s_o, s_out, s_add, s_turn = ph.sem("o"), ph.sem("out"), ph.sem("add"), ph.sem("turn")
        OUTS = [(j, c) for j in range(LIST) for c in range(D // BANK)]
        NO = len(OUTS)
        with nc.Block() as block:
            @block.sync
            def _(sp):
                for e in range(E_N):
                    if e:
                        sp.wait_ge(s_alo, e)
                    sp.dma_start(raw[:, 0, :].rearrange("p (k h) -> p k h", h=H0),
                                 w1[e].rearrange("(k p) h -> p k h", p=P)).then_inc(s_raw[0], 16)
                    if e:
                        sp.wait_ge(s_blo, e)
                    sp.dma_start(raw[:, 1, :].rearrange("p (k d) -> p k d", d=D),
                                 w2[e].rearrange("(k p) d -> p k d", p=P)).then_inc(s_raw[1], 16)

            @block.gpsimd
            def _(pool):
                def gather(h):
                    for j in range(LIST):
                        pool.indirect_dma_start(rows[:, h, j, :], None, y, bass.IndirectOffsetOnAxis(
                            ap=now[:, h, j:j + 1].bitcast(U32), axis=0)).then_inc(s_rows[h], 16)

                pool.wait_ge(s_now, 1)
                gather(0)
                for e in range(E_N):
                    if e:
                        pool.wait_ge(s_add, 16 * LIST * e)
                    pool.sem_inc(s_turn, 1)
                    if e + 1 < E_N:
                        pool.wait_ge(s_now, e + 2)
                        gather((e + 1) % 2)
                    for j in range(LIST):
                        pool.wait_ge(s_out, NO * (e + 1) + 2 * (j + 1))
                        pool.indirect_dma_start(dst, bass.IndirectOffsetOnAxis(
                            ap=now[:, e % 2, j:j + 1].bitcast(U32), axis=0), out[:, j, :], None,
                            compute_op=ALU.add).then_inc(s_add, 16)
                pool.wait_ge(s_add, 16 * LIST * E_N)

            @block.vector
            def _(dve):
                def list_of(e, h):
                    dve.tensor_copy(now[:, h, :], chosen[:, :, bass.ds(e, 1)].rearrange("p j o -> p (j o)")) \
                       .then_inc(s_now, 1)

                def split(e):
                    dve.wait_ge(s_ahi, e + 1)
                    dve.tensor_tensor(a[1][:, :, :].rearrange("p k h -> p (k h)"), raw[:, 0, :],
                                      a[0][:, :, :].rearrange("p k h -> p (k h)").bitcast(F32), ALU.subtract) \
                       .then_inc(s_alo, 1)

                def expert(e, h, last=False):
                    if not last:
                        dve.wait_ge(s_turn, e + 1)
                        list_of(e + 1, 1 - h)
                    for k in range(KD):
                        dve.wait_ge(s_xhi, KD * e + k + 1)
                        dve.tensor_tensor(x[1][:, k, :], px[k % 4][:, 0:CAP0], x[0][:, k, :].bitcast(F32),
                                          ALU.subtract).then_inc(s_xlo, 1)
                    dve.wait_ge(s_bhi, e + 1)
                    dve.tensor_tensor(b[1][:, :, :].rearrange("p k d -> p (k d)"), raw[:, 1, :],
                                      b[0][:, :, :].rearrange("p k d -> p (k d)").bitcast(F32), ALU.subtract) \
                       .then_inc(s_blo, 1)
                    for m in range(KH0):
                        dve.wait_ge(s_hhi, KH0 * e + m + 1)
                        dve.tensor_tensor(hid[1][:, m, :], hid_f[:, m % 2, :], hid[0][:, m, :].bitcast(F32),
                                          ALU.subtract).then_inc(s_hlo, 1)
                    if not last:
                        split(e + 1)
                    dve.wait_ge(s_turn, e + 1)
                    for i, (j, c) in enumerate(OUTS):
                        dve.wait_ge(s_o, NO * e + i + 1)
                        dve.tensor_scalar(out[:, j, c * BANK:(c + 1) * BANK], po[i % 4][0:CAPR, :],
                                          share[:, j, bass.ds(e, 1)], None, ALU.mult).then_inc(s_out, 1)

                dve.sem_inc(s_out, NO)
                list_of(0, 0)
                split(0)
                with dve.Fori(0, E_N // 2 - 1) as i:
                    for h in range(2):
                        expert(2 * i + h, h)
                expert(E_N - 2, 0)
                expert(E_N - 1, 1, last=True)

            @block.scalar
            def _(act):
                def split(e):
                    act.wait_ge(s_raw[0], 16 * e + 16)
                    act.activation(a[0][:, :, :].rearrange("p k h -> p (k h)"), raw[:, 0, :], ACT.Copy).then_inc(s_ahi, 1)

                def expert(e, last=False):
                    for k in range(KD):
                        act.wait_ge(s_tr, KD * e + k + 1)
                        act.activation(x[0][:, k, :], px[k % 4][:, 0:CAP0], ACT.Copy).then_inc(s_xhi, 1)
                    act.wait_ge(s_raw[1], 16 * e + 16)
                    act.activation(b[0][:, :, :].rearrange("p k d -> p (k d)"), raw[:, 1, :], ACT.Copy).then_inc(s_bhi, 1)
                    for m in range(KH0):
                        act.wait_ge(s_h, KH0 * e + m + 1)
                        if m >= 2:
                            act.wait_ge(s_hlo, KH0 * e + m - 1)
                        act.activation(hid_f[:, m % 2, :], px[m % 4][:, 0:CAP0], ACT.Gelu).then_inc(s_gelu, 1)
                        act.wait_ge(s_gelu, KH0 * e + m + 1)
                        act.activation(hid[0][:, m, :], hid_f[:, m % 2, :], ACT.Copy).then_inc(s_hhi, 1)
                    if not last:
                        split(e + 1)
                    act.wait_ge(s_o, NO * e + NO)

                split(0)
                with act.Fori(0, E_N - 1) as e:
                    expert(e)
                expert(E_N - 1, last=True)

            @block.tensor
            def _(pe):
                def expert(e, h, turn):
                    pe.wait_ge(s_rows[h], 16 * LIST * turn)
                    for k in range(KD):
                        if k >= 4:
                            pe.wait_ge(s_xlo, KD * e + k - 3)
                        for j in range(LIST):
                            ins = pe.transpose(px[k % 4][:, j * CAPR:(j + 1) * CAPR],
                                               rows[:, h, j, k * P:(k + 1) * P], ident[0:CAPR, 0:CAPR])
                        ins.then_inc(s_tr, 1)
                    pe.wait_ge(s_xlo, KD * (e + 1))
                    pe.wait_ge(s_alo, e + 1)
                    for m in range(KH0):
                        cols = slice(m * P, (m + 1) * P)
                        for k in range(KD):
                            ins = mm3(pe, px[m % 4][:, 0:CAP0], [w[:, k, cols] for w in a], [v[:, k, :] for v in x],
                                      k == 0, k == KD - 1)
                        ins.then_inc(s_h, 1)
                    pe.wait_ge(s_blo, e + 1)
                    pe.wait_ge(s_hlo, KH0 * (e + 1))
                    for i, (j, c) in enumerate(OUTS):
                        if i < 4:
                            pe.wait_ge(s_out, NO * (e + 1))
                        else:
                            pe.wait_ge(s_out, NO * (e + 1) + i - 3)
                        toks, cols = slice(j * CAPR, (j + 1) * CAPR), slice(c * BANK, (c + 1) * BANK)
                        for k in range(KH0):
                            ins = mm3(pe, po[i % 4][0:CAPR, :], [v[:, k, toks] for v in hid], [w[:, k, cols] for w in b],
                                      k == 0, k == KH0 - 1)
                        ins.then_inc(s_o, 1)

                with pe.Fori(0, E_N // 2) as i:
                    for h in range(2):
                        expert(2 * i + h, h, i + 1)


def sage_phase(nc, name, act_hi, act_lo, at, deg_inv, w_self, w_neigh, bias, resid, dst):
    with Phase(nc, name) as ph:
        cnt = ph.sb("cnt", [R, T, N], F32R)
        raw = ph.sb("raw", [P, KD, SLAB], F32)
        w = [[ph.sb(f"w{c}_{s}", [P, KD, SLAB], F32R) for s in ("hi", "lo")] for c in "ns"]
        z = [ph.sb(f"z_{s}", [R, T, SLAB], F32R) for s in ("hi", "lo")]
        add = ph.sb("add", [R, 2, SLAB], F32)
        bb = ph.sb("bias", [R, D], F32)
        own = ph.sb("own", [R, 2, SLAB], F32)
        out = ph.sb("out", [R, 2, SLAB], F32)
        pz = [ph.ps(f"pz{i}", [R, BANK]) for i in range(4)]
        pown = [ph.ps(f"pown{i}", [R, BANK]) for i in range(2)]
        pagg = [ph.ps(f"pagg{i}", [R, BANK]) for i in range(2)]
        s_cnt, s_bias, s_raw, s_whi, s_wlo = ph.sem("cnt"), ph.sem("bias"), ph.sem("raw"), ph.sem("whi"), ph.sem("wlo")
        s_zm, s_zhi, s_zlo = ph.sem("zm"), ph.sem("zhi"), ph.sem("zlo")
        s_add, s_sum, s_own, s_agg = ph.sems("add", 2), ph.sem("sum"), ph.sem("own"), ph.sem("agg")
        s_part, s_tot, s_out, s_st = ph.sem("part"), ph.sem("tot"), ph.sem("out"), ph.sems("st", 2)
        tiles = NSLAB * T

        def store(sp, u):
            g, t = u // T, u % T
            sp.wait_ge(s_out, u + 1)
            sp.dma_start(dst[t * R:(t + 1) * R, g * SLAB:(g + 1) * SLAB], out[:, u % 2, :]).then_inc(s_st[u % 2], 16)

        with nc.Block() as block:
            @block.sync
            def _(sp):
                def slab(s):
                    if s:
                        sp.wait_ge(s_wlo, s)
                    m = (w_neigh, w_self)[s % 2]
                    sp.dma_start(raw[:, :, :], m[:, s // 2 * SLAB:(s // 2 + 1) * SLAB].rearrange("(k p) n -> p k n", p=P)) \
                        .then_inc(s_raw, 16)

                slab(0)
                sp.dma_start(bb[:, :], bias.rearrange("(o n) -> o n", o=1).to_broadcast([R, D])).then_inc(s_bias, 16)
                for k in range(T):
                    sp.dma_start(cnt[:, k, :].bitcast(F32), at[k]).then_inc(s_cnt, 16)
                slab(1)
                for u in range(tiles):
                    g, t = u // T, u % T
                    rows, cols = slice(t * R, (t + 1) * R), slice(g * SLAB, (g + 1) * SLAB)
                    if t == 4 and g + 1 < NSLAB:
                        slab(2 * g + 2)
                    if t == 9 and g + 1 < NSLAB:
                        slab(2 * g + 3)
                    if resid is not None:
                        if u >= 2:
                            sp.wait_ge(s_part, u - 1)
                        sp.dma_start(add[:, u % 2, :], resid[rows, cols]).then_inc(s_add[u % 2], 16)
                    if u:
                        store(sp, u - 1)
                store(sp, tiles - 1)
                for h in range(2):
                    sp.wait_ge(s_st[h], 16 * tiles // 2)

            @block.gpsimd
            def _(pool):
                if resid is not None:
                    pool.wait_ge(s_bias, 16)
                    for u in range(tiles):
                        g = u // T
                        pool.wait_ge(s_add[u % 2], 16 * (u // 2 + 1))
                        pool.tensor_tensor(add[:, u % 2, :], add[:, u % 2, :], bb[:, g * SLAB:(g + 1) * SLAB], ALU.add) \
                            .then_inc(s_sum, 1)

            @block.vector
            def _(dve):
                def split(s):
                    dve.wait_ge(s_whi, s + 1)
                    dve.tensor_tensor(w[s % 2][1][:, :, :], raw[:, :, :], w[s % 2][0][:, :, :].bitcast(F32), ALU.subtract) \
                       .then_inc(s_wlo, 1)

                split(0)
                split(1)
                dve.wait_ge(s_bias, 16)
                for g in range(NSLAB):
                    for t in range(T):
                        u = T * g + t
                        dve.wait_ge(s_zhi, u + 1)
                        dve.tensor_tensor(z[1][:, t, :], pz[u % 4][:, 0:SLAB], z[0][:, t, :].bitcast(F32), ALU.subtract) \
                           .then_inc(s_zlo, 1)
                    for t in range(T):
                        u = T * g + t
                        if t == 5 and g + 1 < NSLAB:
                            split(2 * g + 2)
                        dve.wait_ge(s_own, u + 1)
                        if resid is not None:
                            dve.wait_ge(s_sum, u + 1)
                            more = add[:, u % 2, :]
                        else:
                            more = bb[:, g * SLAB:(g + 1) * SLAB]
                        dve.tensor_tensor(own[:, u % 2, :], pown[u % 2][:, 0:SLAB], more, ALU.add).then_inc(s_part, 1)
                        dve.wait_ge(s_part, u + 1)
                        dve.wait_ge(s_agg, u + 1)
                        if u >= 2:
                            dve.wait_ge(s_st[u % 2], 16 * (u // 2))
                        whole = out if resid is not None else own
                        dve.scalar_tensor_tensor(whole[:, u % 2, :], pagg[u % 2][:, 0:SLAB], deg_inv[:, t:t + 1],
                                                 own[:, u % 2, :], ALU.mult, ALU.add).then_inc(s_tot, 1)
                        if resid is None:
                            dve.wait_ge(s_tot, u + 1)
                            dve.tensor_scalar(out[:, u % 2, :], own[:, u % 2, :], 0.0, None, ALU.max).then_inc(s_out, 1)
                        else:
                            dve.wait_ge(s_tot, u + 1)
                            dve.sem_inc(s_out, 1)
                    if g + 1 < NSLAB:
                        split(2 * g + 3)

            @block.scalar
            def _(act):
                def split(s):
                    act.wait_ge(s_raw, 16 * (s + 1))
                    act.activation(w[s % 2][0][:, :, :], raw[:, :, :], ACT.Copy).then_inc(s_whi, 1)

                split(0)
                split(1)
                for g in range(NSLAB):
                    for t in range(T):
                        u = T * g + t
                        act.wait_ge(s_zm, u + 1)
                        act.activation(z[0][:, t, :], pz[u % 4][:, 0:SLAB], ACT.Copy).then_inc(s_zhi, 1)
                    if g + 1 < NSLAB:
                        split(2 * g + 2)
                        act.wait_ge(s_own, T * (g + 1))
                        split(2 * g + 3)
                        act.wait_ge(s_agg, T * (g + 1))

            @block.tensor
            def _(pe):
                for g in range(NSLAB):
                    pe.wait_ge(s_wlo, 2 * g + 1)
                    for t in range(T):
                        u = T * g + t
                        if u >= 4:
                            pe.wait_ge(s_zlo, u - 3)
                        rows = slice(t * R, (t + 1) * R)
                        for k in range(KD):
                            ins = mm3(pe, pz[u % 4][:, 0:SLAB], (act_hi[:, k, rows], act_lo[:, k, rows]),
                                      [x[:, k, :] for x in w[0]], k == 0, k == KD - 1)
                        ins.then_inc(s_zm, 1)
                    pe.wait_ge(s_wlo, 2 * g + 2)
                    if not g:
                        pe.wait_ge(s_cnt, 16 * T)
                    for t in range(T):
                        u = T * g + t
                        if u >= 2:
                            pe.wait_ge(s_tot, u - 1)
                        rows = slice(t * R, (t + 1) * R)
                        for k in range(KD):
                            ins = mm3(pe, pown[u % 2][:, 0:SLAB], (act_hi[:, k, rows], act_lo[:, k, rows]),
                                      [x[:, k, :] for x in w[1]], k == 0, k == KD - 1)
                        ins.then_inc(s_own, 1)
                        if not t:
                            pe.wait_ge(s_zlo, T * (g + 1))
                        for k in range(T):
                            for s in range(2):
                                ins = pe.matmul(pagg[u % 2][:, 0:SLAB], cnt[:, k, rows], z[s][:, k, :],
                                                start=(k, s) == (0, 0), stop=(k, s) == (T - 1, 1))
                        ins.then_inc(s_agg, 1)


def assign_phase(nc, act_hi, act_lo, gate_w, ident, slots, expert_of):
    with Phase(nc, "assign") as ph:
        prob, s_prob, g_sync, g_scalar, g_tensor, g_vector = gate_steps(ph, nc)
        work = ph.sb("work", [E_N, TOPW], F32)
        best = ph.sb("best", [E_N, 8], F32)
        picked = ph.sb("picked", [E_N, N], F32)
        pick = ph.sb("pick", [R, T, E_N], F32)
        score = ph.sb("score", [R, T, E_N], F32)
        one = ph.sb("one", [R, T], F32)
        hot = ph.sb("hot", [R, T, E_N], F32)
        num_i = ph.sb("num_i", [R, E_N], I32)
        num = ph.sb("num", [R, E_N], F32)
        first = ph.sb("first", [R, T], F32)
        hot_e = ph.sb("hot_e", [E_N, N], F32)
        rank = ph.sb("rank", [E_N, N], F32)
        size = ph.sb("size", [E_N, 4], F32)
        size_i = ph.sb("size_i", [E_N, 2], I32)
        before = ph.sb("before", [E_N, E_N], F32)
        ones = ph.sb("ones", [E_N, 2], F32)
        block_i = ph.sb("block_i", [E_N, BLOCKS], I32)
        ends = ph.sb("ends", [E_N, BLOCKS], F32)
        slot = ph.sb("slot", [R, T], I32)
        node = ph.sb("node", [R, T], I32)
        row = ph.sb("row", [R, T, 2], F32)
        free = ph.sb("free", [P, BLOCKS, 2], F32)
        pt = ph.ps("pt", [E_N, 3, BANK])
        pp = ph.ps("pp", [R, T, E_N])
        ps = ph.ps("ps", [R, BANK])
        pe_of = ph.ps("pe_of", [1, BANK])
        s_tr, s_link, s_pick, s_back, s_hot, s_he = (ph.sem(x) for x in ("tr", "link", "pick", "back", "hot", "he"))
        s_iota, s_const, s_size, s_start = (ph.sem(x) for x in ("iota", "const", "size", "start"))
        s_val, s_slot, s_ends, s_ex, s_row = (ph.sem(x) for x in ("val", "slot", "ends", "ex", "row"))
        s_free, s_fill, s_put, s_done = (ph.sem(x) for x in ("free", "fill", "put", "done"))
        with nc.Block() as block:
            @block.sync
            def _(sp):
                g_sync(sp, gate_w)
                sp.wait_ge(s_free, 2)
                sp.dma_start(slots.rearrange("(b p) c -> p b c", p=P), free[:, :, :]).then_inc(s_fill, 16)

            @block.gpsimd
            def _(pool):
                pool.iota(num_i[:, :], [[1, E_N]], base=0, channel_multiplier=0).then_inc(s_iota, 1)
                pool.iota(block_i[:, :], [[1, BLOCKS]], base=0, channel_multiplier=0).then_inc(s_iota, 1)
                pool.iota(node[:, :], [[R, T]], base=0, channel_multiplier=1).then_inc(s_iota, 1)
                pool.iota(free[:, :, 0].bitcast(I32), [[0, BLOCKS]], base=N, channel_multiplier=0).then_inc(s_free, 1)
                pool.memset(free[:, :, 1], 0.0).then_inc(s_free, 1)
                pool.memset(ones[:, :], 1.0).then_inc(s_const, 1)
                pool.memset(before[:, :], 1.0).then_inc(s_const, 1)
                pool.wait_ge(s_const, 2)
                pool.affine_select(out=before[:, :], in_=before[:, :], compare_op=ALU.is_gt, fill=0.0,
                                   base=0, pattern=[[1, E_N]], channel_multiplier=-1).then_inc(s_const, 1)
                pool.wait_ge(s_fill, 16)
                pool.wait_ge(s_row, 1)
                for t in range(T):
                    pool.indirect_dma_start(slots, bass.IndirectOffsetOnAxis(ap=slot[:, t:t + 1].bitcast(U32), axis=0),
                                            row[:, t, :], None).then_inc(s_put, 16)
                pool.wait_ge(s_put, 16 * T)

            @block.scalar
            def _(act):
                g_scalar(act)

            @block.tensor
            def _(pe):
                g_tensor(pe, act_hi, act_lo)
                pe.wait_ge(s_prob, 1)
                spread_nodes(pe, pt, prob, ident).then_inc(s_tr, 1)
                pe.wait_ge(s_pick, 1)
                for t in range(T):
                    ins = pe.transpose(pp[:, t, :], picked[:, t * R:(t + 1) * R], ident[0:E_N, 0:E_N])
                ins.then_inc(s_back, 1)
                pe.wait_ge(s_hot, 1)
                spread_nodes(pe, pt, hot, ident).then_inc(s_tr, 1)
                pe.wait_ge(s_const, 3)
                pe.wait_ge(s_size, 1)
                pe.matmul(ps[0:E_N, 0:2], before[:, :], size[:, 2:4], start=True, stop=True).then_inc(s_start, 1)
                pe.wait_ge(s_val, 1)
                for t in range(T):
                    ins = pe.matmul(ps[:, 2 + t:3 + t], rank[:, t * R:(t + 1) * R], ones[:, 0:1], start=True, stop=True)
                ins.then_inc(s_slot, 1)
                pe.wait_ge(s_ends, 1)
                pe.matmul(pe_of[0:1, 0:BLOCKS], ones[:, 0:1], ends[:, :], start=True, stop=True).then_inc(s_ex, 1)

            @block.vector
            def _(dve):
                g_vector(dve)
                link = Link(dve, s_link)
                dve.wait_ge(s_tr, 1)
                dve.memset(work[:, N:N + PAD1], 2.0)
                dve.memset(work[:, N + PAD1:TOPW], -2.0)
                link(gather_nodes(dve, work, pt))
                for i in range((CAP1 + PAD1) // 8):
                    link(dve.max(best[:, :], work[:, :]))
                    link(dve.match_replace(work[:, :], best[:, :], work[:, :], -1.0))
                dve.tensor_scalar(picked[:, :], work[:, 0:N], 0.0, None, ALU.is_lt).then_inc(s_pick, 1)
                dve.wait_ge(s_back, 1)
                dve.wait_ge(s_iota, 3)
                dve.tensor_copy(num[:, :], num_i[:, :])
                link(dve.tensor_reduce(one[:, :], pp[:, :, :], AX.X, ALU.max))
                link(dve.tensor_scalar(one[:, :], one[:, :], -1.0, 1.0, ALU.mult, ALU.add))
                wide = one[:, :].unsqueeze(2).to_broadcast([R, T, E_N])
                link(dve.tensor_tensor(pick[:, :, :], pp[:, :, :], wide, ALU.add))
                link(dve.tensor_tensor(score[:, :, :], prob[:, :, :], pick[:, :, :], ALU.mult))
                link(dve.tensor_scalar(pick[:, :, :], pick[:, :, :], -1.0, None, ALU.add))
                link(dve.tensor_tensor(score[:, :, :], score[:, :, :], pick[:, :, :], ALU.add))
                link(dve.tensor_reduce(one[:, :], score[:, :, :], AX.X, ALU.max))
                dve.tensor_copy(row[:, :, 1], one[:, :])
                link(dve.tensor_tensor(pick[:, :, :], score[:, :, :], wide, ALU.is_lt))
                numbers = num[:, :].unsqueeze(1).to_broadcast([R, T, E_N])
                link(dve.scalar_tensor_tensor(pick[:, :, :], pick[:, :, :], float(E_N), numbers, ALU.mult, ALU.add))
                link(dve.tensor_reduce(first[:, :], pick[:, :, :], AX.X, ALU.min))
                dve.tensor_tensor(hot[:, :, :], pick[:, :, :], first[:, :].unsqueeze(2).to_broadcast([R, T, E_N]),
                                  ALU.is_equal).then_inc(s_hot, 1)
                dve.tensor_copy(row[:, :, 0].bitcast(I32), node[:, :])
                dve.wait_ge(s_tr, 2)
                link(gather_nodes(dve, hot_e, pt))
                link(dve.tensor_tensor_scan(rank[:, :], hot_e[:, :], hot_e[:, :], 0.0, ALU.add, ALU.max))
                link(dve.tensor_scalar(size_i[:, 0:1], rank[:, N - 1:N], float(P - 1), None, ALU.add))
                link(dve.tensor_scalar(size_i[:, 1:2], size_i[:, 0:1], P.bit_length() - 1, None, ALU.arith_shift_right))
                dve.tensor_copy(size[:, 2:3], size_i[:, 1:2])
                dve.tensor_copy(size[:, 3:4], size_i[:, 1:2]).then_inc(s_size, 1)
                dve.wait_ge(s_start, 1)
                link(dve.tensor_scalar(size[:, 0:1], ps[0:E_N, 0:1], float(P), -1.0, ALU.mult, ALU.add))
                link(dve.tensor_tensor(size[:, 1:2], ps[0:E_N, 0:1], size[:, 2:3], ALU.add))
                dve.scalar_tensor_tensor(rank[:, :], rank[:, :], size[:, 0:1], hot_e[:, :], ALU.add, ALU.mult) \
                   .then_inc(s_val, 1)
                dve.tensor_scalar(ends[:, :], block_i[:, :], size[:, 1:2], None, ALU.is_ge).then_inc(s_ends, 1)
                dve.wait_ge(s_slot, 1)
                dve.tensor_copy(slot[:, :], ps[:, 2:2 + T]).then_inc(s_row, 1)
                dve.wait_ge(s_ex, 1)
                dve.tensor_scalar(expert_of[:, :], pe_of[0:1, 0:BLOCKS], float(E_N - 1), None, ALU.min) \
                   .then_inc(s_done, 1)
                dve.wait_ge(s_done, 1)


def block_phase(nc, y, x, slots, expert_of, w1, w2, ident, dst):
    with Phase(nc, "block") as ph:
        now = ph.sb("now", [P, 2, 2], F32)
        rows = ph.sb("rows", [P, 2, D], F32)
        keep = ph.sb("keep", [P, 2, D], F32)
        out = ph.sb("out", [P, 2, D], F32)
        t_ = [ph.sb(f"t_{s}", [P, 2, KD, P], F32R) for s in ("hi", "lo")]
        act_f = ph.sb("act_f", [P, 2, H1], F32)
        hid = [ph.sb(f"hid_{s}", [P, 2, KH1, P], F32R) for s in ("hi", "lo")]
        raw = ph.sb("raw", [P, 2, 2, KD * H1], F32)
        a = [ph.sb(f"w1_{s}", [P, 2, KD, H1], F32R) for s in ("hi", "lo")]
        b = [ph.sb(f"w2_{s}", [P, 2, KH1, D], F32R) for s in ("hi", "lo")]
        px = ph.ps("px", [P, 2, BANK])
        phid = ph.ps("phid", [P, BANK])
        pht = ph.ps("pht", [P, KH1, P])
        po = [ph.ps(f"po{i}", [P, 2, BANK]) for i in range(2)]
        s_now, s_rows, s_keep, s_raw = ph.sems("now", 2), ph.sems("rows", 2), ph.sems("keep", 2), ph.sems("raw", 2)
        s_zero, s_whi, s_wlo = ph.sem("zero"), ph.sem("whi"), ph.sem("wlo")
        s_tr, s_thi, s_tlo = ph.sem("tr"), ph.sem("thi"), ph.sem("tlo")
        s_h, s_gelu, s_ht, s_hhi, s_hlo = ph.sem("h"), ph.sem("gelu"), ph.sem("ht"), ph.sem("hhi"), ph.sem("hlo")
        s_o, s_out, s_st = ph.sem("o"), ph.sem("out"), ph.sems("st", 2)
        with nc.Block() as block:
            @block.sync
            def _(sp):
                for n in range(BLOCKS):
                    h = n % 2
                    if n >= 2:
                        sp.wait_ge(s_st[h], 16 * (n // 2))
                    sp.dma_start(now[:, h, :], slots[n * P:(n + 1) * P, :]).then_inc(s_now[h], 16)
                    if n >= 2:
                        sp.wait_ge(s_wlo, n - 1)
                    e = sp.value_load(expert_of[0:1, n:n + 1], min_val=0, max_val=E_N - 1)
                    sp.dma_start(raw[:, h, 0, :].rearrange("p (k h) -> p k h", h=H1),
                                 w1[bass.ds(e, 1)].rearrange("e (k p) h -> p (e k) h", p=P)).then_inc(s_raw[h], 16)
                    sp.dma_start(raw[:, h, 1, :].rearrange("p (k d) -> p k d", d=D),
                                 w2[bass.ds(e, 1)].rearrange("e (k p) d -> p (e k) d", p=P)).then_inc(s_raw[h], 16)

            @block.gpsimd
            def _(pool):
                def offset(h):
                    return bass.IndirectOffsetOnAxis(ap=now[:, h, 0:1].bitcast(U32), axis=0)

                def gather(n):
                    h = n % 2
                    pool.wait_ge(s_now[h], 16 * (n // 2 + 1))
                    if n >= 2:
                        pool.wait_ge(s_tr, n - 1)
                        pool.wait_ge(s_out, n - 1)
                    for buf, src, sem in ((rows, y, s_rows[h]), (keep, x, s_keep[h])):
                        pool.indirect_dma_start(buf[:, h, :], None, src, offset(h), bounds_check=N - 1,
                                                oob_is_err=False).then_inc(sem, 16)

                for buf in (rows, keep):
                    pool.memset(buf[:, :, :], 0.0).then_inc(s_zero, 1)
                pool.wait_ge(s_zero, 2)
                gather(0)
                for n in range(BLOCKS):
                    if n + 1 < BLOCKS:
                        gather(n + 1)
                    pool.wait_ge(s_out, n + 1)
                    pool.indirect_dma_start(dst, offset(n % 2), out[:, n % 2, :], None, bounds_check=N - 1,
                                            oob_is_err=False).then_inc(s_st[n % 2], 16)
                pool.wait_ge(s_st[0], 16 * ((BLOCKS + 1) // 2))
                pool.wait_ge(s_st[1], 16 * (BLOCKS // 2))

            @block.scalar
            def _(act):
                def prepare(n):
                    h = n % 2
                    act.wait_ge(s_raw[h], 32 * (n // 2 + 1))
                    if n >= 2:
                        act.wait_ge(s_o, n - 1)
                    act.activation(a[0][:, h, :, :].rearrange("p k c -> p (k c)"), raw[:, h, 0, :], ACT.Copy)
                    act.activation(b[0][:, h, :, :].rearrange("p k c -> p (k c)"), raw[:, h, 1, :], ACT.Copy) \
                       .then_inc(s_whi, 1)
                    act.wait_ge(s_tr, n + 1)
                    for c in range(2):
                        ins = act.activation(t_[0][:, h, 4 * c:4 * c + 4, :].rearrange("p k r -> p (k r)"),
                                             px[:, c, :], ACT.Copy)
                    ins.then_inc(s_thi, 1)

                prepare(0)
                for n in range(BLOCKS):
                    h = n % 2
                    if n + 1 < BLOCKS:
                        prepare(n + 1)
                    act.wait_ge(s_h, n + 1)
                    act.activation(act_f[:, h, :], phid[:, 0:H1], ACT.Gelu).then_inc(s_gelu, 1)
                    act.wait_ge(s_ht, n + 1)
                    act.activation(hid[0][:, h, :, :], pht[:, :, :], ACT.Copy).then_inc(s_hhi, 1)

            @block.vector
            def _(dve):
                def prepare(n):
                    h = n % 2
                    dve.wait_ge(s_whi, n + 1)
                    dve.tensor_tensor(a[1][:, h, :, :].rearrange("p k c -> p (k c)"), raw[:, h, 0, :],
                                      a[0][:, h, :, :].rearrange("p k c -> p (k c)").bitcast(F32), ALU.subtract)
                    dve.tensor_tensor(b[1][:, h, :, :].rearrange("p k c -> p (k c)"), raw[:, h, 1, :],
                                      b[0][:, h, :, :].rearrange("p k c -> p (k c)").bitcast(F32), ALU.subtract) \
                       .then_inc(s_wlo, 1)
                    dve.wait_ge(s_thi, n + 1)
                    for c in range(2):
                        part = [t_[s][:, h, 4 * c:4 * c + 4, :].rearrange("p k r -> p (k r)") for s in range(2)]
                        ins = dve.tensor_tensor(part[1], px[:, c, :], part[0].bitcast(F32), ALU.subtract)
                    ins.then_inc(s_tlo, 1)

                prepare(0)
                for n in range(BLOCKS):
                    h = n % 2
                    if n + 1 < BLOCKS:
                        prepare(n + 1)
                    dve.wait_ge(s_hhi, n + 1)
                    dve.tensor_tensor(hid[1][:, h, :, :], pht[:, :, :], hid[0][:, h, :, :].bitcast(F32), ALU.subtract) \
                       .then_inc(s_hlo, 1)
                    dve.wait_ge(s_o, n + 1)
                    dve.wait_ge(s_keep[h], 16 * (n // 2 + 1))
                    if n >= 2:
                        dve.wait_ge(s_st[h], 16 * (n // 2))
                    for c in range(2):
                        cols = slice(c * BANK, (c + 1) * BANK)
                        ins = dve.scalar_tensor_tensor(out[:, h, cols], po[h][:, c, :], now[:, h, 1:2],
                                                       keep[:, h, cols], ALU.mult, ALU.add)
                    ins.then_inc(s_out, 1)

            @block.tensor
            def _(pe):
                def flip(n):
                    h = n % 2
                    pe.wait_ge(s_rows[h], 16 * (n // 2 + 1))
                    if n:
                        pe.wait_ge(s_tlo, n)
                    for k in range(KD):
                        ins = pe.transpose(px[:, k // 4, (k % 4) * P:(k % 4 + 1) * P], rows[:, h, k * P:(k + 1) * P],
                                           ident[:, :])
                    ins.then_inc(s_tr, 1)

                flip(0)
                for n in range(BLOCKS):
                    h = n % 2
                    pe.wait_ge(s_tlo, n + 1)
                    pe.wait_ge(s_wlo, n + 1)
                    if n:
                        pe.wait_ge(s_gelu, n)
                    for k in range(KD):
                        ins = mm3(pe, phid[:, 0:H1], [v[:, h, k, :] for v in t_], [w[:, h, k, :] for w in a],
                                  k == 0, k == KD - 1)
                    ins.then_inc(s_h, 1)
                    if n + 1 < BLOCKS:
                        flip(n + 1)
                    pe.wait_ge(s_gelu, n + 1)
                    if n:
                        pe.wait_ge(s_hlo, n)
                    for k in range(KH1):
                        ins = pe.transpose(pht[:, k, :], act_f[:, h, k * P:(k + 1) * P], ident[:, :])
                    ins.then_inc(s_ht, 1)
                    pe.wait_ge(s_hlo, n + 1)
                    if n >= 2:
                        pe.wait_ge(s_out, n - 1)
                    for c in range(2):
                        for k in range(KH1):
                            ins = mm3(pe, po[h][:, c, :], [v[:, h, k, :] for v in hid],
                                      [w[:, h, k, c * BANK:(c + 1) * BANK] for w in b], k == 0, k == KH1 - 1)
                    ins.then_inc(s_o, 1)


def gps_kernel(nc, x, src, dst, rms_w, w_down, wl, wr, att, w_up, wq, bq, wk, bk, wv, bv, wo, bo,
               gate0_w, w1_0, w2_0, w_self0, w_neigh0, b0, w_self1, w_neigh1, b1, w_qkv, w_o,
               gate1_w, w1_1, w2_1, out):
    def dram(name, shape):
        return nc.dram_tensor(name, shape, F32, kind="Internal").ap()

    scores, at = dram("scores", (N * N, HEADS)), dram("at", (T, R, N))
    xl, xr = dram("xl", (N, HID)), dram("xr", (N, HID))
    mixt = [dram(f"mixt{i}", (D, N)) for i in range(2)]
    xs = [dram(f"x{i}", (N, D)) for i in range(2)]
    y = [dram(f"y{i}", (N, D)) for i in range(2)]
    hidden, resid, part = (dram(x, (N, D)) for x in ("hidden", "resid", "part"))
    slots = dram("slots", (BLOCKS * P, 2))

    with Phase(nc, "all") as keep:
        ident = keep.sb("ident", [P, P], F32)
        deg_inv = keep.sb("deg_inv", [R, T], F32)
        expert_of = keep.sb("expert_of", [1, BLOCKS], I32)

        def activations(ph):
            return [ph.sb(f"act_{s}", [P, KD, N], F32R) for s in ("hi", "lo")]

        with Phase(nc, "ffn0") as ffn0:
            chosen = ffn0.sb("chosen", [CAPR, LIST, E_N], I32)
            share = ffn0.sb("share", [CAPR, LIST, E_N], F32)
            with Phase(nc, "layer0") as layer:
                act = activations(layer)
                loops = layer.sb("loops", [R, T, HEADS], F32)
                with Phase(nc, "front") as front:
                    hole = front.sb("hole", [R, N], F32)
                    rms = front.sb("rms", [R, T], F32)
                    filled = constants_phase(nc, ident, hole, scores)
                    norm_phase(nc, "norm0", x, *act, ident, rms=rms)
                    gat_project_phase(nc, *act, rms, rms_w, w_down, wl, wr, att, xl, xr, loops)
                with Phase(nc, "edge") as edge:
                    edges = Edges(edge, src, dst, att, xl, xr, scores, loops, filled)
                    with Phase(nc, "sums0") as sums:
                        z = [sums.sb(f"z_{s}", [MHEADS, N], F32R) for s in ("hi", "lo")]
                        mix_phase(nc, "mix0", *act, wq, wk, wv, [bq, bk, bv], 1e-6, True, ident, mixt[0], z, edges)
                        output_phase(nc, "out0", *act, mixt[0], z, wo, True, ident, x, part, edges)
            count_phase(nc, src, dst, ident, at, deg_inv)
            gat_phase(nc, scores, at, xl, ident, w_up, bo, part, xs[0])
            with Phase(nc, "gate0") as layer:
                act = activations(layer)
                norm_phase(nc, "norm1", xs[0], *act, ident, dst=y[0])
                choose_phase(nc, *act, gate0_w, ident, chosen, share)
            expert_phase(nc, y[0], chosen, share, w1_0, w2_0, ident, xs[0])

        with Phase(nc, "layer1") as layer:
            act = activations(layer)
            norm_phase(nc, "norm2", xs[0], *act, ident)
            sage_phase(nc, "sage0", *act, at, deg_inv, w_self0, w_neigh0, b0, None, hidden)
            with Phase(nc, "sums1") as sums:
                z = [sums.sb(f"z_{s}", [MHEADS, N], F32R) for s in ("hi", "lo")]
                mix_phase(nc, "mix1", *act, w_qkv[:, 0:D], w_qkv[:, D:2 * D], w_qkv[:, 2 * D:3 * D], None, 0.0, False,
                          ident, mixt[1], z)
                output_phase(nc, "out1", *act, mixt[1], z, w_o, False, ident, xs[0], resid)
            norm_phase(nc, "flip", hidden, *act, ident, normalize=False)
            sage_phase(nc, "sage1", *act, at, deg_inv, w_self1, w_neigh1, b1, resid, xs[1])
            norm_phase(nc, "norm3", xs[1], *act, ident, dst=y[1])
            assign_phase(nc, *act, gate1_w, ident, slots, expert_of)
        block_phase(nc, y[1], xs[1], slots, expert_of, w1_1, w2_1, ident, out)


_INS = ['x', 'src', 'dst', 'L0_gnn_rms_w', 'L0_gnn_W_down', 'L0_gnn_Wl', 'L0_gnn_Wr', 'L0_gnn_att', 'L0_gnn_W_up',
        'L0_mix_Wq', 'L0_mix_bq', 'L0_mix_Wk', 'L0_mix_bk', 'L0_mix_Wv', 'L0_mix_bv', 'L0_mix_Wo', 'L0_mix_bo',
        'L0_ffn_gate_w', 'L0_ffn_w1', 'L0_ffn_w2', 'L1_gnn_W_self0', 'L1_gnn_W_neigh0', 'L1_gnn_b0',
        'L1_gnn_W_self1', 'L1_gnn_W_neigh1', 'L1_gnn_b1', 'L1_mix_w_qkv', 'L1_mix_w_o',
        'L1_ffn_Wg', 'L1_ffn_W1', 'L1_ffn_W2']
_OUTS = [((N, D), 'float32')]


def kernel(**inputs):
    import numpy as _np
    import concourse.bacc as _bacc
    from concourse import mybir as _mybir
    from concourse.bass_utils import run_bass_kernel_spmd as _run

    nc = _bacc.Bacc("TRN2", target_bir_lowering=False, num_devices=1)
    arrays, args = {}, []
    for name in _INS:
        a = _np.ascontiguousarray(inputs[name])
        arrays[f"in_{name}_dram"] = a
        args.append(nc.dram_tensor(f"in_{name}_dram", a.shape, _mybir.dt.from_np(a.dtype), kind="ExternalInput").ap())
    for i, (shape, dtype) in enumerate(_OUTS):
        dt = _mybir.dt.from_np(_np.dtype(dtype))
        args.append(nc.dram_tensor(f"out_{i}_dram", shape, dt, kind="ExternalOutput").ap())
    gps_kernel(nc, *args)
    r = _run(nc, [arrays], core_ids=[0])
    got = tuple(r.results[0][f"out_{i}_dram"] for i in range(len(_OUTS)))
    return got[0]
```
